# Optimizing a Trainium2 kernel written in Bass

```python
import numpy as np
import jax
import jax.numpy as jnp

def _softmax(x, axis=-1):
    return jax.nn.softmax(x, axis=axis)

def _gelu(x):
    return jax.nn.gelu(x, approximate=True)

def _silu(x):
    return jax.nn.silu(x)

def _sigmoid(x):
    return jax.nn.sigmoid(x)

def _layernorm(x, axis=-1, eps=1e-05):
    m = jnp.mean(x, axis=axis, keepdims=True)
    v = jnp.var(x, axis=axis, keepdims=True)
    return (x - m) / jnp.sqrt(v + eps)

def _scatter_add(tgt, idx, src, axis=0):
    return tgt.at[idx].add(src)

def _segment_sum(src, seg, n):
    return jax.ops.segment_sum(src, seg, n)
kernel_name = 'mk_flamingo_gated_d4_seqx_r8_d970b9'

def setup_inputs(seed: int=0):
    np.random.seed(seed)
    _w = jnp.asarray

    def _rec_inputs():
        import jax
        import jax.numpy as jnp
        _rk = jax.random.key(seed)
        x = 0.5 + 0.2887 * jax.random.normal(jax.random.fold_in(_rk, 1), (4, 256, 256), jnp.float32)
        _lenS = 256 - jax.random.randint(jax.random.fold_in(_rk, 7), (4,), 0, max(1, 256 // 4) + 1, jnp.int32)
        _lenS2 = 256 - jax.random.randint(jax.random.fold_in(_rk, 8), (4,), 0, max(1, 256 // 4) + 1, jnp.int32)
        _ctx_512P = jax.random.normal(jax.random.fold_in(_rk, 11), (4, 16, 64), jnp.float32)
        _ctx_512c = jax.random.dirichlet(jax.random.fold_in(_rk, 511), 0.3 * jnp.ones((16,), jnp.float32), (4, 256))
        _ctx_512t = jnp.einsum('bsk,bkd->bsd', _ctx_512c, _ctx_512P)
        _ctx_512t = _ctx_512t * jax.lax.rsqrt(jnp.mean(jnp.square(_ctx_512t)) + 1e-12) * 0.953939
        ctx_512 = -0.000392918 + 0.999932 * (_ctx_512t + 0.3 * jax.random.normal(jax.random.fold_in(_rk, 611), (4, 256, 64), jnp.float32))
        _g = jax.random.normal(jax.random.fold_in(_rk, 9001), (2, 4), jnp.float32)
        _g = jnp.sign(_g) * jnp.maximum(jnp.abs(_g), 1.0) + (_g == 0) * 1.0
        g_xattn = _g[0]
        g_ffn = _g[1]
        return (x, ctx_512, g_xattn, g_ffn)
    x, ctx_512, g_xattn, g_ffn = _rec_inputs()

    def _L0_xattn_setup():
        import jax, jax.numpy as jnp
        import numpy as np
        B, N, D = (16, 256, 64)
        H = 4
        TOP_K_RATIO = 0.3
        key = jax.random.key(seed)
        k1, k2, k3, k4 = jax.random.split(key, 4)
        h = jax.random.normal(k1, (B, N, D), dtype=jnp.float32)
        adj_raw = jax.random.uniform(k2, (B, N, N), dtype=jnp.float32)
        lim = 1.0 / np.sqrt(D)
        Wq = jax.random.uniform(k3, (D, D), minval=-lim, maxval=lim, dtype=jnp.float32)
        Wk = jax.random.uniform(k4, (D, D), minval=-lim, maxval=lim, dtype=jnp.float32)
        gamma_raw = jnp.float32(-0.85)
        return {'h': h, 'adj_raw': adj_raw, 'Wq': Wq, 'Wk': Wk, 'gamma_raw': gamma_raw}
    _L0_xattn_all = _L0_xattn_setup()
    _L0_xattn_in = {k: v for k, v in _L0_xattn_all.items() if k in ('Wq', 'Wk', 'gamma_raw')}
    del _L0_xattn_all

    def _L0_ffn_setup():
        import jax, jax.numpy as jnp
        import numpy as np
        from jax import lax
        H = 256
        I = 176
        E = 16
        TOP_K = 6
        IS = 2 * I

        def _swiglu(x, w13_, w2_):
            gu = x @ w13_.T
            g, u = jnp.split(gu, 2, axis=-1)
            return jax.nn.silu(g) * u @ w2_.T
        key = jax.random.key(seed)
        ks = jax.random.split(key, 6)
        return {'hidden_states': jax.random.normal(ks[0], (1, 256, H), jnp.float32), 'gate_w': jax.random.normal(ks[1], (E, H), jnp.float32) * 0.02, 'w13': jax.random.normal(ks[2], (E, 2 * I, H), jnp.float32) * 0.02, 'w2': jax.random.normal(ks[3], (E, H, I), jnp.float32) * 0.02, 'sw13': jax.random.normal(ks[4], (2 * IS, H), jnp.float32) * 0.02, 'sw2': jax.random.normal(ks[5], (H, IS), jnp.float32) * 0.02}
    _L0_ffn_all = _L0_ffn_setup()
    _L0_ffn_in = {k: v for k, v in _L0_ffn_all.items() if k in ('gate_w', 'w13', 'w2', 'sw13', 'sw2')}
    del _L0_ffn_all

    def _L1_xattn_setup():
        import jax, jax.numpy as jnp
        import numpy as np
        B, S, L = (2, 128, 128)
        DIM_Q, H, K, D_C, D_CQ, R = (256, 16, 128, 64, 192, 64)

        def _rope_tables(seq_len, dim, dtype):
            inv_freq = 1.0 / 10000.0 ** (jnp.arange(0, dim, 2, dtype=dtype) / dim)
            t = jnp.arange(seq_len, dtype=dtype)
            freqs = t[:, None] * inv_freq[None, :]
            sin = jnp.repeat(jnp.sin(freqs), 2, axis=-1)
            cos = jnp.repeat(jnp.cos(freqs), 2, axis=-1)
            return (sin, cos)

        def _rotate_half(x):
            h = x.shape[-1] // 2
            return jnp.concatenate([-x[..., h:], x[..., :h]], axis=-1)
        key = jax.random.key(seed)
        ks = jax.random.split(key, 8)
        s_in = 1.0 / np.sqrt(DIM_Q)
        s_k = 1.0 / np.sqrt(K)
        s_cq = 1.0 / np.sqrt(D_CQ)
        s_c = 1.0 / np.sqrt(D_C)
        return {'hidden_q': jax.random.normal(ks[0], (B, S, DIM_Q), jnp.float32), 'kv_c': jax.random.normal(ks[1], (B, L, D_C), jnp.float32), 'Wq': jax.random.normal(ks[2], (H * K, DIM_Q), jnp.float32) * s_in, 'w_kc_q': jax.random.normal(ks[3], (H, K, D_CQ), jnp.float32) * s_k, 'w_kc_kv': jax.random.normal(ks[4], (H, K, D_C), jnp.float32) * s_k, 'W_qr': jax.random.normal(ks[5], (H, D_CQ, R), jnp.float32) * s_cq / np.sqrt(R), 'W_kr': jax.random.normal(ks[6], (H, D_C, R), jnp.float32) * s_c, 'Wo': jax.random.normal(ks[7], (DIM_Q, H * K), jnp.float32) * s_k}
    _L1_xattn_all = _L1_xattn_setup()
    _L1_xattn_in = {k: v for k, v in _L1_xattn_all.items() if k in ('Wq', 'w_kc_q', 'w_kc_kv', 'W_qr', 'W_kr', 'Wo')}
    del _L1_xattn_all

    def _L1_ffn_setup():
        import jax, jax.numpy as jnp
        import numpy as np
        EPS = 1e-08

        def _quantize(w):
            gamma = jnp.mean(jnp.abs(w))
            return jnp.clip(jnp.round(w / (gamma + EPS)), -1.0, 1.0)

        def _bitlinear(x, w):
            return jnp.matmul(x, _quantize(w).T)
        key = jax.random.key(seed)
        k1, k2, k3, k4 = jax.random.split(key, 4)
        d, h = (256, 704)
        x = jax.random.normal(k1, (4, 256, d), dtype=jnp.float32)
        w1 = jax.random.normal(k2, (h, d), dtype=jnp.float32)
        w2 = jax.random.normal(k3, (h, d), dtype=jnp.float32)
        w3 = jax.random.normal(k4, (d, h), dtype=jnp.float32)
        return {'x': x, 'w1': w1, 'w2': w2, 'w3': w3}
    _L1_ffn_all = _L1_ffn_setup()
    _L1_ffn_in = {k: v for k, v in _L1_ffn_all.items() if k in ('w1', 'w2', 'w3')}
    del _L1_ffn_all

    def _L2_xattn_setup():
        import jax, jax.numpy as jnp
        import numpy as np
        import math
        D_MODEL = 256
        N_HEADS = 16
        N_GROUPS = 4
        HEADS_PER_GROUP = N_HEADS // N_GROUPS
        HEAD_DIM = D_MODEL // N_HEADS
        B, S = (2, 256)
        key = jax.random.key(seed)
        k1, k2, k3, k4, k5 = jax.random.split(key, 5)
        q = jax.random.normal(k1, (B, S, D_MODEL), dtype=jnp.float32)
        k = jax.random.normal(k2, (B, S, N_GROUPS * HEAD_DIM), dtype=jnp.float32)
        v = jax.random.normal(k3, (B, S, N_GROUPS * HEAD_DIM), dtype=jnp.float32)
        lim = 1.0 / math.sqrt(D_MODEL)
        Wc = jax.random.uniform(k4, (D_MODEL, D_MODEL), minval=-lim, maxval=lim, dtype=jnp.float32)
        bc = jax.random.uniform(k5, (D_MODEL,), minval=-lim, maxval=lim, dtype=jnp.float32)
        return {'q': q, 'k': k, 'v': v, 'Wc': Wc, 'bc': bc}
    _L2_xattn_all = _L2_xattn_setup()
    _L2_xattn_in = {k: v for k, v in _L2_xattn_all.items() if k in ('Wc', 'bc')}
    del _L2_xattn_all

    def _L2_ffn_setup():
        import jax, jax.numpy as jnp
        import numpy as np
        B, S, D_IN, D_OUT = (4, 256, 256, 256)
        E, R, TOP_K = (8, 8, 2)
        ALPHA = 16.0
        SCALE = ALPHA / R
        key = jax.random.key(seed)
        ks = jax.random.split(key, 6)
        x = jax.random.normal(ks[0], (B, S, D_IN), dtype=jnp.float32)
        W_base = jax.random.normal(ks[1], (D_OUT, D_IN), dtype=jnp.float32) / np.sqrt(D_IN)
        b_base = jax.random.normal(ks[2], (D_OUT,), dtype=jnp.float32) * 0.01
        W_router = jax.random.normal(ks[3], (E, D_IN), dtype=jnp.float32) / np.sqrt(D_IN)
        A_w = jax.random.normal(ks[4], (E, R, D_IN), dtype=jnp.float32) / np.sqrt(D_IN)
        B_w = jax.random.normal(ks[5], (E, D_OUT, R), dtype=jnp.float32) * 0.02
        return {'x': x, 'W_base': W_base, 'b_base': b_base, 'W_router': W_router, 'A_w': A_w, 'B_w': B_w}
    _L2_ffn_all = _L2_ffn_setup()
    _L2_ffn_in = {k: v for k, v in _L2_ffn_all.items() if k in ('W_base', 'b_base', 'W_router', 'A_w', 'B_w')}
    del _L2_ffn_all

    def _L3_xattn_setup():
        import jax, jax.numpy as jnp
        import numpy as np
        B, S, H, NH, L = (2, 256, 256, 16, 64)
        HD = H // NH
        key = jax.random.key(seed)
        k1, k2, k3, k4, k5 = jax.random.split(key, 5)
        scale = 0.02
        return {'q': jax.random.normal(k1, (B, S, H), dtype=jnp.float32), 'latent_kv': jax.random.normal(k2, (B, S, L), dtype=jnp.float32), 'Wq': jax.random.normal(k3, (H, H), dtype=jnp.float32) * scale, 'Wkv_expand': jax.random.normal(k4, (2 * H, L), dtype=jnp.float32) * scale, 'Wout': jax.random.normal(k5, (H, H), dtype=jnp.float32) * scale}
    _L3_xattn_all = _L3_xattn_setup()
    _L3_xattn_in = {k: v for k, v in _L3_xattn_all.items() if k in ('Wq', 'Wkv_expand', 'Wout')}
    del _L3_xattn_all

    def _L3_ffn_setup():
        import jax, jax.numpy as jnp
        import numpy as np
        D = 256
        E = 8
        R = 16
        K = 2
        INIT_BONUS = 3.0
        ANNEAL_STEPS = 625
        CURRENT_STEP = 1
        key = jax.random.key(seed)
        ks = jax.random.split(key, 7)
        s_in = 1.0 / np.sqrt(D)
        s_r = 1.0 / np.sqrt(R)
        return {'x': jax.random.normal(ks[0], (2, 512, D), dtype=jnp.float32), 'Wr': jax.random.normal(ks[1], (D, E), dtype=jnp.float32) * s_in, 'br': jax.random.normal(ks[2], (E,), dtype=jnp.float32) * 0.01, 'Wd': jax.random.normal(ks[3], (E, D, R), dtype=jnp.float32) * s_in, 'bd': jnp.zeros((E, R), dtype=jnp.float32), 'Wu': jax.random.normal(ks[4], (E, R, D), dtype=jnp.float32) * s_r, 'bu': jnp.zeros((E, D), dtype=jnp.float32)}
    _L3_ffn_all = _L3_ffn_setup()
    _L3_ffn_in = {k: v for k, v in _L3_ffn_all.items() if k in ('Wr', 'br', 'Wd', 'bd', 'Wu', 'bu')}
    del _L3_ffn_all
    return {'x': x, 'ctx_512': ctx_512, 'g_xattn': g_xattn, 'g_ffn': g_ffn, 'L0_xattn_Wq': _L0_xattn_in['Wq'], 'L0_xattn_Wk': _L0_xattn_in['Wk'], 'L0_xattn_gamma_raw': _L0_xattn_in['gamma_raw'], 'L0_ffn_gate_w': _L0_ffn_in['gate_w'], 'L0_ffn_w13': _L0_ffn_in['w13'], 'L0_ffn_w2': _L0_ffn_in['w2'], 'L0_ffn_sw13': _L0_ffn_in['sw13'], 'L0_ffn_sw2': _L0_ffn_in['sw2'], 'L1_xattn_Wq': _L1_xattn_in['Wq'], 'L1_xattn_w_kc_q': _L1_xattn_in['w_kc_q'], 'L1_xattn_w_kc_kv': _L1_xattn_in['w_kc_kv'], 'L1_xattn_W_qr': _L1_xattn_in['W_qr'], 'L1_xattn_W_kr': _L1_xattn_in['W_kr'], 'L1_xattn_Wo': _L1_xattn_in['Wo'], 'L1_ffn_w1': _L1_ffn_in['w1'], 'L1_ffn_w2': _L1_ffn_in['w2'], 'L1_ffn_w3': _L1_ffn_in['w3'], 'L2_xattn_Wc': _L2_xattn_in['Wc'], 'L2_xattn_bc': _L2_xattn_in['bc'], 'L2_ffn_W_base': _L2_ffn_in['W_base'], 'L2_ffn_b_base': _L2_ffn_in['b_base'], 'L2_ffn_W_router': _L2_ffn_in['W_router'], 'L2_ffn_A_w': _L2_ffn_in['A_w'], 'L2_ffn_B_w': _L2_ffn_in['B_w'], 'L3_xattn_Wq': _L3_xattn_in['Wq'], 'L3_xattn_Wkv_expand': _L3_xattn_in['Wkv_expand'], 'L3_xattn_Wout': _L3_xattn_in['Wout'], 'L3_ffn_Wr': _L3_ffn_in['Wr'], 'L3_ffn_br': _L3_ffn_in['br'], 'L3_ffn_Wd': _L3_ffn_in['Wd'], 'L3_ffn_bd': _L3_ffn_in['bd'], 'L3_ffn_Wu': _L3_ffn_in['Wu'], 'L3_ffn_bu': _L3_ffn_in['bu']}

def reference(x, ctx_512, g_xattn, g_ffn, L0_xattn_Wq, L0_xattn_Wk, L0_xattn_gamma_raw, L0_ffn_gate_w, L0_ffn_w13, L0_ffn_w2, L0_ffn_sw13, L0_ffn_sw2, L1_xattn_Wq, L1_xattn_w_kc_q, L1_xattn_w_kc_kv, L1_xattn_W_qr, L1_xattn_W_kr, L1_xattn_Wo, L1_ffn_w1, L1_ffn_w2, L1_ffn_w3, L2_xattn_Wc, L2_xattn_bc, L2_ffn_W_base, L2_ffn_b_base, L2_ffn_W_router, L2_ffn_A_w, L2_ffn_B_w, L3_xattn_Wq, L3_xattn_Wkv_expand, L3_xattn_Wout, L3_ffn_Wr, L3_ffn_br, L3_ffn_Wd, L3_ffn_bd, L3_ffn_Wu, L3_ffn_bu):
    import jax
    import jax.numpy as jnp

    def _L0_xattn_ref(h, adj_raw, Wq, Wk, gamma_raw):
        import jax, jax.numpy as jnp
        import numpy as np
        B, N, D = (16, 256, 64)
        H = 4
        TOP_K_RATIO = 0.3
        b, n, dm = h.shape
        d = dm // H
        Q = (h @ Wq.T).reshape(b, n, H, d).transpose(0, 2, 1, 3)
        K = (h @ Wk.T).reshape(b, n, H, d).transpose(0, 2, 1, 3)
        sim = jnp.einsum('bhnd,bhmd->bnm', Q, K) / (jnp.sqrt(jnp.float32(d)) * H)
        k = max(1, int(n * TOP_K_RATIO))
        topk_vals = jax.lax.top_k(sim, k)[0]
        threshold = topk_vals[:, :, -1:]
        sparse_mask = (sim >= threshold).astype(sim.dtype)
        A_learned = jax.nn.sigmoid(sim) * sparse_mask
        A_learned = (A_learned + jnp.swapaxes(A_learned, -1, -2)) * 0.5
        gamma = jax.nn.sigmoid(gamma_raw)
        return (1.0 - gamma) * adj_raw + gamma * A_learned

    def _L0_ffn_ref(hidden_states, gate_w, w13, w2, sw13, sw2):
        import jax, jax.numpy as jnp
        import numpy as np
        from jax import lax
        H = 256
        I = 176
        E = 16
        TOP_K = 6
        IS = 2 * I

        def _swiglu(x, w13_, w2_):
            gu = x @ w13_.T
            g, u = jnp.split(gu, 2, axis=-1)
            return jax.nn.silu(g) * u @ w2_.T
        B, S, Hd = hidden_states.shape
        x = hidden_states.reshape(-1, Hd)
        T = x.shape[0]
        scores = jax.nn.softmax(x @ gate_w.T, axis=-1)
        topk_w, topk_ids = lax.top_k(scores, TOP_K)
        topk_w = topk_w / (topk_w.sum(-1, keepdims=True) + 1e-20)
        combine = jnp.einsum('tk,tke->te', topk_w, jax.nn.one_hot(topk_ids, E, dtype=topk_w.dtype))

        def body(acc, ew):
            w13_e, w2_e, c_e = ew
            y = _swiglu(x, w13_e, w2_e)
            return (acc + c_e[:, None] * y, None)
        out, _ = lax.scan(body, jnp.zeros_like(x), (w13, w2, combine.T))
        out = out + _swiglu(x, sw13, sw2)
        return out.reshape(B, S, Hd)

    def _L1_xattn_ref(hidden_q, kv_c, Wq, w_kc_q, w_kc_kv, W_qr, W_kr, Wo):
        import jax, jax.numpy as jnp
        import numpy as np
        B, S, L = (2, 128, 128)
        DIM_Q, H, K, D_C, D_CQ, R = (256, 16, 128, 64, 192, 64)

        def _rope_tables(seq_len, dim, dtype):
            inv_freq = 1.0 / 10000.0 ** (jnp.arange(0, dim, 2, dtype=dtype) / dim)
            t = jnp.arange(seq_len, dtype=dtype)
            freqs = t[:, None] * inv_freq[None, :]
            sin = jnp.repeat(jnp.sin(freqs), 2, axis=-1)
            cos = jnp.repeat(jnp.cos(freqs), 2, axis=-1)
            return (sin, cos)

        def _rotate_half(x):
            h = x.shape[-1] // 2
            return jnp.concatenate([-x[..., h:], x[..., :h]], axis=-1)
        b, s, _ = hidden_q.shape
        l = kv_c.shape[1]
        q_hk = (hidden_q @ Wq.T).reshape(b, s, H, K)
        q_big = jnp.einsum('bshk,hkq->bshq', q_hk, w_kc_q)
        sin, cos = _rope_tables(l, D_C, kv_c.dtype)
        kv_rope = kv_c * cos[None] + _rotate_half(kv_c) * sin[None]
        q_r = jnp.einsum('bshq,hqr->bhsr', q_big, W_qr)
        k_r = jnp.einsum('bld,hdr->bhlr', kv_rope, W_kr)
        scores = jnp.einsum('bhsr,bhlr->bhsl', q_r, k_r)
        attn = jax.nn.softmax(scores, axis=-1)
        ctx_c = jnp.einsum('bhsl,bld->bhsd', attn, kv_rope)
        ctx_lat = jnp.einsum('bhsd,hkd->bshk', ctx_c, w_kc_kv)
        out = ctx_lat.reshape(b, s, H * K) @ Wo.T
        return out

    def _L1_ffn_ref(x, w1, w2, w3):
        import jax, jax.numpy as jnp
        import numpy as np
        EPS = 1e-08

        def _quantize(w):
            gamma = jnp.mean(jnp.abs(w))
            return jnp.clip(jnp.round(w / (gamma + EPS)), -1.0, 1.0)

        def _bitlinear(x, w):
            return jnp.matmul(x, _quantize(w).T)
        x1 = _bitlinear(x, w1)
        x2 = _bitlinear(x, w2)
        hidden = jax.nn.sigmoid(x1) * x2
        return _bitlinear(hidden, w3)

    def _L2_xattn_ref(q, k, v, Wc, bc):
        import jax, jax.numpy as jnp
        import numpy as np
        import math
        D_MODEL = 256
        N_HEADS = 16
        N_GROUPS = 4
        HEADS_PER_GROUP = N_HEADS // N_GROUPS
        HEAD_DIM = D_MODEL // N_HEADS
        B, S = (2, 256)
        b, s, _ = q.shape
        qh = q.reshape(b, s, N_GROUPS, HEADS_PER_GROUP, HEAD_DIM).transpose(0, 2, 3, 1, 4)
        kh = k.reshape(b, s, N_GROUPS, HEAD_DIM).transpose(0, 2, 1, 3)
        vh = v.reshape(b, s, N_GROUPS, HEAD_DIM).transpose(0, 2, 1, 3)
        scale = 1.0 / math.sqrt(HEAD_DIM)
        scores = jnp.einsum('bghsd,bgtd->bghst', qh, kh) * scale
        probs = jax.nn.softmax(scores, axis=-1)
        out = jnp.einsum('bghst,bgtd->bghsd', probs, vh)
        out = out.transpose(0, 3, 1, 2, 4).reshape(b, s, D_MODEL)
        return out @ Wc.T + bc

    def _L2_ffn_ref(x, W_base, b_base, W_router, A_w, B_w):
        import jax, jax.numpy as jnp
        import numpy as np
        B, S, D_IN, D_OUT = (4, 256, 256, 256)
        E, R, TOP_K = (8, 8, 2)
        ALPHA = 16.0
        SCALE = ALPHA / R
        y = jnp.einsum('bsd,od->bso', x, W_base) + b_base
        logits = jnp.einsum('bsd,ed->bse', x, W_router)
        topk_vals, topk_idx = jax.lax.top_k(logits, TOP_K)
        gates = jax.nn.softmax(topk_vals, axis=-1)
        h = jnp.einsum('bsd,erd->bser', x, A_w)
        expert_outs = jnp.einsum('bser,eor->bseo', h, B_w) * SCALE
        topk_outs = jnp.take_along_axis(expert_outs, topk_idx[..., None], axis=2)
        fused = jnp.sum(topk_outs * gates[..., None], axis=2)
        return y + fused

    def _L3_xattn_ref(q, latent_kv, Wq, Wkv_expand, Wout):
        import jax, jax.numpy as jnp
        import numpy as np
        B, S, H, NH, L = (2, 256, 256, 16, 64)
        HD = H // NH
        b, sq, _ = q.shape
        sk = latent_kv.shape[1]
        qp = q @ Wq.T
        kv = latent_kv @ Wkv_expand.T
        k, v = jnp.split(kv, 2, axis=-1)
        qh = qp.reshape(b, sq, NH, HD).transpose(0, 2, 1, 3)
        kh = k.reshape(b, sk, NH, HD).transpose(0, 2, 1, 3)
        vh = v.reshape(b, sk, NH, HD).transpose(0, 2, 1, 3)
        inv_sqrt_d = 1.0 / jnp.sqrt(jnp.float32(HD))
        scores = jnp.einsum('bhqd,bhkd->bhqk', qh, kh) * inv_sqrt_d
        causal = jnp.tril(jnp.ones((sq, sk), dtype=bool))
        scores = jnp.where(causal, scores, jnp.finfo(scores.dtype).min)
        attn = jax.nn.softmax(scores, axis=-1)
        out = jnp.einsum('bhqk,bhkd->bhqd', attn, vh)
        out = out.transpose(0, 2, 1, 3).reshape(b, sq, H)
        return out @ Wout.T

    def _L3_ffn_ref(x, Wr, br, Wd, bd, Wu, bu):
        import jax, jax.numpy as jnp
        import numpy as np
        D = 256
        E = 8
        R = 16
        K = 2
        INIT_BONUS = 3.0
        ANNEAL_STEPS = 625
        CURRENT_STEP = 1
        logits = jnp.einsum('btd,de->bte', x, Wr) + br
        progress = min(CURRENT_STEP / ANNEAL_STEPS, 1.0)
        bonus = INIT_BONUS * (1.0 - progress)
        logits = logits + bonus
        gates = jax.nn.softmax(logits, axis=-1)
        topk_vals, topk_idx = jax.lax.top_k(gates, K)
        topk_vals = topk_vals / topk_vals.sum(axis=-1, keepdims=True)
        w = (jax.nn.one_hot(topk_idx, E, dtype=x.dtype) * topk_vals[..., None]).sum(axis=-2)
        h = jax.nn.relu(jnp.einsum('btd,edr->betr', x, Wd) + bd[None, :, None, :])
        eo = jnp.einsum('betr,erd->betd', h, Wu) + bu[None, :, None, :]
        out = jnp.einsum('bte,betd->btd', w, eo)
        return out
    x = x + jnp.tanh(g_xattn[0]) * _L0_xattn_ref(ctx_512, _layernorm(x, axis=-1), L0_xattn_Wq, L0_xattn_Wk, L0_xattn_gamma_raw)
    x = x + jnp.tanh(g_ffn[0]) * _L0_ffn_ref(_layernorm(x, axis=-1), L0_ffn_gate_w, L0_ffn_w13, L0_ffn_w2, L0_ffn_sw13, L0_ffn_sw2)
    x = x + jnp.tanh(g_xattn[1]) * _L1_xattn_ref(_layernorm(x, axis=-1), ctx_512, L1_xattn_Wq, L1_xattn_w_kc_q, L1_xattn_w_kc_kv, L1_xattn_W_qr, L1_xattn_W_kr, L1_xattn_Wo)
    x = x + jnp.tanh(g_ffn[1]) * _L1_ffn_ref(_layernorm(x, axis=-1), L1_ffn_w1, L1_ffn_w2, L1_ffn_w3)
    x = x + jnp.tanh(g_xattn[2]) * _L2_xattn_ref(_layernorm(x, axis=-1), ctx_512, ctx_512, L2_xattn_Wc, L2_xattn_bc)
    x = x + jnp.tanh(g_ffn[2]) * _L2_ffn_ref(_layernorm(x, axis=-1), L2_ffn_W_base, L2_ffn_b_base, L2_ffn_W_router, L2_ffn_A_w, L2_ffn_B_w)
    x = x + jnp.tanh(g_xattn[3]) * _L3_xattn_ref(_layernorm(x, axis=-1), ctx_512, L3_xattn_Wq, L3_xattn_Wkv_expand, L3_xattn_Wout)
    x = x + jnp.tanh(g_ffn[3]) * _L3_ffn_ref(_layernorm(x, axis=-1), L3_ffn_Wr, L3_ffn_br, L3_ffn_Wd, L3_ffn_bd, L3_ffn_Wu, L3_ffn_bu)
    return x

_drawn_inputs = setup_inputs


def setup_inputs(seed=0):
    import zlib

    import numpy as np

    out = dict(_drawn_inputs(seed))
    spreads = {'L3_ffn_bd': (0.0, 2.0), 'L3_ffn_bu': (0.0, 2.0)}
    factors = {'L0_ffn_gate_w': 8.0,
     'L0_ffn_w13': 8.0,
     'L0_ffn_w2': 8.0,
     'L2_xattn_Wc': 33.388,
     'L2_xattn_bc': 200.0,
     'L2_ffn_W_base': 8.0,
     'L2_ffn_b_base': 200.0,
     'L2_ffn_W_router': 8.0,
     'L2_ffn_A_w': 8.0,
     'L2_ffn_B_w': 8.0,
     'L3_xattn_Wq': 43.243,
     'L3_xattn_Wkv_expand': 32.538,
     'L3_xattn_Wout': 31.506,
     'L3_ffn_Wr': 8.0,
     'L3_ffn_br': 64.0,
     'L3_ffn_Wd': 8.0,
     'L3_ffn_Wu': 8.0,
     'L0_ffn_sw13': 7.037,
     'L0_ffn_sw2': 7.656}
    for name, (base, spread) in spreads.items():
        noise = np.random.default_rng([zlib.crc32(name.encode()), seed]).standard_normal(out[name].shape)
        drawn = base * np.exp(spread * noise) if base else spread * noise
        out[name] = jnp.asarray(drawn.astype(out[name].dtype))
    for name, factor in factors.items():
        out[name] = (out[name] * factor).astype(out[name].dtype)
    return out
```

```python
from contextlib import ExitStack

import concourse.bass as bass
from concourse import mybir

F32 = mybir.dt.float32
BF16 = mybir.dt.bfloat16
ACT = mybir.ActivationFunctionType
ALU = mybir.AluOpType
AX = mybir.AxisListType.X

P = 128
NB = 4
S = 256
D = 256
TILES = NB * S // P
NH = 16
DC = 64
TOPK = int(S * 0.3)
E0, I0, K0 = 16, 176, 6
F0 = E0 * I0 + 2 * I0
CH0 = -(-F0 // P)
PAIRS0 = -(-CH0 // 2)
PART = E0 + 1
H1 = 704
CH1 = -(-H1 // P)
E2, R2 = 8, 8
E3, R3 = 8, 16
LOW = -3.0e38
BONUS = 3.0 * (1.0 - 1.0 / 625.0)

PHASES = ["moe", "latent", "ternary", "grouped", "lora", "causal", "adapter"]
FILLS = {
    "moe": {0: 7, 1: 6, 2: 7, 3: 6, 4: 7, 5: 6, 6: 1, 7: 3},
    "latent": {0: 16, 1: 16, 2: 4, 4: 4, 6: 1, 7: 2},
    "ternary": {0: 2, 1: 2, 2: 2, 6: 1, 7: 1},
    "grouped": {0: 14, 1: 14, 2: 4, 4: 4, 6: 5, 7: 2},
    "lora": {0: 1, 1: 1, 6: 1, 7: 1},
    "causal": {0: 14, 1: 14, 2: 4, 4: 4, 6: 5, 7: 2},
    "adapter": {0: 1, 1: 1, 6: 1, 7: 1},
}
def fills_before(phase, bank):
    n = 2 if bank == 7 else 1
    for name in PHASES[:PHASES.index(phase)]:
        n += NB * FILLS[name].get(bank, 0)
    return n


def fill(phase, bank, b, k):
    return fills_before(phase, bank) + b * FILLS[phase][bank] + k + 1


def build(nc, a, out):
    with ExitStack() as ctx:
        def sb(name, shape, dt=F32):
            return ctx.enter_context(nc.sbuf_tensor(name, shape, dt))

        def sem(name):
            return ctx.enter_context(nc.semaphore(name))

        PS = ctx.enter_context(nc.psum_tensor("PS", [P, 8, 512], F32))

        X = sb("X", [P, TILES, D])
        XN = sb("XN", [P, 2, D])
        XT = [sb(f"XT{p}", [P, 2, S]) for p in range(2)]
        BN = sb("BN", [P, 2, 6])
        MV = sb("MV", [P, 2, 2])
        RS = sb("RS", [P, 2])
        neg_half = sb("neg_half", [P, 2])
        eps = sb("eps", [P, 2])
        carrier = sb("carrier", [P, 4])
        ident = sb("ident", [P, P])
        identb = sb("identb", [P, P], BF16)
        ones = sb("ones", [P, P])
        gates = sb("gates", [P, 9])
        TG = sb("TG", [P, 9])
        CA = sb("CA", [P, 4])
        ctxT = sb("ctxT", [DC + 1, NB * S])
        W_g = sb("W_g", [P, 2, F0])
        W_u = sb("W_u", [P, 2, F0])
        W_d = sb("W_d", [P, CH0, D])
        W_r = sb("W_r", [P, 2, E0])
        sel_e = sb("sel_e", [3 * PART, F0], BF16)
        tanh_g = sb("tanh_g", [P, 2, 512])
        mlp_tmp = sb("mlp_tmp", [P, 4 * 512])
        gated, hidden = mlp_tmp[:, 0:512], mlp_tmp[:, 512:1024]
        H = mlp_tmp[:, 1024:2048].rearrange("p (a b s) -> p a b s", a=2, b=2)
        CT = [sb(f"CT{p}", [3 * PART, S], BF16) for p in range(2)]
        NMAX = sb("NMAX", [P, 2])
        EX = sb("EX", [P, 2, 16])
        Z = sb("Z", [P, 2])
        RZ = sb("RZ", [P, 2])
        SC = sb("SC", [P, 2, 18])
        T8 = sb("T8", [P, 2, 8])
        REP = sb("REP", [P, 2, 18])
        CM = sb("CM", [P, 2, PART])
        SU = sb("SU", [P, 2])
        C3 = sb("C3", [P, 2, P], BF16)
        NW = sb("NW", [P, 2, NH * DC])
        PM = sb("PM", [P, NH // 2, D])
        ropeN = sb("ropeN", [P, 2, 2, DC])
        ropeT = sb("ropeT", [DC, 2, S])
        KR = [sb(f"KR{p}", [DC + 1, S]) for p in range(2)]
        VV = [sb(f"VV{p}", [P, 2, 3 * DC]) for p in range(2)]
        def areas(flat, start):
            at = [start]

            def cut(parts, *shape):
                n = 1
                for x in shape:
                    n *= x
                v = flat[0:parts, at[0]:at[0] + n]
                at[0] += n
                assert at[0] <= flat.shape[1]
                if len(shape) == 2:
                    return v.rearrange("p (a b) -> p a b", a=shape[0])
                if len(shape) == 3:
                    return v.rearrange("p (a b c) -> p a b c", a=shape[0], b=shape[1])
                return v
            return cut

        arena = sb("arena", [P, 8992])
        FG = NH // 4
        fold_w = []
        for slot in range(2):
            cut = areas(arena, slot * 4352)
            fold_w.append([cut(P, 4, D), cut(96, 2, 4, P), cut(DC, 4, 192), cut(DC, 4, DC),
                           cut(P, 4, DC), cut(P, 4, D)])
        cut = areas(arena, 0)
        qT1 = cut(DC + 1, NH, S)
        probs = cut(P, 2, 2, 512)
        OT1 = cut(P, NH // 2, S)
        NM = cut(P, 2, NH)
        NMT = cut(NH, S)
        RD = cut(P, 2, S)
        cut = areas(arena, 0)
        QT, KTB, VB, OTR = cut(P, 4, S), cut(P, 4, S), cut(P, 2, 512), cut(P, 4, S)
        OTN = areas(arena, 4096 + 2048)(P, 4, S)
        fold_b = sb("fold_b", [96, 4, 2, DC])
        fold_c = sb("fold_c", [P, 4, DC])
        wqk0 = sb("wqk0", [DC, 2, DC])
        cut = areas(W_d[:, :, :].rearrange("p a b -> p (a b)"), 0)
        sim = [cut(P, 2, S) for _ in range(2)]
        sg = [cut(P, 2, S) for _ in range(2)]
        work = cut(P, 2, S)
        AM = [cut(P, 2, S) for _ in range(2)]
        qk0 = cut(DC, 2, NB * S)
        S2 = cut(P, 2, S)
        g8 = sb("g8", [P, 2, 8])
        cut = areas(W_g[:, :, :].rearrange("p a b -> p (a b)"), 0)
        sel_q2 = cut(P, 4, P)
        wk_2, wv_2 = cut(DC + 1, 512), cut(DC + 1, 512)
        wo_2 = cut(P, 4, D)
        bias_2 = cut(1, D)
        wb_2 = cut(P, 2, D)
        ra_2 = cut(P, 2, E2 + E2 * R2)
        bt_2 = cut(E2 * R2, D)
        biasb_2 = cut(1, D)
        ctxTs = cut(DC, NB * S)
        r3, r4 = cut(DC, S), cut(DC, S)
        cut = areas(W_u[:, :, :].rearrange("p a b -> p (a b)"), 0)
        wq_3 = cut(P, 2, 512)
        wk_3, wv_3 = cut(DC + 1, 512), cut(DC + 1, 512)
        wo_3 = cut(P, 4, D)
        dr_3 = cut(P, 2, E3 * R3 + E3)
        bdr_3 = cut(1, E3 * R3 + E3)
        wu_3 = cut(E3 * R3, D)
        bu_3 = cut(E3, D)
        sel_den = sb("sel_den", [P, P])
        maskS = sb("maskS", [P, P], BF16)
        maskT = sb("maskT", [P, P], BF16)
        w12 = sb("w12", [P, 4, H1])
        w3 = sb("w3", [P, CH1, D])
        absum = sb("absum", [P, 4])
        thr = sb("thr", [P, 2, 3])
        less = mlp_tmp[:, 0:2 * H1]
        HD = areas(arena, 0)(P, CH1, S)
        HW = sb("HW", [P, 2, P])
        HWT = sb("HWT", [P, S])
        WT = sb("WT", [E3, S])
        LG = sb("LG", [P, 2, 14])
        ctxN = sb("ctxN", [P, TILES, DC])
        ctxNs = sb("ctxNs", [P, TILES, DC])
        r1, r2 = sb("r1", [P, 2 * DC]), sb("r2", [P, 2 * DC])
        CB = [sb(f"CB{p}", [DC + 1, S]) for p in range(2)]

        filled = [sem(f"bank_filled{k}") for k in range(8)]
        drained = [sem(f"bank_drained{k}") for k in range(8)]
        consts_set = sem("consts_set")
        ident_ready = sem("ident_ready")
        first_loaded = sem("first_loaded")
        fold_loaded = [sem(f"fold_loaded{n}") for n in range(2)]
        down_loaded = sem("down_loaded")
        expert_loaded = sem("expert_loaded")
        rope_loaded = sem("rope_loaded")
        mlp_loaded = sem("mlp_loaded")
        late_loaded = sem("late_loaded")
        stored = sem("stored")
        v_step = sem("v_step")
        g_step = sem("g_step")
        gates_ready = sem("gates_ready")
        qk_filled, qk_copied = sem("qk_filled"), sem("qk_copied")
        sim_filled, sim_scaled = sem("sim_filled"), sem("sim_scaled")
        masked = sem("masked")
        turned = sem("turned")
        graph_added = sem("graph_added")
        fold_filled, fold_copied = sem("fold_filled"), sem("fold_copied")
        mv_ready, rstd_ready, xn_ready = sem("mv_ready"), sem("rstd_ready"), sem("xn_ready")
        nmax_ready, comb_ready = sem("nmax_ready"), sem("comb_ready")
        tanh_ready, h_used = sem("tanh_ready"), sem("h_used")
        kv_ready = sem("kv_ready")
        max_placed = sem("max_placed")
        abs_ready, abs_summed, thr_ready, ternary_ready = \
            sem("abs_ready"), sem("abs_summed"), sem("thr_ready"), sem("ternary_ready")
        tanh1_ready = sem("tanh1_ready")
        probs_used = sem("probs_used")
        norm_ready = sem("norm_ready")
        exp_ready = sem("exp_ready")
        block = ctx.enter_context(nc.Block())

        def pairs(eng, body):
            with eng.Fori(0, NB // 2) as j:
                for p in range(2):
                    body(j * 2 + p, p, (j * 2 + 1) if p == 0 else (j * -2 + 2))

        def pre_no(phase, b):
            return PHASES.index(phase) * NB + b + 1

        N_FIRST = 5

        @block.sync
        def _(sp):
            xv = a["x"].rearrange("(t p) d -> p t d", p=P)
            sp.dma_start(ctxT[0:DC, :], a["ctxT"]).then_inc(first_loaded, 16)
            sp.dma_start(wqk0[:, :, :], a["wqk0"]).then_inc(first_loaded, 16)
            sp.dma_start(ident[:, :], a["ident"]).then_inc(first_loaded, 16)
            sp.dma_start(gates[:, :], a["gates"]).then_inc(first_loaded, 16)
            sp.dma_start(X[:, :, :], xv).then_inc(first_loaded, 16)

            def fold_group(n):
                for dst, name in zip(fold_w[n % 2], ("wq1", "wkq1T", "wqr1T", "wkr1T", "wkv1", "wo1T")):
                    sp.dma_start(dst, a[name][n]).then_inc(fold_loaded[n % 2], 16)

            fold_group(0)
            fold_group(1)
            sp.dma_start(W_r[:, :, :], a["w_r0"]).then_inc(expert_loaded, 16)
            sp.dma_start(sel_e[:, :], a["sel_e"]).then_inc(expert_loaded, 16)
            sp.dma_start(W_g[:, :, :], a["w_g0"]).then_inc(expert_loaded, 16)
            sp.dma_start(W_u[:, :, :], a["w_u0"]).then_inc(expert_loaded, 16)
            for n in range(2, FG):
                sp.wait_ge(fold_filled, 4 * (n - 2) + 4)
                fold_group(n)
            sp.dma_start(ctxN[:, :, :], a["ctx"].rearrange("(t p) d -> p t d", p=P)).then_inc(rope_loaded, 16)
            sp.dma_start(ctxNs[:, :, :], a["ctx_swapped"].rearrange("(t p) d -> p t d", p=P)) \
                .then_inc(rope_loaded, 16)
            sp.dma_start(ropeN[:, :, :, :], a["ropeN"]).then_inc(rope_loaded, 16)
            sp.dma_start(ropeT[:, :, :], a["ropeT"]).then_inc(rope_loaded, 16)
            sp.dma_start(w12[:, :, :], a["w12"]).then_inc(mlp_loaded, 16)
            full = H1 // P
            sp.dma_start(w3[:, 0:full, :], a["w3T"][0:full * P, :].rearrange("(c p) d -> p c d", p=P)) \
                .then_inc(mlp_loaded, 16)
            sp.dma_start(w3[0:H1 - full * P, full, :], a["w3T"][full * P:H1, :]).then_inc(mlp_loaded, 16)
            sp.wait_ge(graph_added, NB)
            full = F0 // P
            sp.dma_start(W_d[:, 0:full, :], a["w_d0"][0:full * P, :].rearrange("(c p) d -> p c d", p=P)) \
                .then_inc(down_loaded, 16)
            sp.dma_start(W_d[0:F0 - full * P, full, :], a["w_d0"][full * P:F0, :]).then_inc(down_loaded, 16)
            sp.wait_ge(filled[6], fill("moe", 6, NB - 1, 0))
            sp.dma_start(ctxTs, a["ctxT_swapped"]).then_inc(rope_loaded, 16)
            for dst, name in ((sel_q2, "sel_q2"), (wk_2, "sel_k2"), (wv_2, "sel_v2"), (wo_2, "wo_2"),
                              (bias_2, "bias_2"), (wb_2, "wb_2"), (ra_2, "ra_2"), (bt_2, "bt_2"),
                              (biasb_2, "biasb_2"), (wq_3, "wq_3"), (wk_3, "wk_3"), (wv_3, "wv_3"),
                              (wo_3, "wo_3"), (dr_3, "dr_3"), (bdr_3, "bdr_3"), (wu_3, "wu_3"),
                              (bu_3, "bu_3"), (sel_den[:, :], "sel_den"), (maskS[:, :], "maskS"),
                              (maskT[:, :], "maskT")):
                sp.dma_start(dst, a[name]).then_inc(late_loaded, 16)

            def place_max(phase):
                def body(b, p, nb):
                    sp.wait_ge(drained[7], fill(phase, 7, b, 0))
                    if phase == "latent":
                        sp.dma_start(qT1[DC:DC + 1, :, :], NMT).then_inc(max_placed, 16)
                        return
                    for j in range(4):
                        row = 32 * j + 16
                        sp.dma_start(QT[row:row + 1, :, :], NMT[4 * j:4 * j + 4, :]).then_inc(max_placed, 16)
                pairs(sp, body)

            place_max("latent")
            place_max("grouped")
            place_max("causal")
            ov = out.rearrange("(t p) d -> p t d", p=P)
            for b in range(NB):
                sp.wait_ge(drained[6], fill("adapter", 6, b, 0))
                sp.dma_start(ov[:, 2 * b:2 * b + 2, :], X[:, 2 * b:2 * b + 2, :]).then_inc(stored, 16)
            sp.wait_ge(stored, 16 * NB)

        LATE = 16 * 20

        @block.gpsimd
        def _(pool):
            def rstd(n, first=False):
                pool.wait_ge(mv_ready, n + 1)
                if not first:
                    pool.wait_ge(xn_ready, n)
                pool.tensor_tensor(RS[:, :], MV[:, :, 1], eps[:, :], ALU.add).then_inc(g_step, 1)
                pool.wait_ge(g_step, n + 1)
                pool.tensor_tensor(RS[:, :], RS[:, :], neg_half[:, :], ALU.pow).then_inc(rstd_ready, 1)

            pool.wait_ge(consts_set, 1)

            def graph(b, p, nb):
                rstd(b, first=True)
            pairs(pool, graph)
            rstd(NB)
            BASE = NB

            def prepare(phase):
                def body(b, p, nb):
                    rstd(pre_no(phase, b) + BASE)
                return body

            pairs(pool, prepare("moe"))
            pool.wait_ge(rope_loaded, 16 * 5)
            pool.wait_ge(first_loaded, 16 * N_FIRST)
            pool.wait_ge(consts_set, 1)

            def rotate(b, p, nb):
                pool.wait_ge(filled[6], fills_before("latent", 6) + b - 1)
                s = bass.ts(b, S)
                rn = [ropeN[:, :, k, :] for k in range(2)]
                v1 = r1[:, :].rearrange("p (a b) -> p a b", a=2)
                v2 = r2[:, :].rearrange("p (a b) -> p a b", a=2)
                n = b * 4
                pool.tensor_tensor(v1, ctxN[:, bass.ds(b * 2, 2), :], rn[0], ALU.mult)
                pool.tensor_tensor(v2, ctxNs[:, bass.ds(b * 2, 2), :], rn[1], ALU.mult).then_inc(kv_ready, 1)
                pool.wait_ge(kv_ready, n + 1)
                pool.tensor_tensor(r3[:, :], ctxT[0:DC, s], ropeT[:, 0, :], ALU.mult)
                pool.tensor_tensor(r4[:, :], ctxTs[:, s], ropeT[:, 1, :], ALU.mult).then_inc(kv_ready, 1)
                pool.wait_ge(kv_ready, n + 2)
                pool.tensor_tensor(VV[p][:, :, DC:2 * DC], v1, v2, ALU.add).then_inc(kv_ready, 1)
                pool.wait_ge(kv_ready, n + 3)
                pool.tensor_tensor(KR[p][0:DC, :], r3[:, :], r4[:, :], ALU.add).then_inc(kv_ready, 1)
                pool.wait_ge(kv_ready, n + 4)

            def latent(b, p, nb):
                rotate(b, p, nb)
                prepare("latent")(b, p, nb)
            pairs(pool, latent)

            pool.wait_ge(thr_ready, 1)
            for k, (w, c) in enumerate(((w12[:, 0:2, :], 0), (w12[:, 2:4, :], 1), (w3[:, 0:5, :], 2),
                                        (w3[0:H1 - 5 * P, 5, :], 2))):
                parts = P if k < 3 else H1 - 5 * P
                wf = w.rearrange("p a b -> p (a b)") if k < 3 else w
                n = 2 * H1 if k < 2 else (5 * D if k == 2 else D)
                pool.tensor_scalar(less[0:parts, 0:n], wf, thr[0:parts, 1, c:c + 1], None, ALU.is_lt) \
                    .then_inc(ternary_ready, 1)
                pool.tensor_scalar(wf, wf, thr[0:parts, 0, c:c + 1], None, ALU.is_gt) \
                    .then_inc(ternary_ready, 1)
                pool.wait_ge(ternary_ready, 3 * k + 2)
                pool.tensor_tensor(wf, wf, less[0:parts, 0:n], ALU.subtract).then_inc(ternary_ready, 1)
                pool.wait_ge(ternary_ready, 3 * k + 3)
            pairs(pool, prepare("ternary"))

            def stage(phase):
                def body(b, p, nb):
                    pool.wait_ge(filled[6], fills_before(phase, 6) + (b - 1) * 5)
                    pool.wait_ge(rstd_ready, pre_no(phase, b) + BASE)
                    n = b + 4 * NB + (NB if phase == "causal" else 0)
                    pool.tensor_copy(CB[p][:, :], ctxT[:, bass.ts(b, S)]).then_inc(kv_ready, 1)
                    pool.wait_ge(kv_ready, n + 1)
                    prepare(phase)(b, p, nb)
                return body
            pairs(pool, stage("grouped"))
            pairs(pool, prepare("lora"))
            pairs(pool, stage("causal"))
            for b in range(NB - 1):
                rstd(pre_no("adapter", b) + BASE)

        @block.scalar
        def _(act):
            act.wait_ge(first_loaded, 16 * N_FIRST)
            act.activation(TG[:, 0:8], gates[:, 0:8], ACT.Tanh)
            act.activation(TG[:, 8:9], gates[:, 8:9], ACT.Tanh, scale=0.5).then_inc(gates_ready, 1)
            act.activation(identb[:, :], ident[:, :], ACT.Copy).then_inc(ident_ready, 1)
            for k in range(2):
                act.wait_ge(qk_filled, k + 1)
                act.activation(qk0[:, k, :], PS[0:DC, 4 + 2 * k:6 + 2 * k, :].rearrange("p a b -> p (a b)"),
                               ACT.Copy).then_inc(qk_copied, 1)

            act.wait_ge(sim_filled, 1)
            for b in range(NB):
                p = b % 2
                if b >= 2:
                    act.wait_ge(graph_added, b - 1)
                src = PS[:, b, :].rearrange("p (a b) -> p a b", a=2)
                act.activation(sim[p], src, ACT.Copy, scale=0.0625)
                act.activation(sg[p], src, ACT.Tanh, scale=0.03125).then_inc(sim_scaled, 1)
                n = 4 * b
                act.wait_ge(fold_filled, n + 1)
                act.activation(fold_b[:, :, :, :], PS[0:96, 6, :].rearrange("p (h c d) -> p h c d", h=4, c=2),
                               ACT.Copy).then_inc(fold_copied, 1)
                act.wait_ge(fold_filled, n + 2)
                act.activation(fold_c[:, :, :], PS[:, 7, 0:4 * DC].rearrange("p (h d) -> p h d", h=4),
                               ACT.Copy).then_inc(fold_copied, 1)
                act.wait_ge(fold_filled, n + 3)
                act.activation(NW[:, :, n * DC:(n + 4) * DC], PS[:, 6, :].rearrange("p (c n) -> p c n", c=2),
                               ACT.Copy).then_inc(fold_copied, 1)
                act.wait_ge(fold_filled, n + 4)
                act.activation(PM[:, 2 * b:2 * b + 2, :], PS[:, 7, :].rearrange("p (h d) -> p h d", h=2),
                               ACT.Copy).then_inc(fold_copied, 1)

            def xt_out(value, p):
                act.wait_ge(filled[7], value)
                act.activation(XT[p][:, :, :], PS[:, 7, :].rearrange("p (c s) -> p c s", c=2), ACT.Copy) \
                    .then_inc(drained[7], 1)

            xt_out(fills_before("moe", 7), 0)

            def moe(b, p, nb):
                act.wait_ge(nmax_ready, b + 1)
                for i in range(2):
                    last = act.activation(EX[:, i, :], PS[:, 7, i * E0:(i + 1) * E0], ACT.Exp,
                                          bias=NMAX[:, i:i + 1], accum_out=Z[:, i:i + 1])
                last.then_inc(drained[7], 1)
                for c in range(PAIRS0):
                    g = c % 2
                    act.wait_ge(filled[g], fill("moe", g, b, c // 2))
                    if c >= 2:
                        act.wait_ge(drained[g], fill("moe", g, b, c // 2 - 1))
                    else:
                        act.wait_ge(drained[g], fill("moe", g, b, -1))
                    if c == PAIRS0 - 1:
                        act.activation(tanh_g[0:F0 % P, g, 0:S], PS[0:F0 % P, g, 0:S], ACT.Tanh, scale=0.5) \
                            .then_inc(tanh_ready, 1)
                    else:
                        act.activation(tanh_g[:, g, :], PS[:, g, :], ACT.Tanh, scale=0.5) \
                            .then_inc(tanh_ready, 1)
                    if c == 1:
                        act.wait_ge(filled[7], fill("moe", 7, b, 1))
                        act.activation(CT[p][:, :], PS[0:3 * PART, 7, 0:P].bitcast(BF16), ACT.Copy) \
                            .then_inc(drained[7], 1)
                xt_out(fill("moe", 7, b, 2), 1 - p)
            pairs(act, moe)

            def latent(b, p, nb):
                act.wait_ge(filled[6], fills_before("latent", 6) + b)
                for hp in range(NH // 2):
                    k = hp % 2
                    act.wait_ge(filled[k], fill("latent", k, b, hp // 2))
                    act.activation(qT1[0:DC, 2 * hp, :], PS[0:DC, k, 0:S], ACT.Copy)
                    act.activation(qT1[0:DC, 2 * hp + 1, :], PS[DC:P, k, 0:S], ACT.Copy) \
                        .then_inc(drained[k], 1)
                act.wait_ge(filled[7], fill("latent", 7, b, 0))
                act.activation(NMT, PS[0:NH, 7, 0:S], ACT.Copy).then_inc(drained[7], 1)
                xt_out(fill("latent", 7, b, 1), 1 - p)
                for hp in range(NH // 2):
                    s = hp % 2
                    act.wait_ge(filled[2 + 2 * s], fill("latent", 2 + 2 * s, b, hp // 2))
                    act.wait_ge(filled[s], fill("latent", s, b, 12 + hp // 2 - 1))
                    act.activation(probs[:, s, :, :], PS[:, 2 + 2 * s:4 + 2 * s, :], ACT.Exp) \
                        .then_inc(drained[2 + 2 * s], 1)
            pairs(act, latent)

            def ternary(b, p, nb):
                for k in range(CH1):
                    m = min(P, H1 - k * P)
                    act.wait_ge(filled[k % 3], fill("ternary", k % 3, b, k // 3))
                    if k >= 2:
                        act.wait_ge(drained[(k - 2) % 3], fill("ternary", (k - 2) % 3, b, (k - 2) // 3))
                    else:
                        act.wait_ge(drained[(k + 1) % 3], fill("ternary", (k + 1) % 3, b, -1))
                    act.activation(tanh_g[0:m, k % 2, 0:S], PS[0:m, k % 3, 0:S], ACT.Tanh, scale=0.5) \
                        .then_inc(tanh1_ready, 1)
                xt_out(fill("ternary", 7, b, 0), 1 - p)
            pairs(act, ternary)

            def attention(phase):
                def body(b, p, nb):
                    for g in range(4):
                        act.wait_ge(filled[g % 2], fill(phase, g % 2, b, g // 2))
                        act.activation(QT[:, g, :], PS[:, g % 2, 0:S], ACT.Copy).then_inc(drained[g % 2], 1)
                    for g in range(2):
                        act.wait_ge(filled[g], fill(phase, g, b, 2))
                        act.activation(KTB[:, 2 * g:2 * g + 2, :],
                                       PS[:, g, :].rearrange("p (a s) -> p a s", a=2), ACT.Copy) \
                            .then_inc(drained[g], 1)
                    for t in range(2):
                        act.wait_ge(filled[t], fill(phase, t, b, 3))
                        act.activation(VB[:, t, :], PS[:, t, :], ACT.Copy).then_inc(drained[t], 1)
                    act.wait_ge(filled[7], fill(phase, 7, b, 0))
                    act.activation(NMT, PS[0:NH, 7, 0:S], ACT.Copy).then_inc(drained[7], 1)
                    xt_out(fill(phase, 7, b, 1), 1 - p)
                    half = 4 * b if phase == "grouped" else 4 * b + 4 * NB
                    for hp in range(NH // 2):
                        s, g = hp % 2, hp // 2
                        act.wait_ge(filled[2 + 2 * s], fill(phase, 2 + 2 * s, b, hp // 2))
                        if s == 0 and g:
                            act.wait_ge(probs_used, half + g)
                        elif g:
                            act.wait_ge(filled[(g - 1) % 2], fill(phase, (g - 1) % 2, b, 12 + (g - 1) // 2))
                        n = 512 if phase == "grouped" else 384
                        act.activation(probs[:, s, :, 0:n], PS[:, 2 + 2 * s:4 + 2 * s, 0:n], ACT.Exp,
                                       scale=0.25).then_inc(drained[2 + 2 * s], 1)
                        if s == 0 and g:
                            take(phase, b, g - 1)
                    take(phase, b, 3)
                return body

            def take(phase, b, g):
                act.wait_ge(filled[g % 2], fill(phase, g % 2, b, 12 + g // 2))
                act.activation(OTR[:, g, :], PS[:, g % 2, 0:S], ACT.Copy).then_inc(drained[g % 2], 1)

            pairs(act, attention("grouped"))

            def lora(b, p, nb):
                act.wait_ge(nmax_ready, NB + b + 1)
                for i in range(2):
                    last = act.activation(EX[:, i, 0:E2], LG[:, i, 0:E2], ACT.Exp, bias=NMAX[:, i:i + 1])
                last.then_inc(exp_ready, 1)
                act.wait_ge(filled[1], fill("lora", 1, b, 0))
                act.activation(HWT[0:E2 * R2, :], PS[0:E2 * R2, 1, 0:S], ACT.Copy).then_inc(drained[1], 1)
                xt_out(fill("lora", 7, b, 0), 1 - p)
            pairs(act, lora)
            pairs(act, attention("causal"))

            def adapter(b, p, nb):
                act.wait_ge(nmax_ready, 2 * NB + b + 1)
                for i in range(2):
                    last = act.activation(EX[:, i, 0:E3], LG[:, i, 0:E3], ACT.Exp, bias=NMAX[:, i:i + 1],
                                          accum_out=Z[:, i:i + 1])
                last.then_inc(exp_ready, 1)
                act.wait_ge(filled[1], fill("adapter", 1, b, 0))
                act.activation(HWT[:, :], PS[:, 1, 0:S], ACT.Copy)
                act.activation(WT[:, :], PS[0:E3, 1, S:2 * S], ACT.Copy).then_inc(drained[1], 1)
                if b < NB - 1:
                    xt_out(fill("adapter", 7, b, 0), 1 - p)
            for b in range(NB):
                adapter(b, b % 2, None)

        @block.vector
        def _(dve):
            done = [0, 0]

            parts = [0]

            def part():
                k = parts[0] % 4
                parts[0] += 1
                dve.memset(carrier[:, k:k + 1], 0.0)

            def start(at_):
                done[0], done[1] = at_, 0

            def link(ins):
                ins.then_inc(v_step, 1)
                done[1] += 1
                dve.wait_ge(v_step, done[0] + done[1])

            def loop(name, body, count):
                base = v_total[0]
                def one(b, p, nb):
                    start(base + b * count)
                    body(b, p, nb)
                    assert done[1] == count, (name, done[1])
                pairs(dve, one)
                v_total[0] = base + NB * count
                start(v_total[0])

            v_total = [0]

            def stats(b):
                link(dve.bn_stats(BN[:, 0, :], X[:, b * 2, :]))
                link(dve.bn_stats(BN[:, 1, :], X[:, b * 2 + 1, :]))
                part()
                dve.bn_aggr(MV[:, 0, :], BN[:, 0, :])
                dve.bn_aggr(MV[:, 1, :], BN[:, 1, :]).then_inc(mv_ready, 1)

            def normalise(n, b, used):
                dve.wait_ge(rstd_ready, n + 1)
                if used is not None:
                    dve.wait_ge(filled[7], used)
                for i in range(2):
                    last = dve.tensor_scalar(XN[:, i, :], X[:, b * 2 + i, :], MV[:, i, 0:1], RS[:, i:i + 1],
                                             ALU.subtract, ALU.mult)
                last.then_inc(xn_ready, 1)

            def prepare_stats(phase, b, nb):
                stats(nb)

            def prepare_norm(phase, b, nb):
                normalise(pre_no(phase, b) + NB, nb, fill(phase, 7, b, -1))

            def add_residual(phase, b, k, gate):
                dve.wait_ge(filled[6], fill(phase, 6, b, k))
                xb = X[:, bass.ds(b * 2, 2), :]
                dve.scalar_tensor_tensor(xb, PS[:, 6, :].rearrange("p (a d) -> p a d", a=2), gate, xb,
                                         ALU.mult, ALU.add).then_inc(drained[6], 1)
                dve.wait_ge(drained[6], fill(phase, 6, b, k))

            for dst, value in ((neg_half[:, :], -0.5), (eps[:, :], 1e-5), (ones[:, :], 1.0),
                               (ctxT[DC:DC + 1, :], 1.0), (KR[0][DC:DC + 1, :], 1.0),
                               (KR[1][DC:DC + 1, :], 1.0), (VV[0][:, :, :], 1.0), (VV[1][:, :, :], 1.0),
                               (SC[:, :, :], LOW), (LG[:, :, :], LOW), (CM[:, :, :], 0.5),
                               (HW[:, :, :], 0.0), (C3[:, :, :], 0.0)):
                last = dve.memset(dst, value)
            last.then_inc(consts_set, 1)

            dve.wait_ge(gates_ready, 1)
            start(0)
            link(dve.tensor_scalar(CA[:, 2:3], TG[:, 8:9], -0.5, 0.5, ALU.mult, ALU.add))
            link(dve.tensor_tensor(CA[:, 0:1], CA[:, 2:3], TG[:, 0:1], ALU.mult))
            link(dve.tensor_scalar(CA[:, 3:4], TG[:, 8:9], 0.125, 0.125, ALU.mult, ALU.add))
            link(dve.tensor_tensor(CA[:, 1:2], CA[:, 3:4], TG[:, 0:1], ALU.mult))
            link(dve.tensor_scalar(CA[:, 2:3], TG[:, 5:6], 0.5, None, ALU.mult))
            v_total[0] = 5

            rounds = (TOPK - 1) // 8

            def graph(b, p, nb):
                stats(b)
                dve.wait_ge(sim_scaled, b + 1)
                n = 0
                for r in range(rounds + 1):
                    cur = sim[p] if r == 0 else work
                    part()
                    for i in range(2):
                        last = dve.max(g8[:, i, :], cur[:, i, :])
                    link(last)
                    if r < rounds:
                        part()
                        for i in range(2):
                            last = dve.match_replace(work[:, i, :], g8[:, i, :], cur[:, i, :], LOW)
                        link(last)
                link(dve.tensor_scalar(sg[p], sg[p], 1.0, None, ALU.add))
                kth = (TOPK - 1) % 8
                for i in range(2):
                    last = dve.scalar_tensor_tensor(AM[p][:, i, :], sim[p][:, i, :], g8[:, i, kth:kth + 1],
                                                    sg[p][:, i, :], ALU.is_ge, ALU.mult)
                last.then_inc(masked, 1)
                normalise(b, b, None)
                dve.wait_ge(xn_ready, b + 1)
                xb = X[:, bass.ds(b * 2, 2), :]
                link(dve.scalar_tensor_tensor(xb, XN[:, :, :], CA[:, 0:1], xb, ALU.mult, ALU.add))
                dve.wait_ge(masked, b + 1)
                dve.wait_ge(turned, b + 1)
                link(dve.tensor_tensor(S2, AM[p], PS[:, 4 + p, :].rearrange("p (a s) -> p a s", a=2),
                                       ALU.add))
                dve.scalar_tensor_tensor(xb, S2, CA[:, 1:2], xb, ALU.mult, ALU.add).then_inc(graph_added, 1)
                dve.wait_ge(graph_added, b + 1)
            loop("graph", graph, 2 + 2 * rounds + 1 + 1 + 2)

            stats(0)
            normalise(NB, 0, None)
            dve.wait_ge(mlp_loaded, 16 * 3)
            link(dve.memset(absum[:, :], 0.0))
            dve.tensor_reduce(absum[:, 0:1], w12[:, 0:2, :].rearrange("p a b -> p (a b)"), AX, ALU.add,
                              apply_absolute_value=True)
            dve.tensor_reduce(absum[:, 1:2], w12[:, 2:4, :].rearrange("p a b -> p (a b)"), AX, ALU.add,
                              apply_absolute_value=True)
            dve.tensor_reduce(absum[:, 2:3], w3[:, 0:5, :].rearrange("p a b -> p (a b)"), AX, ALU.add,
                              apply_absolute_value=True)
            dve.tensor_reduce(absum[0:H1 - 5 * P, 3:4], w3[0:H1 - 5 * P, 5, :], AX, ALU.add,
                              apply_absolute_value=True).then_inc(abs_ready, 1)
            v_total[0] = done[0] + done[1]
            dve.wait_ge(consts_set, 1)

            def moe(b, p, nb):
                dve.wait_ge(filled[7], fill("moe", 7, b, 0))
                dve.tensor_reduce(NMAX[:, :], PS[:, 7, 0:2 * E0].rearrange("p (a e) -> p a e", a=2), AX, ALU.max,
                                  negate=True).then_inc(nmax_ready, 1)
                dve.wait_ge(drained[7], fill("moe", 7, b, 0))
                link(dve.reciprocal(RZ[:, :], Z[:, :]))
                for i in range(2):
                    last = dve.tensor_scalar(SC[:, i, 0:E0], EX[:, i, :], RZ[:, i:i + 1], None, ALU.mult)
                link(last)
                part()
                for i in range(2):
                    last = dve.max(T8[:, i, :], SC[:, i, 0:E0])
                link(last)
                link(dve.memset(T8[:, :, K0:8], LOW))
                part()
                for i in range(2):
                    last = dve.match_replace(REP[:, i, :], T8[:, i, :], SC[:, i, :], 0.0)
                link(last)
                link(dve.tensor_tensor(CM[:, :, 0:E0], SC[:, :, 0:E0], REP[:, :, 0:E0], ALU.subtract))
                link(dve.tensor_reduce(SU[:, :], CM[:, :, 0:E0], AX, ALU.add))
                link(dve.tensor_scalar(SU[:, :], SU[:, :], 1e-20, None, ALU.add))
                link(dve.reciprocal(SU[:, :], SU[:, :]))
                for i in range(2):
                    last = dve.tensor_scalar(CM[:, i, 0:E0], CM[:, i, 0:E0], SU[:, i:i + 1], 0.5,
                                             ALU.mult, ALU.mult)
                link(last)
                link(dve.tensor_copy(C3[:, :, 0:PART], CM[:, :, :]))
                link(dve.tensor_tensor(REP[:, :, 0:PART], CM[:, :, :], C3[:, :, 0:PART], ALU.subtract))
                link(dve.tensor_copy(C3[:, :, PART:2 * PART], REP[:, :, 0:PART]))
                dve.tensor_tensor(C3[:, :, 2 * PART:3 * PART], REP[:, :, 0:PART], C3[:, :, PART:2 * PART],
                                  ALU.subtract).then_inc(comb_ready, 1)
                for c in range(PAIRS0):
                    g, m, n = c % 2, P, 512
                    if c == PAIRS0 - 1:
                        m, n = F0 % P, S
                    dve.wait_ge(tanh_ready, b * PAIRS0 + c + 1)
                    dve.scalar_tensor_tensor(gated[0:m, 0:n], tanh_g[0:m, g, 0:n], 1.0, PS[0:m, g, 0:n],
                                             ALU.add, ALU.mult).then_inc(drained[g], 1)
                    dve.wait_ge(drained[g], fill("moe", g, b, c // 2))
                    dve.wait_ge(filled[2 + g], fill("moe", 2 + g, b, c // 2))
                    dve.tensor_tensor(hidden[0:m, 0:n], gated[0:m, 0:n], PS[0:m, 2 + g, 0:n], ALU.mult) \
                        .then_inc(drained[2 + g], 1)
                    dve.wait_ge(drained[2 + g], fill("moe", 2 + g, b, c // 2))
                    dve.wait_ge(filled[4 + g], fill("moe", 4 + g, b, c // 2))
                    if c >= 2:
                        dve.wait_ge(h_used, b * (PAIRS0 - 1) + c - 1)
                    dve.tensor_tensor(H[0:m, g, :, :].rearrange("p a s -> p (a s)")[:, 0:n], hidden[0:m, 0:n],
                                      PS[0:m, 4 + g, 0:n], ALU.mult).then_inc(drained[4 + g], 1)
                    if c == 8:
                        prepare_stats("moe", b, nb)
                    if c == 10:
                        prepare_norm("moe", b, nb)
                add_residual("moe", b, 0, TG[:, 4:5])
            loop("moe", moe, 15)

            dve.wait_ge(abs_summed, 1)
            link(dve.tensor_copy(less[:, 0:4], PS[:, 7, 0:4]))
            link(dve.tensor_tensor(less[:, 2:3], less[:, 2:3], less[:, 3:4], ALU.add))
            link(dve.tensor_scalar(less[:, 0:3], less[:, 0:3], 1.0 / (H1 * D), 1e-8, ALU.mult, ALU.add))
            link(dve.tensor_scalar(thr[:, 0, :], less[:, 0:3], 0.5, None, ALU.mult))
            dve.tensor_scalar(thr[:, 1, :], less[:, 0:3], -0.5, None, ALU.mult).then_inc(thr_ready, 1)
            v_total[0] += 4

            def latent(b, p, nb):
                dve.wait_ge(filled[7], fill("latent", 7, b, -1))
                for h in range(NH):
                    k = h % 2
                    dve.wait_ge(filled[k], fill("latent", k, b, 4 + h // 2))
                    dve.tensor_reduce(NM[:, :, h], PS[:, k, :].rearrange("p (a s) -> p a s", a=2), AX, ALU.max,
                                      negate=True).then_inc(drained[k], 1)
                prepare_stats("latent", b, nb)
                prepare_norm("latent", b, nb)
                dve.wait_ge(filled[6], fill("latent", 6, b, -1))
                for hp in range(NH // 2):
                    k = hp % 2
                    dve.wait_ge(filled[k], fill("latent", k, b, 12 + hp // 2))
                    dve.reciprocal(RD[0:DC, k, :], PS[DC:P, k, 0:S])
                    link(dve.reciprocal(RD[DC:P, k, :], PS[0:DC, k, S:2 * S]))
                    dve.tensor_tensor(OT1[0:DC, hp, :], PS[0:DC, k, 0:S], RD[0:DC, k, :], ALU.mult)
                    dve.tensor_tensor(OT1[DC:P, hp, :], PS[DC:P, k, S:2 * S], RD[DC:P, k, :], ALU.mult) \
                        .then_inc(drained[k], 1)
                add_residual("latent", b, 0, TG[:, 1:2])
            loop("latent", latent, 2 + 8)

            def ternary(b, p, nb):
                dve.wait_ge(filled[6], fill("ternary", 6, b, -1))
                for k in range(CH1):
                    m = min(P, H1 - k * P)
                    dve.wait_ge(tanh1_ready, b * CH1 + k + 1)
                    dve.scalar_tensor_tensor(HD[0:m, k, :], tanh_g[0:m, k % 2, 0:S], 1.0,
                                             PS[0:m, k % 3, S:2 * S], ALU.add, ALU.mult) \
                        .then_inc(drained[k % 3], 1)
                prepare_stats("ternary", b, nb)
                prepare_norm("ternary", b, nb)
                add_residual("ternary", b, 0, CA[:, 2:3])
            loop("ternary", ternary, 2)

            def attention(phase, gate):
                def body(b, p, nb):
                    dve.wait_ge(filled[7], fill(phase, 7, b, -1))
                    for h in range(NH):
                        k, g, j = h % 2, h // 4, h % 4
                        col = j * 4 + g
                        dve.wait_ge(filled[k], fill(phase, k, b, 4 + h // 2))
                        if phase == "grouped":
                            dve.tensor_reduce(NM[:, :, col], PS[:, k, :].rearrange("p (a s) -> p a s", a=2), AX,
                                              ALU.max, negate=True).then_inc(drained[k], 1)
                        else:
                            dve.tensor_reduce(NM[:, 0, col:col + 1], PS[:, k, 0:P], AX, ALU.max, negate=True)
                            dve.tensor_reduce(NM[:, 1, col:col + 1], PS[:, k, S:2 * S], AX, ALU.max,
                                              negate=True).then_inc(drained[k], 1)
                    prepare_stats(phase, b, nb)
                    prepare_norm(phase, b, nb)
                    dve.wait_ge(filled[6], fill(phase, 6, b, -1))
                    for g in range(4):
                        dve.wait_ge(filled[6], fill(phase, 6, b, g))
                        dve.reciprocal(RD[:, g % 2, :], PS[:, 6, 0:S]).then_inc(drained[6], 1)
                        dve.wait_ge(drained[6], fill(phase, 6, b, g))
                        dve.tensor_tensor(OTN[:, g, :], OTR[:, g, :], RD[:, g % 2, :], ALU.mult) \
                            .then_inc(norm_ready, 1)
                    add_residual(phase, b, 4, gate)
                return body
            loop("grouped", attention("grouped", TG[:, 2:3]), 2)

            def top_two():
                part()
                for i in range(2):
                    last = dve.max(T8[:, i, :], LG[:, i, 0:8])
                link(last)

            def lora(b, p, nb):
                dve.wait_ge(filled[0], fill("lora", 0, b, 0))
                n = E2 + E2 * R2
                ps = PS[:, 0, 0:2 * n].rearrange("p (a n) -> p a n", a=2)
                link(dve.tensor_copy(LG[:, :, 0:E2], ps[:, :, 0:E2]))
                top_two()
                dve.tensor_scalar(NMAX[:, :], T8[:, :, 0], -1.0, None, ALU.mult).then_inc(nmax_ready, 1)
                dve.wait_ge(nmax_ready, NB + b + 1)
                link(dve.memset(T8[:, :, 2:8], LOW))
                part()
                for i in range(2):
                    last = dve.match_replace(REP[:, i, 0:14], T8[:, i, :], LG[:, i, :], -3.3e38)
                link(last)
                link(dve.tensor_tensor(SC[:, :, 0:E2], LG[:, :, 0:E2], REP[:, :, 0:E2], ALU.not_equal))
                dve.wait_ge(exp_ready, b + 1)
                link(dve.tensor_tensor(SC[:, :, 0:E2], SC[:, :, 0:E2], EX[:, :, 0:E2], ALU.mult))
                link(dve.tensor_reduce(SU[:, :], SC[:, :, 0:E2], AX, ALU.add))
                link(dve.reciprocal(SU[:, :], SU[:, :]))
                for i in range(2):
                    last = dve.tensor_scalar(CM[:, i, 0:E2], SC[:, i, 0:E2], SU[:, i:i + 1], 2.0,
                                             ALU.mult, ALU.mult)
                link(last)
                for i in range(2):
                    w = CM[:, i, 0:E2].unsqueeze(2).to_broadcast([P, E2, R2])
                    last = dve.tensor_tensor(HW[:, i, 0:E2 * R2].rearrange("p (e r) -> p e r", e=E2),
                                             ps[:, i, E2:n].rearrange("p (e r) -> p e r", e=E2), w, ALU.mult)
                last.then_inc(drained[0], 1)
                prepare_stats("lora", b, nb)
                prepare_norm("lora", b, nb)
                add_residual("lora", b, 0, TG[:, 6:7])
            loop("lora", lora, 11)
            loop("causal", attention("causal", TG[:, 3:4]), 2)

            for b in range(NB):
                start(v_total[0])
                dve.wait_ge(filled[0], fill("adapter", 0, b, 0))
                n = E3 * R3 + E3
                ps = PS[:, 0, 0:2 * n].rearrange("p (a n) -> p a n", a=2)
                link(dve.tensor_scalar(LG[:, :, 0:E3], ps[:, :, E3 * R3:n], BONUS, None, ALU.add))
                dve.tensor_reduce(NMAX[:, :], LG[:, :, 0:E3], AX, ALU.max, negate=True).then_inc(nmax_ready, 1)
                dve.wait_ge(exp_ready, NB + b + 1)
                link(dve.reciprocal(RZ[:, :], Z[:, :]))
                for i in range(2):
                    last = dve.tensor_scalar(LG[:, i, 0:E3], EX[:, i, 0:E3], RZ[:, i:i + 1], None, ALU.mult)
                link(last)
                top_two()
                link(dve.memset(T8[:, :, 2:8], LOW))
                part()
                for i in range(2):
                    last = dve.match_replace(REP[:, i, 0:14], T8[:, i, :], LG[:, i, :], 0.0)
                link(last)
                link(dve.tensor_tensor(SC[:, :, 0:E3], LG[:, :, 0:E3], REP[:, :, 0:E3], ALU.subtract))
                link(dve.tensor_reduce(SU[:, :], SC[:, :, 0:E3], AX, ALU.add))
                link(dve.reciprocal(SU[:, :], SU[:, :]))
                for i in range(2):
                    last = dve.tensor_scalar(CM[:, i, 0:E3], SC[:, i, 0:E3], SU[:, i:i + 1], None, ALU.mult)
                link(last)
                for i in range(2):
                    w = CM[:, i, 0:E3].unsqueeze(2).to_broadcast([P, E3, R3])
                    last = dve.scalar_tensor_tensor(HW[:, i, :].rearrange("p (e r) -> p e r", e=E3),
                                                    ps[:, i, 0:E3 * R3].rearrange("p (e r) -> p e r", e=E3),
                                                    0.0, w, ALU.max, ALU.mult)
                last.then_inc(drained[0], 1)
                if b < NB - 1:
                    stats(b + 1)
                    normalise(pre_no("adapter", b) + NB, b + 1, fill("adapter", 7, b, -1))
                add_residual("adapter", b, 0, TG[:, 7:8])
                v_total[0] += done[1]

        @block.tensor
        def _(pe):
            mm = pe.matmul
            pe.wait_ge(consts_set, 1)
            for k in range(8):
                pe.sem_inc(filled[k], 1)
                pe.sem_inc(drained[k], 1)
            pe.wait_ge(first_loaded, 16 * N_FIRST)
            for k in range(2):
                for n in range(2):
                    last = mm(PS[0:DC, 4 + 2 * k + n, :], wqk0[:, k, :], ctxT[0:DC, n * 512:(n + 1) * 512],
                              start=True, stop=True)
                last.then_inc(qk_filled, 1)
            pe.wait_ge(qk_copied, 2)
            for b in range(NB):
                for i in range(2):
                    last = mm(PS[:, b, i * S:(i + 1) * S], qk0[:, 0, (2 * b + i) * P:(2 * b + i + 1) * P],
                              qk0[:, 1, b * S:(b + 1) * S], start=True, stop=True)
            last.then_inc(sim_filled, 1)
            for b in range(NB):
                n = 4 * b
                wq1, wkq1T, wqr1T, wkr1T, wkv1, wo1T = fold_w[b % 2]
                pe.wait_ge(fold_loaded[b % 2], 16 * 6 * (b // 2 + 1))
                if b:
                    pe.wait_ge(fold_copied, n)
                for h in range(4):
                    for c in range(2):
                        last = mm(PS[0:96, 6, (h * 2 + c) * DC:(h * 2 + c + 1) * DC],
                                  wqr1T[:, h, c * 96:(c + 1) * 96], wkr1T[:, h, :],
                                  start=True, stop=True)
                last.then_inc(fold_filled, 1)
                pe.wait_ge(fold_copied, n + 1)
                for h in range(4):
                    for c in range(2):
                        last = mm(PS[:, 7, h * DC:(h + 1) * DC], wkq1T[:, c, h, :], fold_b[:, h, c, :],
                                  start=c == 0, stop=c == 1)
                last.then_inc(fold_filled, 1)
                pe.wait_ge(fold_copied, n + 2)
                for h in range(4):
                    for c in range(2):
                        last = mm(PS[:, 6, c * S + h * DC:c * S + (h + 1) * DC],
                                  wq1[:, h, c * P:(c + 1) * P], fold_c[:, h, :], start=True, stop=True)
                last.then_inc(fold_filled, 1)
                for h in range(4):
                    q = DC * (h % 2)
                    last = mm(PS[q:q + DC, 7, (h // 2) * S:(h // 2 + 1) * S], wkv1[:, h, :],
                              wo1T[:, h, :], start=True, stop=True)
                last.then_inc(fold_filled, 1)
                pe.wait_ge(masked, b + 1)
                if b >= 2:
                    pe.wait_ge(graph_added, b - 1)
                p = b % 2
                for m in range(2):
                    for i in range(2):
                        last = pe.transpose(PS[:, 4 + p, m * S + i * P:m * S + (i + 1) * P],
                                            AM[p][:, i, m * P:(m + 1) * P], ident[:, :])
                last.then_inc(turned, 1)

            def turn(n, drain, value):
                pe.wait_ge(xn_ready, n + 1)
                if drain is not None:
                    pe.wait_ge(drained[7], drain)
                for c in range(2):
                    for i in range(2):
                        last = pe.transpose(PS[:, 7, c * S + i * P:c * S + (i + 1) * P],
                                            XN[:, i, c * P:(c + 1) * P], ident[:, :])
                last.then_inc(filled[7], 1)

            def prepare(phase, b):
                k = FILLS[phase][7] - 1
                turn(pre_no(phase, b) + NB, fill(phase, 7, b, k - 1), None)

            def free(phase, k, b, n):
                pe.wait_ge(drained[k], fill(phase, k, b, n - 1))

            pe.wait_ge(fold_copied, 16)
            turn(NB, None, None)
            pe.wait_ge(graph_added, NB)
            pe.wait_ge(expert_loaded, 16 * 4)
            pe.wait_ge(ident_ready, 1)

            def moe(b, p, nb):
                free("moe", 7, b, 0)
                for i in range(2):
                    for c in range(2):
                        last = mm(PS[:, 7, i * E0:(i + 1) * E0], XT[p][:, c, i * P:(i + 1) * P], W_r[:, c, :],
                                  start=c == 0, stop=c == 1)
                last.then_inc(filled[7], 1)

                def chunks(c):
                    for f in range(2 * c, min(2 * c + 2, CH0)):
                        yield f, f % 2, f * P, min(P, F0 - f * P)

                def up(c):
                    for first, w in ((0, W_g), (2, W_u)):
                        k = first + c % 2
                        free("moe", k, b, c // 2)
                        for f, e, f0, m in chunks(c):
                            for d in range(2):
                                last = mm(PS[0:m, k, e * S:(e + 1) * S], w[:, d, f0:f0 + m], XT[p][:, d, :],
                                          start=d == 0, stop=d == 1)
                        last.then_inc(filled[k], 1)

                def weights(c):
                    k = 4 + c % 2
                    free("moe", k, b, c // 2)
                    for f, e, f0, m in chunks(c):
                        last = mm(PS[0:m, k, e * S:(e + 1) * S], sel_e[:, f0:f0 + m], CT[p][:, :],
                                  start=True, stop=True)
                    last.then_inc(filled[k], 1)

                def down(c):
                    k = 4 + c % 2
                    pe.wait_ge(drained[k], fill("moe", k, b, c // 2))
                    if c == 0:
                        pe.wait_ge(down_loaded, 16 * 2)
                        free("moe", 6, b, 0)
                    for f, e, f0, m in chunks(c):
                        for i in range(2):
                            last = mm(PS[:, 6, i * D:(i + 1) * D], H[0:m, c % 2, e, i * P:(i + 1) * P],
                                      W_d[0:m, f, :], start=f == 0 and i == 0, stop=f == CH0 - 1,
                                      skip_group_check=True)
                    last.then_inc(h_used if c < PAIRS0 - 1 else filled[6], 1)

                for c in range(PAIRS0):
                    up(c)
                    if c == 1:
                        pe.wait_ge(comb_ready, b + 1)
                        free("moe", 7, b, 1)
                        turned_w = PS[:, 7, 0:P].bitcast(BF16)
                        for i in range(2):
                            last = pe.transpose(turned_w[:, i * P:(i + 1) * P], C3[:, i, :], identb[:, :])
                        last.then_inc(filled[7], 1)
                        pe.wait_ge(drained[7], fill("moe", 7, b, 1))
                    if c >= 1:
                        weights(c - 1)
                    if c >= 2:
                        down(c - 2)
                weights(PAIRS0 - 1)
                down(PAIRS0 - 2)
                prepare("moe", b)
                down(PAIRS0 - 1)
            pairs(pe, moe)

            pe.wait_ge(abs_ready, 1)
            pe.wait_ge(drained[7], fill("latent", 7, 0, -1))
            mm(PS[:, 7, 0:4], ones[:, :], absum[:, :], start=True, stop=True).then_inc(abs_summed, 1)

            def put_max(phase, b):
                for k in range(2):
                    free(phase, k, b, 12)
                free(phase, 7, b, 0)
                for i in range(2):
                    last = pe.transpose(PS[0:NH, 7, i * P:(i + 1) * P], NM[:, i, :], ident[:, :])
                last.then_inc(filled[7], 1)

            pe.wait_ge(thr_ready, 1)

            def latent(b, p, nb):
                free("latent", 7, b, 0)
                for hp in range(NH // 2):
                    k = hp % 2
                    free("latent", k, b, hp // 2)
                    for c in range(2):
                        last = mm(PS[:, k, 0:S], NW[:, c, hp * P:(hp + 1) * P], XT[p][:, c, :],
                                  start=c == 0, stop=c == 1)
                    last.then_inc(filled[k], 1)
                pe.wait_ge(kv_ready, b * 4 + 4)
                for k in range(2):
                    free("latent", k, b, 4)
                for h in range(NH):
                    k = h % 2
                    free("latent", k, b, 4 + h // 2)
                    for i in range(2):
                        last = mm(PS[:, k, i * S:(i + 1) * S], qT1[0:DC, h, i * P:(i + 1) * P],
                                  KR[p][0:DC, :], start=True, stop=True)
                    last.then_inc(filled[k], 1)
                put_max("latent", b)
                prepare("latent", b)
                pe.wait_ge(max_placed, b * 16 + 16)

                def scores(hp):
                    k = 2 + 2 * (hp % 2)
                    free("latent", k, b, hp // 2)
                    for e in range(2):
                        for t in range(2):
                            last = mm(PS[:, k + e, t * S:(t + 1) * S], KR[p][:, t * P:(t + 1) * P],
                                      qT1[:, 2 * hp + e, :], start=True, stop=True)
                    last.then_inc(filled[k], 1)

                def values(hp):
                    s = hp % 2
                    pe.wait_ge(drained[2 + 2 * s], fill("latent", 2 + 2 * s, b, hp // 2))
                    free("latent", s, b, 12 + hp // 2)
                    for e in range(2):
                        v0 = DC * (1 - e)
                        for t in range(2):
                            last = mm(PS[:, s, e * S:(e + 1) * S], VV[p][:, t, v0:v0 + P],
                                      probs[:, s, e, t * S:(t + 1) * S], start=t == 0, stop=t == 1)
                    last.then_inc(filled[s], 1)

                for hp in range(NH // 2):
                    scores(hp)
                    if hp:
                        values(hp - 1)
                values(NH // 2 - 1)
                for k in range(2):
                    free("latent", k, b, 16)
                free("latent", 6, b, 0)
                for i in range(2):
                    for hp in range(NH // 2):
                        last = mm(PS[:, 6, i * D:(i + 1) * D], OT1[:, hp, i * P:(i + 1) * P], PM[:, hp, :],
                                  start=hp == 0, stop=hp == NH // 2 - 1)
                last.then_inc(filled[6], 1)
            pairs(pe, latent)

            pe.wait_ge(ternary_ready, 12)

            def ternary(b, p, nb):
                free("ternary", 7, b, 0)

                def down(k):
                    m = min(P, H1 - k * P)
                    pe.wait_ge(drained[k % 3], fill("ternary", k % 3, b, k // 3))
                    if k == 0:
                        free("ternary", 6, b, 0)
                    for i in range(2):
                        last = mm(PS[:, 6, i * D:(i + 1) * D], HD[0:m, k, i * P:(i + 1) * P], w3[0:m, k, :],
                                  start=k == 0 and i == 0, stop=k == CH1 - 1, skip_group_check=True)
                    if k == CH1 - 1:
                        last.then_inc(filled[6], 1)

                for k in range(CH1):
                    m = min(P, H1 - k * P)
                    free("ternary", k % 3, b, k // 3)
                    for w in range(2):
                        for c in range(2):
                            last = mm(PS[0:m, k % 3, w * S:(w + 1) * S], w12[:, 2 * w + c, k * P:k * P + m],
                                      XT[p][:, c, :], start=c == 0, stop=c == 1)
                    last.then_inc(filled[k % 3], 1)
                    if k >= 1:
                        down(k - 1)
                prepare("ternary", b)
                down(CH1 - 1)
            pairs(pe, ternary)
            pe.wait_ge(late_loaded, LATE)

            def attention(phase):
                wk, wv, wo = (wk_2, wv_2, wo_2) if phase == "grouped" else (wk_3, wv_3, wo_3)
                causal = phase == "causal"

                def body(b, p, nb):
                    free(phase, 7, b, 0)
                    for g in range(4):
                        free(phase, g % 2, b, g // 2)
                        if causal:
                            for c in range(2):
                                last = mm(PS[:, g % 2, 0:S], wq_3[:, c, g * P:(g + 1) * P], XT[p][:, c, :],
                                          start=c == 0, stop=c == 1)
                        else:
                            last = mm(PS[:, g % 2, 0:S], sel_q2[:, g, :], XT[p][:, g // 2, :],
                                      start=True, stop=True)
                        last.then_inc(filled[g % 2], 1)
                    kv = b + 4 * NB + (NB if causal else 0) + 1
                    pe.wait_ge(kv_ready, kv)
                    for g in range(2):
                        free(phase, g, b, 2)
                        for e in range(2):
                            last = mm(PS[:, g, e * S:(e + 1) * S], wk[:, (2 * g + e) * P:(2 * g + e + 1) * P],
                                      CB[p][:, :], start=True, stop=True)
                        last.then_inc(filled[g], 1)
                    for t in range(2):
                        free(phase, t, b, 3)
                        mm(PS[:, t, :], CB[p][:, t * P:(t + 1) * P], wv, start=True, stop=True) \
                            .then_inc(filled[t], 1)
                    for k in range(2):
                        free(phase, k, b, 4)
                    for h in range(NH):
                        k, g, j = h % 2, h // 4, h % 4
                        free(phase, k, b, 4 + h // 2)
                        rows = slice(32 * j, 32 * j + 16)
                        for i in range(2):
                            n = P if causal and i == 0 else S
                            last = mm(PS[:, k, i * S:i * S + n], QT[rows, g, i * P:(i + 1) * P],
                                      KTB[rows, g, 0:n], start=True, stop=not causal)
                            if causal:
                                last = mm(PS[:, k, i * S + i * P:i * S + (i + 1) * P], identb[:, :], maskS[:, :],
                                          start=False, stop=True)
                        last.then_inc(filled[k], 1)
                    put_max(phase, b)
                    prepare(phase, b)
                    before = NB + (4 * NB if causal else 0)
                    pe.wait_ge(max_placed, (b * 4 + before + 4) * 16)

                    def scores(hp):
                        k = 2 + 2 * (hp % 2)
                        free(phase, k, b, hp // 2)
                        for e in range(2):
                            h = 2 * hp + e
                            g, j = h // 4, h % 4
                            rows = slice(32 * j, 32 * j + 17)
                            for t in range(2):
                                q0 = P if causal and t == 1 else 0
                                last = mm(PS[:, k + e, t * S:t * S + S - q0], KTB[rows, g, t * P:(t + 1) * P],
                                          QT[rows, g, q0:S], start=True, stop=not causal)
                                if causal:
                                    last = mm(PS[:, k + e, t * S:t * S + P], identb[:, :], maskT[:, :],
                                              start=False, stop=True)
                        last.then_inc(filled[k], 1)

                    def values(hp):
                        s, g = hp % 2, hp // 2
                        pe.wait_ge(drained[2 + 2 * s], fill(phase, 2 + 2 * s, b, hp // 2))
                        if s == 0:
                            free(phase, g % 2, b, 12 + g // 2)
                        for e in range(2):
                            h = 2 * hp + e
                            j = h % 4
                            for t in range(2):
                                q0 = P if causal and t == 1 else 0
                                last = mm(PS[32 * j:32 * j + 32, g % 2, q0:S], VB[:, t, h * 32:(h + 1) * 32],
                                          probs[:, s, e, t * S:t * S + S - q0], start=t == 0, stop=t == 1,
                                          skip_group_check=True)
                        last.then_inc(probs_used if s == 0 else filled[g % 2], 1)

                    def spread(g):
                        pe.wait_ge(drained[g % 2], fill(phase, g % 2, b, 12 + g // 2))
                        free(phase, 6, b, g)
                        mm(PS[:, 6, 0:S], sel_den[:, :], OTR[:, g, :], start=True, stop=True) \
                            .then_inc(filled[6], 1)

                    for hp in range(NH // 2):
                        scores(hp)
                        if hp:
                            values(hp - 1)
                        if hp >= 3 and hp % 2:
                            spread((hp - 3) // 2)
                    values(NH // 2 - 1)
                    spread(3)
                    free(phase, 6, b, 4)
                    pe.wait_ge(norm_ready, (b + (NB if causal else 0)) * 4 + 4)
                    for i in range(2):
                        for g in range(4):
                            last = mm(PS[:, 6, i * D:(i + 1) * D], OTN[:, g, i * P:(i + 1) * P], wo[:, g, :],
                                      start=g == 0, stop=causal and g == 3)
                        if not causal:
                            last = mm(PS[:, 6, i * D:(i + 1) * D], ones[0:1, :], bias_2, start=False, stop=True)
                    last.then_inc(filled[6], 1)
                return body
            pairs(pe, attention("grouped"))

            def lora(b, p, nb):
                free("lora", 7, b, 0)
                free("lora", 0, b, 0)
                n = E2 + E2 * R2
                for i in range(2):
                    for c in range(2):
                        last = mm(PS[:, 0, i * n:(i + 1) * n], XT[p][:, c, i * P:(i + 1) * P], ra_2[:, c, :],
                                  start=c == 0, stop=c == 1)
                last.then_inc(filled[0], 1)
                free("lora", 6, b, 0)
                for i in range(2):
                    y = PS[:, 6, i * D:(i + 1) * D]
                    for c in range(2):
                        mm(y, XT[p][:, c, i * P:(i + 1) * P], wb_2[:, c, :], start=c == 0 and i == 0, stop=False,
                           skip_group_check=True)
                    mm(y, ones[0:1, :], biasb_2, start=False, stop=False, skip_group_check=True)
                pe.wait_ge(drained[0], fill("lora", 0, b, 0))
                free("lora", 1, b, 0)
                for i in range(2):
                    last = pe.transpose(PS[:, 1, i * P:(i + 1) * P], HW[:, i, :], ident[:, :])
                last.then_inc(filled[1], 1)
                prepare("lora", b)
                pe.wait_ge(drained[1], fill("lora", 1, b, 0))
                for i in range(2):
                    last = mm(PS[:, 6, i * D:(i + 1) * D], HWT[0:E2 * R2, i * P:(i + 1) * P], bt_2,
                              start=False, stop=True, skip_group_check=True)
                last.then_inc(filled[6], 1)
            pairs(pe, lora)
            pairs(pe, attention("causal"))

            for b in range(NB):
                p = b % 2
                free("adapter", 7, b, 0)
                free("adapter", 0, b, 0)
                n = E3 * R3 + E3
                for i in range(2):
                    for c in range(2):
                        mm(PS[:, 0, i * n:(i + 1) * n], XT[p][:, c, i * P:(i + 1) * P], dr_3[:, c, :],
                           start=c == 0, stop=False)
                    last = mm(PS[:, 0, i * n:(i + 1) * n], ones[0:1, :], bdr_3, start=False, stop=True)
                last.then_inc(filled[0], 1)
                pe.wait_ge(drained[0], fill("adapter", 0, b, 0))
                free("adapter", 1, b, 0)
                for i in range(2):
                    pe.transpose(PS[:, 1, i * P:(i + 1) * P], HW[:, i, :], ident[:, :])
                    last = pe.transpose(PS[0:E3, 1, S + i * P:S + (i + 1) * P], CM[:, i, 0:E3], ident[:, :])
                last.then_inc(filled[1], 1)
                if b < NB - 1:
                    prepare("adapter", b)
                pe.wait_ge(drained[1], fill("adapter", 1, b, 0))
                free("adapter", 6, b, 0)
                for i in range(2):
                    y = PS[:, 6, i * D:(i + 1) * D]
                    mm(y, HWT[:, i * P:(i + 1) * P], wu_3, start=True, stop=False)
                    last = mm(y, WT[:, i * P:(i + 1) * P], bu_3, start=False, stop=True)
                last.then_inc(filled[6], 1)


def kernel(**inputs):
    import ml_dtypes
    import numpy as np
    import concourse.bacc as bacc
    from concourse.bass_utils import run_bass_kernel_spmd

    f32 = np.float32
    g = {k: np.asarray(v) for k, v in inputs.items()}
    arrays = {}

    def chunked(w, c=P):
        return w.reshape(w.shape[0] // c, c, w.shape[1]).transpose(1, 0, 2)

    arrays["x"] = g["x"].reshape(NB * S, D)
    ctx = g["ctx_512"].reshape(NB * S, DC)
    swapped = np.concatenate([ctx[:, DC // 2:], ctx[:, :DC // 2]], axis=1)
    arrays["ctx"], arrays["ctxT"] = ctx, ctx.T
    arrays["ctx_swapped"], arrays["ctxT_swapped"] = swapped, swapped.T
    gates = np.concatenate([g["g_xattn"], g["g_ffn"], g["L0_xattn_gamma_raw"].reshape(1)])
    arrays["gates"] = np.broadcast_to(gates, (P, 9))
    arrays["ident"] = np.eye(P, dtype=f32)
    arrays["wqk0"] = np.stack([g["L0_xattn_Wq"].T, g["L0_xattn_Wk"].T], axis=1)

    w13, sw13 = g["L0_ffn_w13"], g["L0_ffn_sw13"]
    arrays["w_g0"] = chunked(np.concatenate([w13[:, :I0].reshape(-1, D), sw13[:2 * I0]]).T)
    arrays["w_u0"] = chunked(np.concatenate([w13[:, I0:].reshape(-1, D), sw13[2 * I0:]]).T)
    arrays["w_d0"] = np.concatenate([g["L0_ffn_w2"].transpose(0, 2, 1).reshape(-1, D), g["L0_ffn_sw2"].T])
    arrays["w_r0"] = chunked(g["L0_ffn_gate_w"].T)
    sel = np.zeros((3, PART, F0), f32)
    for f in range(F0):
        sel[:, min(f // I0, E0), f] = 1.0
    arrays["sel_e"] = sel.reshape(3 * PART, F0).astype(ml_dtypes.bfloat16)

    def groups(w):
        return w.reshape(4, 4, *w.shape[1:])

    arrays["wq1"] = groups(g["L1_xattn_Wq"].reshape(NH, P, D)).transpose(0, 2, 1, 3)
    arrays["wkq1T"] = groups(g["L1_xattn_w_kc_q"]).reshape(4, 4, P, 2, 96).transpose(0, 4, 3, 1, 2)
    arrays["wqr1T"] = groups(g["L1_xattn_W_qr"]).transpose(0, 3, 1, 2)
    arrays["wkr1T"] = groups(g["L1_xattn_W_kr"]).transpose(0, 3, 1, 2)
    arrays["wkv1"] = groups(g["L1_xattn_w_kc_kv"]).transpose(0, 2, 1, 3)
    arrays["wo1T"] = groups(g["L1_xattn_Wo"].T.reshape(NH, P, D)).transpose(0, 2, 1, 3)
    inv = (f32(1.0) / np.power(f32(10000.0), np.arange(0, DC, 2, dtype=f32) / f32(DC))).astype(f32)
    freq = np.arange(S, dtype=f32)[:, None] * inv[None, :]
    cos, sin = np.repeat(np.cos(freq), 2, axis=1), np.repeat(np.sin(freq), 2, axis=1)
    sin = np.concatenate([-sin[:, :DC // 2], sin[:, DC // 2:]], axis=1)
    rope = np.stack([cos, sin])
    arrays["ropeN"] = rope.reshape(2, 2, P, DC).transpose(2, 1, 0, 3)
    arrays["ropeT"] = rope.transpose(2, 0, 1)
    w12 = np.concatenate([chunked(g["L1_ffn_w1"].T), chunked(g["L1_ffn_w2"].T)], axis=1)
    arrays["w12"], arrays["w3T"] = w12, g["L1_ffn_w3"].T

    def slots(rows, cols=0):
        return np.zeros((rows, NH, 32), f32)

    q2 = np.zeros((P, 4, 4, 32), f32)
    k2, v2 = slots(DC + 1), slots(DC + 1)
    for h in range(NH):
        gr, j = h // 4, h % 4
        for d in range(16):
            q2[(h * 16 + d) % P, gr, j, d] = 1.0
            k2[16 * gr + d, h, d] = 1.0
            v2[16 * gr + d, h, d] = 1.0
    one_k, one_v = slots(1), slots(1)
    one_k[:, :, 16], one_v[:, :, 16:] = 1.0, 1.0
    k2[DC:], v2[DC:] = one_k, one_v
    arrays["sel_q2"] = q2.reshape(P, 4, P)
    arrays["sel_k2"], arrays["sel_v2"] = k2.reshape(DC + 1, 512), v2.reshape(DC + 1, 512)
    wkv = g["L3_xattn_Wkv_expand"]
    k3, v3, q3 = slots(DC + 1), slots(DC + 1), slots(D)
    k3[:DC, :, :16] = wkv[:D].T.reshape(DC, NH, 16)
    v3[:DC, :, :16] = wkv[D:].T.reshape(DC, NH, 16)
    k3[DC:], v3[DC:] = one_k, one_v
    q3[:, :, :16] = g["L3_xattn_Wq"].T.reshape(D, NH, 16)
    arrays["wk_3"], arrays["wv_3"] = k3.reshape(DC + 1, 512), v3.reshape(DC + 1, 512)
    arrays["wq_3"] = chunked(q3.reshape(D, 512))
    for name, w in (("wo_2", g["L2_xattn_Wc"]), ("wo_3", g["L3_xattn_Wout"])):
        o = np.zeros((NH, 32, D), f32)
        o[:, :16] = w.T.reshape(NH, 16, D)
        arrays[name] = chunked(o.reshape(512, D))
    arrays["bias_2"] = g["L2_xattn_bc"].reshape(1, D)
    arrays["wb_2"] = chunked(g["L2_ffn_W_base"].T)
    ra = np.concatenate([g["L2_ffn_W_router"], g["L2_ffn_A_w"].reshape(-1, D)]).T
    arrays["ra_2"] = chunked(ra)
    arrays["bt_2"] = g["L2_ffn_B_w"].transpose(0, 2, 1).reshape(E2 * R2, D)
    arrays["biasb_2"] = g["L2_ffn_b_base"].reshape(1, D)
    wd = g["L3_ffn_Wd"].transpose(1, 0, 2).reshape(D, E3 * R3)
    arrays["dr_3"] = chunked(np.concatenate([wd, g["L3_ffn_Wr"]], axis=1))
    arrays["bdr_3"] = np.concatenate([g["L3_ffn_bd"].reshape(-1), g["L3_ffn_br"]]).reshape(1, -1)
    arrays["wu_3"] = g["L3_ffn_Wu"].reshape(E3 * R3, D)
    arrays["bu_3"] = g["L3_ffn_bu"]
    den = np.zeros((P, P), f32)
    for j in range(4):
        den[32 * j + 16, 32 * j:32 * j + 32] = 1.0
    arrays["sel_den"] = den
    later = np.where(np.arange(P)[None, :] > np.arange(P)[:, None], f32(-1e38), f32(0.0))
    arrays["maskS"] = later.astype(ml_dtypes.bfloat16)
    arrays["maskT"] = later.T.astype(ml_dtypes.bfloat16)

    nc = bacc.Bacc("TRN2", target_bir_lowering=False, num_devices=1)
    arrays = {f"in_{k}": np.ascontiguousarray(v) for k, v in arrays.items()}
    aps = {k[3:]: nc.dram_tensor(k, v.shape, mybir.dt.from_np(v.dtype), kind="ExternalInput").ap()
           for k, v in arrays.items()}
    out = nc.dram_tensor("out", (NB * S, D), F32, kind="ExternalOutput").ap()
    build(nc, aps, out)
    got = run_bass_kernel_spmd(nc, [arrays], core_ids=[0]).results[0]["out"]
    return got.reshape(NB, S, D)
```

```python
from contextlib import ExitStack

import concourse.bass as bass
from concourse import mybir

F32 = mybir.dt.float32
BF16 = mybir.dt.bfloat16
ACT = mybir.ActivationFunctionType
ALU = mybir.AluOpType
AX = mybir.AxisListType.X

P = 128
NB = 4
S = 256
D = 256
TILES = NB * S // P
NH = 16
DC = 64
TOPK = int(S * 0.3)
E0, I0, K0 = 16, 176, 6
F0 = E0 * I0 + 2 * I0
CH0 = -(-F0 // P)
PAIRS0 = -(-CH0 // 2)
SLICE0 = 4 * 2 * P
PART = E0 + 1
H1 = 704
CH1 = -(-H1 // P)
E2, R2 = 8, 8
E3, R3 = 8, 16
LOW = -3.0e38
BONUS = 3.0 * (1.0 - 1.0 / 625.0)

KEY_HEADS = {"grouped": 4, "causal": NH}
ROWS = 6 * 16
ALL_ROWS = ROWS + 3

FOLD_AT = 3
ROUNDS_AT = {1: (0, 1), 2: (2, 3), 3: (4, 5), 4: (6,), 5: (7,), 6: (8,), 7: (9,)}
GRAPH_AT = 9
TURN_AT = 11

PHASES = ["moe", "latent", "ternary", "grouped", "lora", "causal", "adapter"]
ATTENTIONS = ("latent", "grouped", "causal")
FILLS = {
    "moe": {0: 7, 1: 6, 2: 7, 3: 6, 4: 7, 5: 6, 6: 1},
    "ternary": {0: 2, 1: 2, 2: 2, 6: 1, 7: 1},
    "lora": {0: 1, 1: 1, 6: 1, 7: 1},
    "adapter": {0: 1, 1: 1, 6: 1, 7: 1},
}


def front(phase, b):
    if phase == "latent":
        return [], [(i % 2, "q", b, i) for i in range(NH // 2)]
    projected = [(0, "q", b, 0), (1, "k", b, 0)] if phase == "causal" else []
    values = [(5 - t, "v", b, t) for t in range(2)]
    return values, projected


def stacks(phase, b, n):
    return [(5, "qs", b, n)] + ([(4, "ks", b, n)] if n < KEY_HEADS[phase] // 2 else [])


def attention_fills(phase):
    stacked = phase != "latent"

    def scores(b, n):
        return [(h % 2, "s", b, h) for h in (2 * n, 2 * n + 1)] if b < NB and 0 <= n < NH // 2 else []

    order = sum(front(phase, 0), [])
    for hp in range(NH // 2 + 1):
        if stacked:
            order += scores(0, hp - 1)
            if hp < NH // 2:
                order += stacks(phase, 0, hp)
        else:
            order += scores(0, hp)
    order += [(7, "turn", 0, 0), (7, "max", 0, 0)]
    if stacked:
        order += sum(front(phase, 1), [])
    for b in range(NB):
        ahead = b + 1 < NB
        if ahead and not stacked:
            order += front(phase, b + 1)[1]
        for hp in range(NH // 2 + 1):
            if hp < NH // 2:
                order += [(2 + h % 2, "st", b, h) for h in (2 * hp, 2 * hp + 1)] if stacked \
                    else [(2 + 2 * (hp % 2), "st", b, hp)]
            if stacked:
                order += scores(b + 1, hp - 1)
            if hp and (phase == "latent" or hp % 2 == 0):
                order.append((6, "o", b, hp - 1 if phase == "latent" else hp // 2 - 1))
            if not stacked:
                order += scores(b + 1, hp)
            elif ahead and hp < NH // 2:
                order += stacks(phase, b + 1, hp)
            if stacked and hp in (3, 5):
                order.append((7, "den", b, (hp - 3) // 2))
            if stacked and ahead and hp == 7:
                order.append((7, "turn", b + 1, 0))
        values, projected = front(phase, b + 2) if stacked and b + 2 < NB else ([], [])
        order += values
        if ahead:
            order.append((7, "max", b + 1, 0))
            if not stacked:
                order.append((7, "turn", b + 1, 0))
        if stacked:
            order += [(7, "den", b, 2)] + projected + [(7, "den", b, 3)]
        order.append((6 if stacked else 7, "y", b, 0))
    return order


def moe_fills():
    order = [("fold", 0, k) for k in range(4)] + [("graph", 0, 0), ("turn", -1, 0)]
    for b in range(NB):
        order += [("router", b, 0), ("combine", b, 0)]
        if b + 1 < NB:
            order += [("fold", b + 1, k) for k in range(4)] + [("graph", b + 1, 0)]
        else:
            order.append(("abs", 0, 0))
        order.append(("turn", b, 0))
    return [("moe",) + key for key in order]


def all_fills():
    banks = {k: ["start"] for k in range(8)}
    banks[7] += moe_fills()
    for phase in PHASES:
        if phase in ATTENTIONS:
            for bank, what, b, k in attention_fills(phase):
                banks[bank].append((phase, what, b, k))
        else:
            for bank, n in FILLS[phase].items():
                banks[bank] += [(phase, b, k) for b in range(NB) for k in range(n)]
    return banks


BANK_FILLS = all_fills()


def fills_before(phase, bank):
    for n, key in enumerate(BANK_FILLS[bank]):
        if key[0] in PHASES[PHASES.index(phase):]:
            return n
    return len(BANK_FILLS[bank])


def fill(phase, bank, b, k):
    return fills_before(phase, bank) + b * FILLS[phase][bank] + k + 1


def fill_at(phase, what, b, k=0):
    for bank, keys in BANK_FILLS.items():
        if (phase, what, b, k) in keys:
            return bank, keys.index((phase, what, b, k)) + 1
    raise KeyError((phase, what, b, k))


def build(nc, a, out):
    with ExitStack() as ctx:
        def sb(name, shape, dt=F32):
            return ctx.enter_context(nc.sbuf_tensor(name, shape, dt))

        def sem(name):
            return ctx.enter_context(nc.semaphore(name))

        PS = ctx.enter_context(nc.psum_tensor("PS", [P, 8, 512], F32))

        X = sb("X", [P, TILES, D])
        XN = sb("XN", [P, 2, D])
        XT = [sb(f"XT{p}", [P, 2, S]) for p in range(2)]
        BN = sb("BN", [P, 2, 6])
        MV = sb("MV", [P, 2, 2])
        RS = sb("RS", [P, 2])
        neg_half = sb("neg_half", [P, 2])
        eps = sb("eps", [P, 2])
        carrier = sb("carrier", [P, 4])
        ident = sb("ident", [P, P])
        identb = sb("identb", [P, P], BF16)
        ones = sb("ones", [P, P])
        gates = sb("gates", [P, 9])
        TG = sb("TG", [P, 9])
        CA = sb("CA", [P, 4])
        ctxT = sb("ctxT", [DC + 1, NB * S])
        W_g = sb("W_g", [P, 2, F0])
        W_u = sb("W_u", [P, 2, F0])
        W_d = sb("W_d", [P, CH0, D])
        W_r = sb("W_r", [P, 2, E0])
        sel_e = sb("sel_e", [3 * PART, F0], BF16)
        tanh_g = sb("tanh_g", [P, 2, 512])
        mlp_tmp = sb("mlp_tmp", [P, 4 * 512])
        gated, hidden = mlp_tmp[:, 0:512], mlp_tmp[:, 512:1024]
        H = mlp_tmp[:, 1024:2048].rearrange("p (a b s) -> p a b s", a=2, b=2)
        CT = [sb(f"CT{p}", [3 * PART, S], BF16) for p in range(2)]
        NMAX = sb("NMAX", [P, 2])
        EX = sb("EX", [P, 2, 16])
        Z = sb("Z", [P, 2])
        RZ = sb("RZ", [P, 2])
        SC = sb("SC", [P, 2, 18])
        T8 = sb("T8", [P, 2, 8])
        REP = sb("REP", [P, 2, 18])
        CM = sb("CM", [P, 2, PART])
        SU = sb("SU", [P, 2])
        C3 = sb("C3", [P, 2, P], BF16)
        NW = sb("NW", [P, 2, NH * DC])
        PM = sb("PM", [P, NH // 2, D])
        ropeN = sb("ropeN", [P, 2, 2, DC])
        ropeT = sb("ropeT", [DC, 2, S])
        KR = [sb(f"KR{p}", [DC + 1, S]) for p in range(2)]
        VV = [sb(f"VV{p}", [P, 2, 3 * DC]) for p in range(2)]
        def areas(flat, start):
            at = [start]

            def cut(parts, *shape):
                n = 1
                for x in shape:
                    n *= x
                v = flat[0:parts, at[0]:at[0] + n]
                at[0] += n
                assert at[0] <= flat.shape[1]
                if len(shape) == 2:
                    return v.rearrange("p (a b) -> p a b", a=shape[0])
                if len(shape) == 3:
                    return v.rearrange("p (a b c) -> p a b c", a=shape[0], b=shape[1])
                return v
            return cut

        arena = sb("arena", [P, 8992])
        FG = NH // 4
        fold_w = []
        for slot in range(2):
            cut = areas(arena, slot * 4352)
            fold_w.append([cut(P, 4, D), cut(96, 2, 4, P), cut(DC, 4, 192), cut(DC, 4, DC),
                           cut(P, 4, DC), cut(P, 4, D)])
        W_d_flat = W_d[:, :, :].rearrange("p a b -> p (a b)")
        cut = areas(arena, 0)
        qT1 = [cut(DC + 1, NH, S), areas(W_d_flat, 0)(DC + 1, NH, S)]
        probs = cut(P, 2, 2, 512)
        OT1 = cut(P, NH // 2, S)
        NM = cut(P, 2, NH)
        NMT = cut(NH, S)
        RD = cut(P, 2, S)
        cut = areas(arena, 0)
        VB = [cut(P, 2, 512) for _ in range(2)]
        cut = areas(arena, 4096 + 2048)
        OTN, OTR = cut(P, 4, S), cut(P, 4, S)
        fold_b = sb("fold_b", [96, 4, 2, DC])
        fold_c = sb("fold_c", [P, 4, DC])
        wqk0 = sb("wqk0", [DC, 2, DC])
        qk0 = areas(W_d_flat, 0)(DC, 2, NB * S)
        mlp_w = sb("mlp_w", [P, 4 * H1 + CH1 * D])
        cut = areas(mlp_w, 0)
        sim = [cut(P, 2, S) for _ in range(NB)]
        sg, work, AM, S2 = cut(P, 2, S), cut(P, 2, S), cut(P, 2, S), cut(P, 2, S)
        g8 = sb("g8", [P, 2, 8])
        def half(cut, parts, *shape):
            n = 1
            for x in shape:
                n *= x
            v = cut(parts, n // 2).bitcast(BF16)
            if len(shape) == 2:
                return v.rearrange("p (a b) -> p a b", a=shape[0])
            return v.rearrange("p (a b c) -> p a b c", a=shape[0], b=shape[1])

        cut = areas(W_d_flat, 0)
        QS = [half(cut, ALL_ROWS, NH, S) for _ in range(2)]
        QP, KP = half(cut, P, 3, 2, S), half(cut, P, 3, 2, S)
        rest = cut(P, 2, S)
        cut = areas(mlp_w, 0)
        KS = [half(cut, ALL_ROWS, NH, S) for _ in range(2)]
        NM3, RM = sb("NM3", [NH, 3, S], BF16), sb("RM", [NH, S])
        cut = areas(W_g[:, :, :].rearrange("p a b -> p (a b)"), 0)
        stack = half(cut, P, 6, 8, ROWS)
        wv_2 = cut(DC + 1, 512)
        wo_2 = cut(P, 4, D)
        wb_2 = cut(P, 2, D)
        ra_2 = cut(P, 2, E2 + E2 * R2)
        bt_2 = cut(E2 * R2, D)
        biasb_2 = cut(1, D)
        cut = areas(W_u[:, :, :].rearrange("p a b -> p (a b)"), 0)
        wq_3 = cut(P, 2, D)
        wk_3, wv_3 = cut(DC, D), cut(DC + 1, 512)
        wo_3 = cut(P, 4, D)
        dr_3 = cut(P, 2, E3 * R3 + E3)
        bdr_3 = cut(1, E3 * R3 + E3)
        wu_3 = cut(E3 * R3, D)
        bu_3 = cut(E3, D)
        ctxTs = cut(DC, NB * S)
        r3, r4 = cut(DC, S), cut(DC, S)
        sel_den = sb("sel_den", [P, P])
        maskS = sb("maskS", [P, P], BF16)
        maskT = sb("maskT", [P, P], BF16)
        cut = areas(mlp_w, 0)
        w12, w3 = cut(P, 4, H1), cut(P, CH1, D)
        absum, mean_w = sb("absum", [P, 4]), sb("mean_w", [P, 4])
        thr = sb("thr", [P, 2, 3])
        less = mlp_tmp[:, 0:2 * H1]
        HD = areas(arena, 0)(P, CH1, S)
        HW = sb("HW", [P, 2, P])
        HWT = sb("HWT", [P, S])
        WT = sb("WT", [E3, S])
        LG = sb("LG", [P, 2, 14])
        ctxN = sb("ctxN", [P, TILES, DC])
        ctxNs = sb("ctxNs", [P, TILES, DC])
        r1, r2 = sb("r1", [P, 2 * DC]), sb("r2", [P, 2 * DC])

        filled = [sem(f"bank_filled{k}") for k in range(8)]
        drained = [sem(f"bank_drained{k}") for k in range(8)]
        consts_set = sem("consts_set")
        ident_ready = sem("ident_ready")
        first_loaded = sem("first_loaded")
        fold_loaded = [sem(f"fold_loaded{n}") for n in range(2)]
        down_loaded = sem("down_loaded")
        router_loaded = sem("router_loaded")
        expert_loaded = [sem(f"expert_loaded{k}") for k in range(3)]
        rope_loaded = sem("rope_loaded")
        mlp_loaded = sem("mlp_loaded")
        late_loaded = sem("late_loaded")
        stored = sem("stored")
        v_step = sem("v_step")
        g_step = sem("g_step")
        gates_ready = sem("gates_ready")
        qk_filled, qk_copied = sem("qk_filled"), sem("qk_copied")
        sim_filled, sim_scaled, sg_ready = sem("sim_filled"), sem("sim_scaled"), sem("sg_ready")
        masked = sem("masked")
        graph_added = sem("graph_added")
        mv_ready, rstd_ready, xn_ready = sem("mv_ready"), sem("rstd_ready"), sem("xn_ready")
        nmax_ready, comb_ready = sem("nmax_ready"), sem("comb_ready")
        tanh_ready, h_used = sem("tanh_ready"), sem("h_used")
        kv_ready = sem("kv_ready")
        max_placed, max_split = sem("max_placed"), sem("max_split")
        parts_ready, ones_set = sem("parts_ready"), sem("ones_set")
        abs_ready, thr_ready, ternary_ready = sem("abs_ready"), sem("thr_ready"), sem("ternary_ready")
        tanh1_ready = sem("tanh1_ready")
        probs_used = sem("probs_used")
        norm_ready, divided = sem("norm_ready"), sem("divided")
        exp_ready = sem("exp_ready")
        block = ctx.enter_context(nc.Block())

        def pairs(eng, body):
            with eng.Fori(0, NB // 2) as j:
                for p in range(2):
                    body(j * 2 + p, p, (j * 2 + 1) if p == 0 else (j * -2 + 2))

        def pre_no(phase, b):
            return PHASES.index(phase) * NB + b + 1

        N_FIRST = 5

        @block.sync
        def _(sp):
            xv = a["x"].rearrange("(t p) d -> p t d", p=P)
            sp.dma_start(ctxT[0:DC, :], a["ctxT"]).then_inc(first_loaded, 16)
            sp.dma_start(wqk0[:, :, :], a["wqk0"]).then_inc(first_loaded, 16)
            sp.dma_start(ident[:, :], a["ident"]).then_inc(first_loaded, 16)
            sp.dma_start(gates[:, :], a["gates"]).then_inc(first_loaded, 16)
            sp.dma_start(X[:, :, :], xv).then_inc(first_loaded, 16)

            def fold_group(n):
                for dst, name in zip(fold_w[n % 2], ("wq1", "wkq1T", "wqr1T", "wkr1T", "wkv1", "wo1T")):
                    sp.dma_start(dst, a[name][n]).then_inc(fold_loaded[n % 2], 16)

            fold_group(0)
            sp.dma_start(W_r[:, :, :], a["w_r0"]).then_inc(router_loaded, 16)
            sp.dma_start(sel_e[:, :], a["sel_e"]).then_inc(router_loaded, 16)
            for k in range(3):
                cols = slice(k * SLICE0, (k + 1) * SLICE0 if k < 2 else F0)
                sp.dma_start(W_g[:, :, cols], a["w_g0"][:, :, cols]).then_inc(expert_loaded[k], 16)
                sp.dma_start(W_u[:, :, cols], a["w_u0"][:, :, cols]).then_inc(expert_loaded[k], 16)
                if k == 0:
                    sp.wait_ge(sim_filled, 1)
                    full = F0 // P
                    sp.dma_start(W_d[:, 0:full, :], a["w_d0"][0:full * P, :].rearrange("(c p) d -> p c d", p=P)) \
                        .then_inc(down_loaded, 16)
                    sp.dma_start(W_d[0:F0 - full * P, full, :], a["w_d0"][full * P:F0, :]) \
                        .then_inc(down_loaded, 16)
            fold_group(1)
            sp.dma_start(ctxN[:, :, :], a["ctx"].rearrange("(t p) d -> p t d", p=P)).then_inc(rope_loaded, 16)
            sp.dma_start(ctxNs[:, :, :], a["ctx_swapped"].rearrange("(t p) d -> p t d", p=P)) \
                .then_inc(rope_loaded, 16)
            sp.dma_start(ropeN[:, :, :, :], a["ropeN"]).then_inc(rope_loaded, 16)
            sp.dma_start(ropeT[:, :, :], a["ropeT"]).then_inc(rope_loaded, 16)
            for n in range(2, FG):
                sp.wait_ge(filled[7], fill_at("moe", "fold", n - 2, 3)[1])
                fold_group(n)
            sp.wait_ge(graph_added, NB)
            sp.dma_start(w12[:, :, :], a["w12"]).then_inc(mlp_loaded, 16)
            full = H1 // P
            sp.dma_start(w3[:, 0:full, :], a["w3T"][0:full * P, :].rearrange("(c p) d -> p c d", p=P)) \
                .then_inc(mlp_loaded, 16)
            sp.dma_start(w3[0:H1 - full * P, full, :], a["w3T"][full * P:H1, :]).then_inc(mlp_loaded, 16)
            sp.wait_ge(filled[6], fill("moe", 6, NB - 1, 0))
            sp.dma_start(ctxTs, a["ctxT_swapped"]).then_inc(rope_loaded, 16)
            for dst, name in ((stack, "stack"), (wv_2, "sel_v2"), (wo_2, "wo_2"),
                              (wb_2, "wb_2"), (ra_2, "ra_2"), (bt_2, "bt_2"),
                              (biasb_2, "biasb_2"), (wq_3, "wq_3"), (wk_3, "wk_3"), (wv_3, "wv_3"),
                              (wo_3, "wo_3"), (dr_3, "dr_3"), (bdr_3, "bdr_3"), (wu_3, "wu_3"),
                              (bu_3, "bu_3"), (sel_den[:, :], "sel_den"), (maskS[:, :], "maskS"),
                              (maskT[:, :], "maskT")):
                sp.dma_start(dst, a[name]).then_inc(late_loaded, 16)

            def place_max(phase):
                for b in range(NB):
                    if phase == "latent":
                        bank, value = fill_at(phase, "max", b)
                        sp.wait_ge(drained[bank], value)
                        sp.dma_start(qT1[b % 2][DC:DC + 1, :, :], NMT).then_inc(max_placed, 16)
                        continue
                    sp.wait_ge(max_split, b + 1 + (NB if phase == "causal" else 0))
                    for part in range(3):
                        row = ROWS + part
                        sp.dma_start(QS[b % 2][row:row + 1, :, :], NM3[:, part, :]).then_inc(max_placed, 16)

            place_max("latent")
            sp.wait_ge(filled[6], fill("ternary", 6, NB - 1, 0))
            for p in range(2):
                sp.dma_start(KS[p][ROWS:ALL_ROWS, :, :], a["key_ones"]).then_inc(ones_set, 16)
            place_max("grouped")
            place_max("causal")
            ov = out.rearrange("(t p) d -> p t d", p=P)
            for b in range(NB):
                sp.wait_ge(drained[6], fill("adapter", 6, b, 0))
                sp.dma_start(ov[:, 2 * b:2 * b + 2, :], X[:, 2 * b:2 * b + 2, :]).then_inc(stored, 16)
            sp.wait_ge(stored, 16 * NB)

        LATE = 16 * 18

        @block.gpsimd
        def _(pool):
            def rstd(n, first=False):
                pool.wait_ge(mv_ready, n + 1)
                if not first:
                    pool.wait_ge(xn_ready, n)
                pool.tensor_tensor(RS[:, :], MV[:, :, 1], eps[:, :], ALU.add).then_inc(g_step, 1)
                pool.wait_ge(g_step, n + 1)
                pool.tensor_tensor(RS[:, :], RS[:, :], neg_half[:, :], ALU.pow).then_inc(rstd_ready, 1)

            pool.wait_ge(consts_set, 1)

            rstd(0, first=True)
            for n in range(1, 2 * NB + 1):
                rstd(n)
            BASE = NB

            def prepare(phase):
                def body(b, p, nb):
                    rstd(pre_no(phase, b) + BASE)
                return body

            pool.wait_ge(rope_loaded, 16 * 5)
            pool.wait_ge(first_loaded, 16 * N_FIRST)
            pool.wait_ge(consts_set, 1)

            def rotate(b):
                p = b % 2
                if b >= 2:
                    bank, value = fill_at("latent", "y", b - 2)
                    pool.wait_ge(filled[bank], value)
                s = slice(b * S, (b + 1) * S)
                rn = [ropeN[:, :, k, :] for k in range(2)]
                v1 = r1[:, :].rearrange("p (a b) -> p a b", a=2)
                v2 = r2[:, :].rearrange("p (a b) -> p a b", a=2)
                n = b * 4
                pool.tensor_tensor(v1, ctxN[:, 2 * b:2 * b + 2, :], rn[0], ALU.mult)
                pool.tensor_tensor(v2, ctxNs[:, 2 * b:2 * b + 2, :], rn[1], ALU.mult).then_inc(kv_ready, 1)
                pool.wait_ge(kv_ready, n + 1)
                pool.tensor_tensor(r3[:, :], ctxT[0:DC, s], ropeT[:, 0, :], ALU.mult)
                pool.tensor_tensor(r4[:, :], ctxTs[:, s], ropeT[:, 1, :], ALU.mult).then_inc(kv_ready, 1)
                pool.wait_ge(kv_ready, n + 2)
                pool.tensor_tensor(VV[p][:, :, DC:2 * DC], v1, v2, ALU.add).then_inc(kv_ready, 1)
                pool.wait_ge(kv_ready, n + 3)
                pool.tensor_tensor(KR[p][0:DC, :], r3[:, :], r4[:, :], ALU.add).then_inc(kv_ready, 1)
                pool.wait_ge(kv_ready, n + 4)

            rotate(0)
            rstd(pre_no("latent", 0) + BASE)
            rotate(1)
            for b in range(NB):
                if b < NB - 1:
                    rstd(pre_no("latent", b + 1) + BASE)
                if b < NB - 2:
                    rotate(b + 2)

            pool.wait_ge(thr_ready, 1)
            for k, (w, c) in enumerate(((w12[:, 0:2, :], 0), (w12[:, 2:4, :], 1), (w3[:, 0:5, :], 2),
                                        (w3[0:H1 - 5 * P, 5, :], 2))):
                parts = P if k < 3 else H1 - 5 * P
                wf = w.rearrange("p a b -> p (a b)") if k < 3 else w
                n = 2 * H1 if k < 2 else (5 * D if k == 2 else D)
                pool.tensor_scalar(less[0:parts, 0:n], wf, thr[0:parts, 1, c:c + 1], None, ALU.is_lt) \
                    .then_inc(ternary_ready, 1)
                pool.tensor_scalar(wf, wf, thr[0:parts, 0, c:c + 1], None, ALU.is_gt) \
                    .then_inc(ternary_ready, 1)
                pool.wait_ge(ternary_ready, 3 * k + 2)
                pool.tensor_tensor(wf, wf, less[0:parts, 0:n], ALU.subtract).then_inc(ternary_ready, 1)
                pool.wait_ge(ternary_ready, 3 * k + 3)
            pairs(pool, prepare("ternary"))

            for b in range(NB):
                rstd(pre_no("grouped", b) + BASE)
            pairs(pool, prepare("lora"))
            for b in range(NB):
                rstd(pre_no("causal", b) + BASE)
            for b in range(NB - 1):
                rstd(pre_no("adapter", b) + BASE)

        @block.scalar
        def _(act):
            act.wait_ge(first_loaded, 16 * N_FIRST)
            act.activation(TG[:, 0:8], gates[:, 0:8], ACT.Tanh)
            act.activation(TG[:, 8:9], gates[:, 8:9], ACT.Tanh, scale=0.5).then_inc(gates_ready, 1)
            act.activation(identb[:, :], ident[:, :], ACT.Copy).then_inc(ident_ready, 1)
            for k in range(2):
                act.wait_ge(qk_filled, k + 1)
                act.activation(qk0[:, k, :], PS[0:DC, 4 + 2 * k:6 + 2 * k, :].rearrange("p a b -> p (a b)"),
                               ACT.Copy).then_inc(qk_copied, 1)

            act.wait_ge(sim_filled, 1)
            for b in range(NB):
                act.activation(sim[b], PS[:, b, :].rearrange("p (a b) -> p a b", a=2), ACT.Copy, scale=0.0625) \
                    .then_inc(sim_scaled, 1)

            def edge_gates(b):
                act.wait_ge(sim_scaled, b + 1)
                if b:
                    act.wait_ge(masked, b)
                act.activation(sg, sim[b], ACT.Tanh, scale=0.5).then_inc(sg_ready, 1)

            def evacuate(phase, what, b, k, *copies):
                bank, value = fill_at(phase, what, b, k)
                act.wait_ge(filled[bank], value)
                for dst, src in copies:
                    last = act.activation(dst, src, ACT.Copy)
                last.then_inc(drained[bank], 1)

            def fold_out(n, k):
                dst, src = [(fold_b[:, :, :, :], PS[0:96, 7, :].rearrange("p (h c d) -> p h c d", h=4, c=2)),
                            (fold_c[:, :, :], PS[:, 7, 0:4 * DC].rearrange("p (h d) -> p h d", h=4)),
                            (NW[:, :, 4 * n * DC:(4 * n + 4) * DC], PS[:, 7, :].rearrange("p (c n) -> p c n", c=2)),
                            (PM[:, 2 * n:2 * n + 2, :], PS[:, 7, :].rearrange("p (h d) -> p h d", h=2))][k]
                evacuate("moe", "fold", n, k, (dst, src))

            edge_gates(0)
            for k in range(4):
                fold_out(0, k)

            def xt_out(value, p):
                act.wait_ge(filled[7], value)
                act.activation(XT[p][:, :, :], PS[:, 7, :].rearrange("p (c s) -> p c s", c=2), ACT.Copy) \
                    .then_inc(drained[7], 1)

            xt_out(fill_at("moe", "turn", -1)[1], 0)

            for b in range(NB):
                p = b % 2
                act.wait_ge(nmax_ready, b + 1)
                for i in range(2):
                    last = act.activation(EX[:, i, :], PS[:, 7, i * E0:(i + 1) * E0], ACT.Exp,
                                          bias=NMAX[:, i:i + 1], accum_out=Z[:, i:i + 1])
                last.then_inc(drained[7], 1)
                for c in range(PAIRS0):
                    g = c % 2
                    act.wait_ge(filled[g], fill("moe", g, b, c // 2))
                    if c >= 2:
                        act.wait_ge(drained[g], fill("moe", g, b, c // 2 - 1))
                    else:
                        act.wait_ge(drained[g], fill("moe", g, b, -1))
                    if c == PAIRS0 - 1:
                        act.activation(tanh_g[0:F0 % P, g, 0:S], PS[0:F0 % P, g, 0:S], ACT.Tanh, scale=0.5) \
                            .then_inc(tanh_ready, 1)
                    else:
                        act.activation(tanh_g[:, g, :], PS[:, g, :], ACT.Tanh, scale=0.5) \
                            .then_inc(tanh_ready, 1)
                    if c == 1:
                        evacuate("moe", "combine", b, 0, (CT[p][:, :], PS[0:3 * PART, 7, 0:P].bitcast(BF16)))
                    if b + 1 < NB:
                        if c == 2:
                            edge_gates(b + 1)
                        if FOLD_AT <= c < FOLD_AT + 4:
                            fold_out(b + 1, c - FOLD_AT)
                    if c == TURN_AT:
                        xt_out(fill_at("moe", "turn", b)[1], 1 - p)

            def latent_queries(b):
                for i in range(NH // 2):
                    evacuate("latent", "q", b, i, (qT1[b % 2][0:DC, 2 * i, :], PS[0:DC, i % 2, 0:S]),
                             (qT1[b % 2][0:DC, 2 * i + 1, :], PS[DC:P, i % 2, 0:S]))

            def turned_and_max(phase, b, turn_first):
                if turn_first:
                    xt_out(fill_at(phase, "turn", b)[1], (b + 1) % 2)
                evacuate(phase, "max", b, 0, (NMT, PS[0:NH, 7, 0:S]))
                if not turn_first:
                    xt_out(fill_at(phase, "turn", b)[1], (b + 1) % 2)

            def outputs_out(b, hp):
                if b and hp == 0:
                    bank, value = fill_at("latent", "y", b - 1)
                    act.wait_ge(filled[bank], value)
                if b * NH // 2 + hp >= 2:
                    act.wait_ge(divided, b * NH // 2 + hp - 1)
                evacuate("latent", "o", b, hp, (OT1[0:DC, hp, :], PS[0:DC, 6, 0:S]),
                         (OT1[DC:P, hp, :], PS[DC:P, 6, S:2 * S]),
                         (RD[0:DC, hp % 2, :], PS[DC:P, 6, 0:S]), (RD[DC:P, hp % 2, :], PS[0:DC, 6, S:2 * S]))

            latent_queries(0)
            turned_and_max("latent", 0, True)
            for b in range(NB):
                if b < NB - 1:
                    latent_queries(b + 1)
                for hp in range(NH // 2):
                    s = hp % 2
                    bank, value = fill_at("latent", "st", b, hp)
                    act.wait_ge(filled[bank], value)
                    if hp >= 2:
                        act.wait_ge(filled[6], fill_at("latent", "o", b, hp - 2)[1])
                    act.activation(probs[:, s, :, :], PS[:, bank:bank + 2, :], ACT.Exp).then_inc(drained[bank], 1)
                    if hp:
                        outputs_out(b, hp - 1)
                outputs_out(b, NH // 2 - 1)
                if b < NB - 1:
                    turned_and_max("latent", b + 1, False)

            def ternary(b, p, nb):
                for k in range(CH1):
                    m = min(P, H1 - k * P)
                    act.wait_ge(filled[k % 3], fill("ternary", k % 3, b, k // 3))
                    if k >= 2:
                        act.wait_ge(drained[(k - 2) % 3], fill("ternary", (k - 2) % 3, b, (k - 2) // 3))
                    else:
                        act.wait_ge(drained[(k + 1) % 3], fill("ternary", (k + 1) % 3, b, -1))
                    act.activation(tanh_g[0:m, k % 2, 0:S], PS[0:m, k % 3, 0:S], ACT.Tanh, scale=0.5) \
                        .then_inc(tanh1_ready, 1)
                xt_out(fill("ternary", 7, b, 0), 1 - p)
            pairs(act, ternary)

            def values_out(phase, b):
                for t in range(2):
                    evacuate(phase, "v", b, t, (VB[b % 2][:, t, :], PS[:, 5 - t, :]))

            def stacks_out(phase, b, n):
                for bank, what, _, _ in stacks(phase, b, n):
                    to = QS if what == "qs" else KS
                    evacuate(phase, what, b, n, (to[b % 2][0:ROWS, 2 * n:2 * n + 2, :], PS[0:ROWS, bank, :]
                                                 .rearrange("p (a s) -> p a s", a=2)))

            def attention(phase):
                values_out(phase, 0)
                for n in range(NH // 2):
                    stacks_out(phase, 0, n)
                xt_out(fill_at(phase, "turn", 0)[1], 1)
                values_out(phase, 1)
                n = 512 if phase == "grouped" else 384
                for b in range(NB):
                    ahead = b < NB - 1
                    half = 4 * b if phase == "grouped" else 4 * b + 4 * NB
                    for hp in range(NH // 2):
                        s, g = hp % 2, hp // 2
                        if g and s == 0:
                            act.wait_ge(probs_used, half + g)
                        elif g:
                            act.wait_ge(filled[6], fill_at(phase, "o", b, g - 1)[1])
                        for e in range(2):
                            bank, value = fill_at(phase, "st", b, 2 * hp + e)
                            act.wait_ge(filled[bank], value)
                            act.activation(probs[:, s, e, 0:n], PS[:, bank, 0:n], ACT.Exp, scale=0.25) \
                                .then_inc(drained[bank], 1)
                        if ahead:
                            stacks_out(phase, b + 1, hp)
                        if s == 0 and g:
                            evacuate(phase, "o", b, g - 1, (OTR[:, g - 1, :], PS[:, 6, 0:S]))
                        if ahead and hp == 7:
                            xt_out(fill_at(phase, "turn", b + 1)[1], b % 2)
                    evacuate(phase, "o", b, 3, (OTR[:, 3, :], PS[:, 6, 0:S]))
                    if b + 2 < NB:
                        values_out(phase, b + 2)

            attention("grouped")

            def lora(b, p, nb):
                act.wait_ge(nmax_ready, NB + b + 1)
                for i in range(2):
                    last = act.activation(EX[:, i, 0:E2], LG[:, i, 0:E2], ACT.Exp, bias=NMAX[:, i:i + 1])
                last.then_inc(exp_ready, 1)
                act.wait_ge(filled[1], fill("lora", 1, b, 0))
                act.activation(HWT[0:E2 * R2, :], PS[0:E2 * R2, 1, 0:S], ACT.Copy).then_inc(drained[1], 1)
                xt_out(fill("lora", 7, b, 0), 1 - p)
            pairs(act, lora)
            attention("causal")

            def adapter(b, p, nb):
                act.wait_ge(nmax_ready, 2 * NB + b + 1)
                for i in range(2):
                    last = act.activation(EX[:, i, 0:E3], LG[:, i, 0:E3], ACT.Exp, bias=NMAX[:, i:i + 1],
                                          accum_out=Z[:, i:i + 1])
                last.then_inc(exp_ready, 1)
                act.wait_ge(filled[1], fill("adapter", 1, b, 0))
                act.activation(HWT[:, :], PS[:, 1, 0:S], ACT.Copy)
                act.activation(WT[:, :], PS[0:E3, 1, S:2 * S], ACT.Copy).then_inc(drained[1], 1)
                if b < NB - 1:
                    xt_out(fill("adapter", 7, b, 0), 1 - p)
            for b in range(NB):
                adapter(b, b % 2, None)

        @block.vector
        def _(dve):
            done = [0, 0]

            parts = [0]

            def part():
                k = parts[0] % 4
                parts[0] += 1
                dve.memset(carrier[:, k:k + 1], 0.0)

            def start(at_):
                done[0], done[1] = at_, 0

            def link(ins):
                ins.then_inc(v_step, 1)
                done[1] += 1
                dve.wait_ge(v_step, done[0] + done[1])

            def loop(name, body, count):
                base = v_total[0]
                def one(b, p, nb):
                    start(base + b * count)
                    body(b, p, nb)
                    assert done[1] == count, (name, done[1])
                pairs(dve, one)
                v_total[0] = base + NB * count
                start(v_total[0])

            v_total = [0]

            def stats(b):
                link(dve.bn_stats(BN[:, 0, :], X[:, b * 2, :]))
                link(dve.bn_stats(BN[:, 1, :], X[:, b * 2 + 1, :]))
                part()
                dve.bn_aggr(MV[:, 0, :], BN[:, 0, :])
                dve.bn_aggr(MV[:, 1, :], BN[:, 1, :]).then_inc(mv_ready, 1)

            def normalise(n, b, used):
                dve.wait_ge(rstd_ready, n + 1)
                if used is not None:
                    dve.wait_ge(filled[7], used)
                for i in range(2):
                    last = dve.tensor_scalar(XN[:, i, :], X[:, b * 2 + i, :], MV[:, i, 0:1], RS[:, i:i + 1],
                                             ALU.subtract, ALU.mult)
                last.then_inc(xn_ready, 1)

            def prepare_stats(phase, b, nb):
                stats(nb)

            def prepare_norm(phase, b, nb):
                normalise(pre_no(phase, b) + NB, nb, fill(phase, 7, b, -1))

            def add_residual(phase, b, k, gate):
                dve.wait_ge(filled[6], fill(phase, 6, b, k))
                xb = X[:, bass.ds(b * 2, 2), :]
                dve.scalar_tensor_tensor(xb, PS[:, 6, :].rearrange("p (a d) -> p a d", a=2), gate, xb,
                                         ALU.mult, ALU.add).then_inc(drained[6], 1)
                dve.wait_ge(drained[6], fill(phase, 6, b, k))

            for dst, value in ((neg_half[:, :], -0.5), (eps[:, :], 1e-5), (ones[:, :], 1.0),
                               (ctxT[DC:DC + 1, :], 1.0), (KR[0][DC:DC + 1, :], 1.0),
                               (KR[1][DC:DC + 1, :], 1.0), (VV[0][:, :, :], 1.0), (VV[1][:, :, :], 1.0),
                               (SC[:, :, :], LOW), (LG[:, :, :], LOW), (CM[:, :, :], 0.5),
                               (HW[:, :, :], 0.0), (C3[:, :, :], 0.0)):
                last = dve.memset(dst, value)
            last.then_inc(consts_set, 1)

            dve.wait_ge(gates_ready, 1)
            start(0)
            link(dve.tensor_scalar(CA[:, 2:3], TG[:, 8:9], -0.5, 0.5, ALU.mult, ALU.add))
            link(dve.tensor_tensor(CA[:, 0:1], CA[:, 2:3], TG[:, 0:1], ALU.mult))
            link(dve.tensor_scalar(CA[:, 3:4], TG[:, 8:9], 0.125, 0.125, ALU.mult, ALU.add))
            link(dve.tensor_tensor(CA[:, 1:2], CA[:, 3:4], TG[:, 0:1], ALU.mult))
            link(dve.tensor_scalar(CA[:, 2:3], TG[:, 5:6], 0.5, None, ALU.mult))
            v_total[0] = 5

            rounds = (TOPK - 1) // 8

            def graph_round(b, r):
                if r == 0:
                    dve.wait_ge(sim_scaled, b + 1)
                cur = sim[b] if r == 0 else work
                for i in range(2):
                    last = dve.max(g8[:, i, :], cur[:, i, :])
                link(last)
                if r < rounds:
                    for i in range(2):
                        last = dve.match_replace(work[:, i, :], g8[:, i, :], cur[:, i, :], LOW)
                    link(last)

            def graph_mask(b):
                dve.wait_ge(sg_ready, b + 1)
                link(dve.tensor_scalar(sg, sg, 1.0, None, ALU.add))
                kth = (TOPK - 1) % 8
                for i in range(2):
                    last = dve.scalar_tensor_tensor(AM[:, i, :], sim[b][:, i, :], g8[:, i, kth:kth + 1],
                                                    sg[:, i, :], ALU.is_ge, ALU.mult)
                last.then_inc(masked, 1)
                dve.wait_ge(masked, b + 1)

            def graph_norm(b):
                normalise(2 * b, b, fill_at("moe", "turn", b - 2)[1] if b else None)
                dve.wait_ge(xn_ready, 2 * b + 1)
                xb = X[:, 2 * b:2 * b + 2, :]
                link(dve.scalar_tensor_tensor(xb, XN[:, :, :], CA[:, 0:1], xb, ALU.mult, ALU.add))

            def graph_add(b):
                bank, value = fill_at("moe", "graph", b)
                dve.wait_ge(filled[bank], value)
                dve.tensor_tensor(S2, AM, PS[:, bank, :].rearrange("p (a s) -> p a s", a=2), ALU.add) \
                    .then_inc(drained[bank], 1)
                dve.wait_ge(drained[bank], value)
                xb = X[:, 2 * b:2 * b + 2, :]
                dve.scalar_tensor_tensor(xb, S2, CA[:, 1:2], xb, ALU.mult, ALU.add).then_inc(graph_added, 1)
                dve.wait_ge(graph_added, b + 1)

            start(v_total[0])
            stats(0)
            for r in range(rounds + 1):
                graph_round(0, r)
            graph_mask(0)
            graph_norm(0)
            graph_add(0)
            stats(0)
            normalise(1, 0, None)
            dve.wait_ge(consts_set, 1)

            def weight_sums():
                dve.wait_ge(mlp_loaded, 16 * 3)
                link(dve.memset(absum[:, :], 0.0))
                for k, w in enumerate((w12[:, 0:2, :], w12[:, 2:4, :], w3[:, 0:5, :])):
                    dve.tensor_reduce(absum[:, k:k + 1], w.rearrange("p a b -> p (a b)"), AX, ALU.add,
                                      apply_absolute_value=True)
                dve.tensor_reduce(absum[0:H1 - 5 * P, 3:4], w3[0:H1 - 5 * P, 5, :], AX, ALU.add,
                                  apply_absolute_value=True).then_inc(abs_ready, 1)

            def thresholds():
                bank, value = fill_at("moe", "abs", 0)
                dve.wait_ge(filled[bank], value)
                dve.tensor_copy(mean_w[:, :], PS[:, bank, 0:4]).then_inc(drained[bank], 1)
                dve.wait_ge(drained[bank], value)
                link(dve.tensor_tensor(mean_w[:, 2:3], mean_w[:, 2:3], mean_w[:, 3:4], ALU.add))
                link(dve.tensor_scalar(mean_w[:, 0:3], mean_w[:, 0:3], 1.0 / (H1 * D), 1e-8, ALU.mult, ALU.add))
                dve.tensor_scalar(thr[:, 0, :], mean_w[:, 0:3], 0.5, None, ALU.mult)
                dve.tensor_scalar(thr[:, 1, :], mean_w[:, 0:3], -0.5, None, ALU.mult).then_inc(thr_ready, 1)

            for b in range(NB):
                bank, value = fill_at("moe", "router", b)
                dve.wait_ge(filled[bank], value)
                dve.tensor_reduce(NMAX[:, :], PS[:, 7, 0:2 * E0].rearrange("p (a e) -> p a e", a=2), AX, ALU.max,
                                  negate=True).then_inc(nmax_ready, 1)
                dve.wait_ge(drained[bank], value)
                link(dve.reciprocal(RZ[:, :], Z[:, :]))
                for i in range(2):
                    last = dve.tensor_scalar(SC[:, i, 0:E0], EX[:, i, :], RZ[:, i:i + 1], None, ALU.mult)
                link(last)
                for i in range(2):
                    last = dve.max(T8[:, i, :], SC[:, i, 0:E0])
                link(last)
                link(dve.memset(T8[:, :, K0:8], LOW))
                for i in range(2):
                    last = dve.match_replace(REP[:, i, :], T8[:, i, :], SC[:, i, :], 0.0)
                link(last)
                link(dve.tensor_tensor(CM[:, :, 0:E0], SC[:, :, 0:E0], REP[:, :, 0:E0], ALU.subtract))
                link(dve.tensor_reduce(SU[:, :], CM[:, :, 0:E0], AX, ALU.add))
                link(dve.tensor_scalar(SU[:, :], SU[:, :], 1e-20, None, ALU.add))
                link(dve.reciprocal(SU[:, :], SU[:, :]))
                for i in range(2):
                    last = dve.tensor_scalar(CM[:, i, 0:E0], CM[:, i, 0:E0], SU[:, i:i + 1], 0.5,
                                             ALU.mult, ALU.mult)
                link(last)
                link(dve.tensor_copy(C3[:, :, 0:PART], CM[:, :, :]))
                link(dve.tensor_tensor(REP[:, :, 0:PART], CM[:, :, :], C3[:, :, 0:PART], ALU.subtract))
                link(dve.tensor_copy(C3[:, :, PART:2 * PART], REP[:, :, 0:PART]))
                dve.tensor_tensor(C3[:, :, 2 * PART:3 * PART], REP[:, :, 0:PART], C3[:, :, PART:2 * PART],
                                  ALU.subtract).then_inc(comb_ready, 1)
                for c in range(PAIRS0):
                    g, m, n = c % 2, P, 512
                    if c == PAIRS0 - 1:
                        m, n = F0 % P, S
                    dve.wait_ge(tanh_ready, b * PAIRS0 + c + 1)
                    dve.scalar_tensor_tensor(gated[0:m, 0:n], tanh_g[0:m, g, 0:n], 1.0, PS[0:m, g, 0:n],
                                             ALU.add, ALU.mult).then_inc(drained[g], 1)
                    dve.wait_ge(drained[g], fill("moe", g, b, c // 2))
                    dve.wait_ge(filled[2 + g], fill("moe", 2 + g, b, c // 2))
                    dve.tensor_tensor(hidden[0:m, 0:n], gated[0:m, 0:n], PS[0:m, 2 + g, 0:n], ALU.mult) \
                        .then_inc(drained[2 + g], 1)
                    dve.wait_ge(drained[2 + g], fill("moe", 2 + g, b, c // 2))
                    dve.wait_ge(filled[4 + g], fill("moe", 4 + g, b, c // 2))
                    if c >= 2:
                        dve.wait_ge(h_used, b * (PAIRS0 - 1) + c - 1)
                    dve.tensor_tensor(H[0:m, g, :, :].rearrange("p a s -> p (a s)")[:, 0:n], hidden[0:m, 0:n],
                                      PS[0:m, 4 + g, 0:n], ALU.mult).then_inc(drained[4 + g], 1)
                    if b + 1 < NB:
                        if c == 0:
                            stats(b + 1)
                        for r in ROUNDS_AT.get(c, ()):
                            graph_round(b + 1, r)
                        if c == 4:
                            graph_norm(b + 1)
                        if c == 7:
                            graph_mask(b + 1)
                        if c == GRAPH_AT - 1:
                            graph_add(b + 1)
                    else:
                        if c == 2:
                            weight_sums()
                        if c == GRAPH_AT - 1:
                            thresholds()
                    if c == GRAPH_AT - 1:
                        stats((b + 1) % NB)
                    if c == GRAPH_AT:
                        normalise(2 * b + 3 if b + 1 < NB else 2 * NB, (b + 1) % NB,
                                  fill_at("moe", "turn", b - 1)[1])
                add_residual("moe", b, 0, TG[:, 4:5])
            v_total[0] = done[0] + done[1]

            def sequence():
                start(v_total[0])

            def sequence_end():
                v_total[0] = done[0] + done[1]
                start(v_total[0])

            def prepare_next(phase, b, counted=False):
                nb = (b + 1) % NB
                if not counted:
                    stats(nb)
                at_ = [n + 1 for n, key in enumerate(BANK_FILLS[7])
                       if key == (phase, "turn", b - 1, 0)] or [fills_before(phase, 7)]
                normalise(pre_no(phase, b) + NB, nb, at_[0])

            def output(phase, b, gate):
                bank, value = fill_at(phase, "y", b)
                dve.wait_ge(filled[bank], value)
                xb = X[:, 2 * b:2 * b + 2, :]
                dve.scalar_tensor_tensor(xb, PS[:, bank, :].rearrange("p (a d) -> p a d", a=2), gate, xb,
                                         ALU.mult, ALU.add).then_inc(drained[bank], 1)
                dve.wait_ge(drained[bank], value)

            def maximum(phase, b, h):
                bank, value = fill_at(phase, "s", b, h)
                if h == 0:
                    dve.wait_ge(filled[7], fill_at(phase, "max", b - 1)[1] if b else fills_before(phase, 7))
                dve.wait_ge(filled[bank], value)
                if phase == "causal":
                    dve.tensor_reduce(NM[:, 0, h:h + 1], PS[:, bank, 0:P], AX, ALU.max, negate=True)
                    dve.tensor_reduce(NM[:, 1, h:h + 1], PS[:, bank, S:2 * S], AX, ALU.max,
                                      negate=True).then_inc(drained[bank], 1)
                else:
                    dve.tensor_reduce(NM[:, :, h], PS[:, bank, :].rearrange("p (a s) -> p a s", a=2), AX,
                                      ALU.max, negate=True).then_inc(drained[bank], 1)

            def divide(b, hp):
                bank, value = fill_at("latent", "o", b, hp)
                dve.wait_ge(drained[bank], value)
                link(dve.reciprocal(RD[:, hp % 2, :], RD[:, hp % 2, :]))
                dve.tensor_tensor(OT1[:, hp, :], OT1[:, hp, :], RD[:, hp % 2, :], ALU.mult).then_inc(divided, 1)

            sequence()
            prepare_next("latent", 0)
            for h in range(NH):
                maximum("latent", 0, h)
            for b in range(NB):
                for hp in range(NH // 2):
                    if hp:
                        divide(b, hp - 1)
                    if b < NB - 1:
                        maximum("latent", b + 1, 2 * hp)
                        maximum("latent", b + 1, 2 * hp + 1)
                        if hp == 4:
                            prepare_next("latent", b + 1)
                divide(b, NH // 2 - 1)
                output("latent", b, TG[:, 1:2])
            sequence_end()

            def ternary(b, p, nb):
                dve.wait_ge(filled[6], fill("ternary", 6, b, -1))
                for k in range(CH1):
                    m = min(P, H1 - k * P)
                    dve.wait_ge(tanh1_ready, b * CH1 + k + 1)
                    dve.scalar_tensor_tensor(HD[0:m, k, :], tanh_g[0:m, k % 2, 0:S], 1.0,
                                             PS[0:m, k % 3, S:2 * S], ALU.add, ALU.mult) \
                        .then_inc(drained[k % 3], 1)
                prepare_stats("ternary", b, nb)
                prepare_norm("ternary", b, nb)
                add_residual("ternary", b, 0, CA[:, 2:3])
            loop("ternary", ternary, 2)

            dve.wait_ge(late_loaded, LATE)

            def split(parts, source, rest_, ready, n, bank=None, value=None):
                link(dve.tensor_copy(parts[0], source))
                taken = dve.tensor_tensor(rest_, source, parts[0], ALU.subtract)
                if bank is None:
                    link(taken)
                else:
                    taken.then_inc(drained[bank], 1)
                    dve.wait_ge(drained[bank], value)
                link(dve.tensor_copy(parts[1], rest_))
                dve.tensor_tensor(parts[2], rest_, parts[1], ALU.subtract).then_inc(ready, 1)
                dve.wait_ge(ready, n)

            def split_operands(phase, b):
                n = 2 * b + (2 * NB if phase == "causal" else 0)
                if phase == "grouped":
                    bank, value = (7, fills_before(phase, 7)) if b == 0 else fill_at(phase, "turn", b - 1)
                    dve.wait_ge(drained[bank], value)
                    split([QP[:, k, :, :] for k in range(3)], XT[b % 2][:, :, :], rest, parts_ready, n + 1)
                    split([KP[0:DC, k, 0, :] for k in range(3)], ctxT[0:DC, b * S:(b + 1) * S],
                          rest[0:DC, 0, :], parts_ready, n + 2)
                    return
                for k, (what, parts) in enumerate((("q", QP), ("k", KP))):
                    bank, value = fill_at(phase, what, b)
                    dve.wait_ge(filled[bank], value)
                    split([parts[:, i, :, :] for i in range(3)], PS[:, bank, :].rearrange("p (g s) -> p g s", g=2),
                          rest, parts_ready, n + k + 1, bank, value)

            def split_max(phase, b):
                bank, value = fill_at(phase, "max", b)
                dve.wait_ge(filled[bank], value)
                split([NM3[:, k, :] for k in range(3)], PS[0:NH, bank, 0:S], RM[:, :], max_split,
                      b + 1 + (NB if phase == "causal" else 0), bank, value)

            def over_denominator(phase, b, g):
                bank, value = fill_at(phase, "den", b, g)
                dve.wait_ge(filled[bank], value)
                dve.reciprocal(RD[:, g % 2, :], PS[:, bank, 0:S]).then_inc(drained[bank], 1)
                dve.wait_ge(drained[bank], value)
                dve.tensor_tensor(OTN[:, g, :], OTR[:, g, :], RD[:, g % 2, :], ALU.mult).then_inc(norm_ready, 1)

            def attention(phase, gate):
                sequence()
                split_operands(phase, 0)
                prepare_next(phase, 0)
                for h in range(NH):
                    maximum(phase, 0, h)
                split_max(phase, 0)
                split_operands(phase, 1)
                for b in range(NB):
                    ahead = b < NB - 1
                    for hp in range(NH // 2 + 1):
                        if ahead and hp:
                            maximum(phase, b + 1, 2 * hp - 2)
                            maximum(phase, b + 1, 2 * hp - 1)
                            if hp == 4:
                                stats((b + 2) % NB)
                            if hp == 6:
                                prepare_next(phase, b + 1, True)
                        if hp in (3, 5):
                            over_denominator(phase, b, (hp - 3) // 2)
                    if ahead:
                        split_max(phase, b + 1)
                    over_denominator(phase, b, 2)
                    if b + 2 < NB:
                        split_operands(phase, b + 2)
                    over_denominator(phase, b, 3)
                    output(phase, b, gate)
                sequence_end()

            attention("grouped", TG[:, 2:3])

            def top_two():
                part()
                for i in range(2):
                    last = dve.max(T8[:, i, :], LG[:, i, 0:8])
                link(last)

            def lora(b, p, nb):
                dve.wait_ge(filled[0], fill("lora", 0, b, 0))
                n = E2 + E2 * R2
                ps = PS[:, 0, 0:2 * n].rearrange("p (a n) -> p a n", a=2)
                link(dve.tensor_copy(LG[:, :, 0:E2], ps[:, :, 0:E2]))
                top_two()
                dve.tensor_scalar(NMAX[:, :], T8[:, :, 0], -1.0, None, ALU.mult).then_inc(nmax_ready, 1)
                dve.wait_ge(nmax_ready, NB + b + 1)
                link(dve.memset(T8[:, :, 2:8], LOW))
                part()
                for i in range(2):
                    last = dve.match_replace(REP[:, i, 0:14], T8[:, i, :], LG[:, i, :], -3.3e38)
                link(last)
                link(dve.tensor_tensor(SC[:, :, 0:E2], LG[:, :, 0:E2], REP[:, :, 0:E2], ALU.not_equal))
                dve.wait_ge(exp_ready, b + 1)
                link(dve.tensor_tensor(SC[:, :, 0:E2], SC[:, :, 0:E2], EX[:, :, 0:E2], ALU.mult))
                link(dve.tensor_reduce(SU[:, :], SC[:, :, 0:E2], AX, ALU.add))
                link(dve.reciprocal(SU[:, :], SU[:, :]))
                for i in range(2):
                    last = dve.tensor_scalar(CM[:, i, 0:E2], SC[:, i, 0:E2], SU[:, i:i + 1], 2.0,
                                             ALU.mult, ALU.mult)
                link(last)
                for i in range(2):
                    w = CM[:, i, 0:E2].unsqueeze(2).to_broadcast([P, E2, R2])
                    last = dve.tensor_tensor(HW[:, i, 0:E2 * R2].rearrange("p (e r) -> p e r", e=E2),
                                             ps[:, i, E2:n].rearrange("p (e r) -> p e r", e=E2), w, ALU.mult)
                last.then_inc(drained[0], 1)
                prepare_stats("lora", b, nb)
                prepare_norm("lora", b, nb)
                add_residual("lora", b, 0, TG[:, 6:7])
            loop("lora", lora, 11)
            attention("causal", TG[:, 3:4])

            for b in range(NB):
                start(v_total[0])
                dve.wait_ge(filled[0], fill("adapter", 0, b, 0))
                n = E3 * R3 + E3
                ps = PS[:, 0, 0:2 * n].rearrange("p (a n) -> p a n", a=2)
                link(dve.tensor_scalar(LG[:, :, 0:E3], ps[:, :, E3 * R3:n], BONUS, None, ALU.add))
                dve.tensor_reduce(NMAX[:, :], LG[:, :, 0:E3], AX, ALU.max, negate=True).then_inc(nmax_ready, 1)
                dve.wait_ge(exp_ready, NB + b + 1)
                link(dve.reciprocal(RZ[:, :], Z[:, :]))
                for i in range(2):
                    last = dve.tensor_scalar(LG[:, i, 0:E3], EX[:, i, 0:E3], RZ[:, i:i + 1], None, ALU.mult)
                link(last)
                top_two()
                link(dve.memset(T8[:, :, 2:8], LOW))
                part()
                for i in range(2):
                    last = dve.match_replace(REP[:, i, 0:14], T8[:, i, :], LG[:, i, :], 0.0)
                link(last)
                link(dve.tensor_tensor(SC[:, :, 0:E3], LG[:, :, 0:E3], REP[:, :, 0:E3], ALU.subtract))
                link(dve.tensor_reduce(SU[:, :], SC[:, :, 0:E3], AX, ALU.add))
                link(dve.reciprocal(SU[:, :], SU[:, :]))
                for i in range(2):
                    last = dve.tensor_scalar(CM[:, i, 0:E3], SC[:, i, 0:E3], SU[:, i:i + 1], None, ALU.mult)
                link(last)
                for i in range(2):
                    w = CM[:, i, 0:E3].unsqueeze(2).to_broadcast([P, E3, R3])
                    last = dve.scalar_tensor_tensor(HW[:, i, :].rearrange("p (e r) -> p e r", e=E3),
                                                    ps[:, i, 0:E3 * R3].rearrange("p (e r) -> p e r", e=E3),
                                                    0.0, w, ALU.max, ALU.mult)
                last.then_inc(drained[0], 1)
                if b < NB - 1:
                    stats(b + 1)
                    normalise(pre_no("adapter", b) + NB, b + 1, fill("adapter", 7, b, -1))
                add_residual("adapter", b, 0, TG[:, 7:8])
                v_total[0] += done[1]

        @block.tensor
        def _(pe):
            mm = pe.matmul
            pe.wait_ge(consts_set, 1)
            for k in range(8):
                pe.sem_inc(filled[k], 1)
                pe.sem_inc(drained[k], 1)
            pe.wait_ge(first_loaded, 16 * N_FIRST)
            for k in range(2):
                for n in range(2):
                    last = mm(PS[0:DC, 4 + 2 * k + n, :], wqk0[:, k, :], ctxT[0:DC, n * 512:(n + 1) * 512],
                              start=True, stop=True)
                last.then_inc(qk_filled, 1)
            pe.wait_ge(qk_copied, 2)
            for b in range(NB):
                for i in range(2):
                    last = mm(PS[:, b, i * S:(i + 1) * S], qk0[:, 0, (2 * b + i) * P:(2 * b + i + 1) * P],
                              qk0[:, 1, b * S:(b + 1) * S], start=True, stop=True)
            last.then_inc(sim_filled, 1)

            def begin(phase, what, b, k=0):
                bank, value = fill_at(phase, what, b, k)
                pe.wait_ge(drained[bank], value - 1)
                return bank

            def fold(n, k):
                wq1, wkq1T, wqr1T, wkr1T, wkv1, wo1T = fold_w[n % 2]
                if k == 0:
                    pe.wait_ge(fold_loaded[n % 2], 16 * 6 * (n // 2 + 1))
                begin("moe", "fold", n, k)
                for h in range(4):
                    if k == 3:
                        q = DC * (h % 2)
                        last = mm(PS[q:q + DC, 7, (h // 2) * S:(h // 2 + 1) * S], wkv1[:, h, :],
                                  wo1T[:, h, :], start=True, stop=True)
                        continue
                    for c in range(2):
                        if k == 0:
                            last = mm(PS[0:96, 7, (h * 2 + c) * DC:(h * 2 + c + 1) * DC],
                                      wqr1T[:, h, c * 96:(c + 1) * 96], wkr1T[:, h, :], start=True, stop=True)
                        elif k == 1:
                            last = mm(PS[:, 7, h * DC:(h + 1) * DC], wkq1T[:, c, h, :], fold_b[:, h, c, :],
                                      start=c == 0, stop=c == 1)
                        else:
                            last = mm(PS[:, 7, c * S + h * DC:c * S + (h + 1) * DC],
                                      wq1[:, h, c * P:(c + 1) * P], fold_c[:, h, :], start=True, stop=True)
                last.then_inc(filled[7], 1)

            def graph_turn(b):
                pe.wait_ge(masked, b + 1)
                bank = begin("moe", "graph", b)
                for m in range(2):
                    for i in range(2):
                        last = pe.transpose(PS[:, bank, m * S + i * P:m * S + (i + 1) * P],
                                            AM[:, i, m * P:(m + 1) * P], ident[:, :])
                last.then_inc(filled[bank], 1)

            def turn(n, drain, value):
                pe.wait_ge(xn_ready, n + 1)
                if drain is not None:
                    pe.wait_ge(drained[7], drain)
                for c in range(2):
                    for i in range(2):
                        last = pe.transpose(PS[:, 7, c * S + i * P:c * S + (i + 1) * P],
                                            XN[:, i, c * P:(c + 1) * P], ident[:, :])
                last.then_inc(filled[7], 1)

            def prepare(phase, b):
                k = FILLS[phase][7] - 1
                turn(pre_no(phase, b) + NB, fill(phase, 7, b, k - 1), None)

            def free(phase, k, b, n):
                pe.wait_ge(drained[k], fill(phase, k, b, n - 1))

            for k in range(4):
                fold(0, k)
            graph_turn(0)
            turn(1, fill_at("moe", "graph", 0)[1], None)
            pe.wait_ge(sim_scaled, NB)
            pe.wait_ge(router_loaded, 16 * 2)
            pe.wait_ge(ident_ready, 1)

            for b in range(NB):
                p = b % 2
                begin("moe", "router", b)
                for i in range(2):
                    for c in range(2):
                        last = mm(PS[:, 7, i * E0:(i + 1) * E0], XT[p][:, c, i * P:(i + 1) * P], W_r[:, c, :],
                                  start=c == 0, stop=c == 1)
                last.then_inc(filled[7], 1)

                def chunks(c):
                    for f in range(2 * c, min(2 * c + 2, CH0)):
                        yield f, f % 2, f * P, min(P, F0 - f * P)

                def up(c):
                    for first, w in ((0, W_g), (2, W_u)):
                        k = first + c % 2
                        free("moe", k, b, c // 2)
                        for f, e, f0, m in chunks(c):
                            for d in range(2):
                                last = mm(PS[0:m, k, e * S:(e + 1) * S], w[:, d, f0:f0 + m], XT[p][:, d, :],
                                          start=d == 0, stop=d == 1)
                        last.then_inc(filled[k], 1)

                def weights(c):
                    k = 4 + c % 2
                    free("moe", k, b, c // 2)
                    for f, e, f0, m in chunks(c):
                        last = mm(PS[0:m, k, e * S:(e + 1) * S], sel_e[:, f0:f0 + m], CT[p][:, :],
                                  start=True, stop=True)
                    last.then_inc(filled[k], 1)

                def down(c):
                    k = 4 + c % 2
                    pe.wait_ge(drained[k], fill("moe", k, b, c // 2))
                    if c == 0:
                        pe.wait_ge(down_loaded, 16 * 2)
                        free("moe", 6, b, 0)
                    for f, e, f0, m in chunks(c):
                        for i in range(2):
                            last = mm(PS[:, 6, i * D:(i + 1) * D], H[0:m, c % 2, e, i * P:(i + 1) * P],
                                      W_d[0:m, f, :], start=f == 0 and i == 0, stop=f == CH0 - 1,
                                      skip_group_check=True)
                    last.then_inc(h_used if c < PAIRS0 - 1 else filled[6], 1)

                for c in range(PAIRS0):
                    if b == 0 and c % 4 == 0 and c < 12:
                        pe.wait_ge(expert_loaded[c // 4], 16 * 2)
                    up(c)
                    if c == 1:
                        pe.wait_ge(comb_ready, b + 1)
                        begin("moe", "combine", b)
                        turned_w = PS[:, 7, 0:P].bitcast(BF16)
                        for i in range(2):
                            last = pe.transpose(turned_w[:, i * P:(i + 1) * P], C3[:, i, :], identb[:, :])
                        last.then_inc(filled[7], 1)
                        bank, value = fill_at("moe", "combine", b)
                        pe.wait_ge(drained[bank], value)
                    if c >= 1:
                        weights(c - 1)
                    if c >= 2:
                        down(c - 2)
                    if b + 1 < NB and FOLD_AT <= c < FOLD_AT + 4:
                        fold(b + 1, c - FOLD_AT)
                    if c == GRAPH_AT and b + 1 < NB:
                        graph_turn(b + 1)
                    elif c == GRAPH_AT:
                        pe.wait_ge(abs_ready, 1)
                        bank = begin("moe", "abs", 0)
                        mm(PS[:, bank, 0:4], ones[:, :], absum[:, :], start=True, stop=True) \
                            .then_inc(filled[bank], 1)
                    if c == TURN_AT:
                        turn(2 * b + 3 if b + 1 < NB else 2 * NB, fill_at("moe", "turn", b)[1] - 1, None)
                weights(PAIRS0 - 1)
                down(PAIRS0 - 2)
                down(PAIRS0 - 1)

            def turned_max(phase, b):
                for h in (NH - 2, NH - 1):
                    bank, value = fill_at(phase, "s", b, h)
                    pe.wait_ge(drained[bank], value)
                bank = begin(phase, "max", b)
                for i in range(2):
                    last = pe.transpose(PS[0:NH, bank, i * P:(i + 1) * P], NM[:, i, :], ident[:, :])
                last.then_inc(filled[bank], 1)

            def turned_next(phase, b):
                bank, value = fill_at(phase, "turn", b)
                turn(pre_no(phase, b) + NB, value - 1, None)

            def xt_there(phase, b):
                if b == 0:
                    pe.wait_ge(drained[7], fills_before(phase, 7))
                else:
                    pe.wait_ge(drained[7], fill_at(phase, "turn", b - 1)[1])

            def latent_queries(b):
                xt_there("latent", b)
                for i in range(NH // 2):
                    bank = begin("latent", "q", b, i)
                    for c in range(2):
                        last = mm(PS[:, bank, 0:S], NW[:, c, i * P:(i + 1) * P], XT[b % 2][:, c, :],
                                  start=c == 0, stop=c == 1)
                    last.then_inc(filled[bank], 1)

            def latent_scores(b, h):
                if h == 0:
                    pe.wait_ge(kv_ready, b * 4 + 4)
                    for i in (NH // 2 - 2, NH // 2 - 1):
                        bank, value = fill_at("latent", "q", b, i)
                        pe.wait_ge(drained[bank], value)
                bank = begin("latent", "s", b, h)
                for i in range(2):
                    last = mm(PS[:, bank, i * S:(i + 1) * S], qT1[b % 2][0:DC, h, i * P:(i + 1) * P],
                              KR[b % 2][0:DC, :], start=True, stop=True)
                last.then_inc(filled[bank], 1)

            def latent_exponents(b, hp):
                bank = begin("latent", "st", b, hp)
                for e in range(2):
                    for t in range(2):
                        last = mm(PS[:, bank + e, t * S:(t + 1) * S], KR[b % 2][:, t * P:(t + 1) * P],
                                  qT1[b % 2][:, 2 * hp + e, :], start=True, stop=True)
                last.then_inc(filled[bank], 1)

            def latent_values(b, hp):
                s = hp % 2
                bank, value = fill_at("latent", "st", b, hp)
                pe.wait_ge(drained[bank], value)
                bank = begin("latent", "o", b, hp)
                for e in range(2):
                    v0 = DC * (1 - e)
                    for t in range(2):
                        last = mm(PS[:, bank, e * S:(e + 1) * S], VV[b % 2][:, t, v0:v0 + P],
                                  probs[:, s, e, t * S:(t + 1) * S], start=t == 0, stop=t == 1)
                last.then_inc(filled[bank], 1)

            latent_queries(0)
            for h in range(NH):
                latent_scores(0, h)
            turned_next("latent", 0)
            turned_max("latent", 0)
            for b in range(NB):
                ahead = b < NB - 1
                if ahead:
                    latent_queries(b + 1)
                pe.wait_ge(max_placed, (b + 1) * 16)
                for hp in range(NH // 2 + 1):
                    if hp < NH // 2:
                        latent_exponents(b, hp)
                    if hp:
                        latent_values(b, hp - 1)
                    if ahead and hp < NH // 2:
                        latent_scores(b + 1, 2 * hp)
                        latent_scores(b + 1, 2 * hp + 1)
                if ahead:
                    turned_max("latent", b + 1)
                    turned_next("latent", b + 1)
                bank = begin("latent", "y", b)
                for hp in range(NH // 2):
                    pe.wait_ge(divided, b * NH // 2 + hp + 1)
                    for i in range(2):
                        last = mm(PS[:, bank, i * D:(i + 1) * D], OT1[:, hp, i * P:(i + 1) * P], PM[:, hp, :],
                                  start=hp == 0 and i == 0, stop=hp == NH // 2 - 1, skip_group_check=True)
                last.then_inc(filled[bank], 1)

            pe.wait_ge(ternary_ready, 12)

            def ternary(b, p, nb):
                free("ternary", 7, b, 0)

                def down(k):
                    m = min(P, H1 - k * P)
                    pe.wait_ge(drained[k % 3], fill("ternary", k % 3, b, k // 3))
                    if k == 0:
                        free("ternary", 6, b, 0)
                    for i in range(2):
                        last = mm(PS[:, 6, i * D:(i + 1) * D], HD[0:m, k, i * P:(i + 1) * P], w3[0:m, k, :],
                                  start=k == 0 and i == 0, stop=k == CH1 - 1, skip_group_check=True)
                    if k == CH1 - 1:
                        last.then_inc(filled[6], 1)

                for k in range(CH1):
                    m = min(P, H1 - k * P)
                    free("ternary", k % 3, b, k // 3)
                    for w in range(2):
                        for c in range(2):
                            last = mm(PS[0:m, k % 3, w * S:(w + 1) * S], w12[:, 2 * w + c, k * P:k * P + m],
                                      XT[p][:, c, :], start=c == 0, stop=c == 1)
                    last.then_inc(filled[k % 3], 1)
                    if k >= 1:
                        down(k - 1)
                prepare("ternary", b)
                down(CH1 - 1)
            pairs(pe, ternary)
            pe.wait_ge(late_loaded, LATE)

            def attention(phase):
                wv, wo = (wv_2, wo_2) if phase == "grouped" else (wv_3, wo_3)
                causal = phase == "causal"
                key_heads = KEY_HEADS[phase]

                def operands(b, which):
                    context = ctxT[:, b * S:(b + 1) * S]
                    if which == "values":
                        for t in range(2):
                            bank = begin(phase, "v", b, t)
                            mm(PS[:, bank, :], context[:, t * P:(t + 1) * P], wv, start=True, stop=True) \
                                .then_inc(filled[bank], 1)
                    elif causal:
                        xt_there(phase, b)
                        bank = begin(phase, "q", b)
                        for g in range(2):
                            for c in range(2):
                                last = mm(PS[:, bank, g * S:(g + 1) * S], wq_3[:, c, g * P:(g + 1) * P],
                                          XT[b % 2][:, c, :], start=c == 0, stop=c == 1)
                        last.then_inc(filled[bank], 1)
                        bank = begin(phase, "k", b)
                        for g in range(2):
                            last = mm(PS[:, bank, g * S:(g + 1) * S], wk_3[:, g * P:(g + 1) * P],
                                      context[0:DC, :], start=True, stop=True)
                        last.then_inc(filled[bank], 1)

                def stacked(b, n, kind):
                    done = 2 * b + (2 * NB if causal else 0)
                    for bank, what, _, _ in stacks(phase, b, n):
                        if what != kind:
                            continue
                        keys = what == "ks"
                        pe.wait_ge(parts_ready, done + keys + 1)
                        begin(phase, what, b, n)
                        parts, rows = (KP, P if causal else DC) if keys else (QP, P)
                        for e in range(2):
                            h = 2 * n + e
                            for k in range(3):
                                last = mm(PS[0:ROWS, bank, e * S:(e + 1) * S], stack[0:rows, 3 * keys + k, h % 8, :],
                                          parts[0:rows, k, h // 8, :], start=k == 0, stop=k == 2)
                        last.then_inc(filled[bank], 1)

                def key_head(h):
                    return h * key_heads // NH

                def there(b, n):
                    for what, m in (("qs", n), ("ks", key_head(2 * n) // 2)):
                        bank, value = fill_at(phase, what, b, m)
                        pe.wait_ge(drained[bank], value)

                def scores(b, h):
                    if h % 2 == 0:
                        there(b, h // 2)
                    bank = begin(phase, "s", b, h)
                    for i in range(2):
                        n = P if causal and i == 0 else S
                        last = mm(PS[:, bank, i * S:i * S + n], QS[b % 2][0:ROWS, h, i * P:(i + 1) * P],
                                  KS[b % 2][0:ROWS, key_head(h), 0:n], start=True, stop=not causal)
                        if causal:
                            last = mm(PS[:, bank, i * S + i * P:i * S + (i + 1) * P], identb[:, :], maskS[:, :],
                                      start=False, stop=True)
                    last.then_inc(filled[bank], 1)

                def exponents(b, hp):
                    for h in (2 * hp, 2 * hp + 1):
                        bank = begin(phase, "st", b, h)
                        for t in range(2):
                            q0 = P if causal and t == 1 else 0
                            last = mm(PS[:, bank, t * S:t * S + S - q0],
                                      KS[b % 2][:, key_head(h), t * P:(t + 1) * P],
                                      QS[b % 2][:, h, q0:S], start=True, stop=not causal)
                            if causal:
                                last = mm(PS[:, bank, t * S:t * S + P], identb[:, :], maskT[:, :],
                                          start=False, stop=True)
                        last.then_inc(filled[bank], 1)

                def values(b, hp):
                    s, g = hp % 2, hp // 2
                    if s == 0:
                        begin(phase, "o", b, g)
                    for e in range(2):
                        h = 2 * hp + e
                        bank, value = fill_at(phase, "st", b, h)
                        pe.wait_ge(drained[bank], value)
                        j = h % 4
                        for t in range(2):
                            q0 = P if causal and t == 1 else 0
                            last = mm(PS[32 * j:32 * j + 32, 6, q0:S], VB[b % 2][:, t, h * 32:(h + 1) * 32],
                                      probs[:, s, e, t * S:t * S + S - q0], start=t == 0, stop=t == 1,
                                      skip_group_check=True)
                    last.then_inc(probs_used if s == 0 else filled[6], 1)

                def denominators(b, g):
                    bank, value = fill_at(phase, "o", b, g)
                    pe.wait_ge(drained[bank], value)
                    bank = begin(phase, "den", b, g)
                    mm(PS[:, bank, 0:S], sel_den[:, :], OTR[:, g, :], start=True, stop=True) \
                        .then_inc(filled[bank], 1)

                operands(0, "values")
                operands(0, "projected")
                for hp in range(NH // 2 + 1):
                    if hp:
                        scores(0, 2 * hp - 2)
                        scores(0, 2 * hp - 1)
                    if hp < NH // 2:
                        stacked(0, hp, "qs")
                        stacked(0, hp, "ks")
                turned_next(phase, 0)
                turned_max(phase, 0)
                operands(1, "values")
                operands(1, "projected")
                for b in range(NB):
                    ahead = b < NB - 1
                    before = NB + (3 * NB if causal else 0)
                    pe.wait_ge(max_placed, (b * 3 + before + 3) * 16)
                    pe.wait_ge(ones_set, 32)
                    for hp in range(NH // 2 + 1):
                        if hp < NH // 2:
                            exponents(b, hp)
                        if ahead and hp:
                            scores(b + 1, 2 * hp - 2)
                            scores(b + 1, 2 * hp - 1)
                        if ahead and hp < NH // 2:
                            stacked(b + 1, hp, "qs")
                        if hp:
                            values(b, hp - 1)
                        if ahead and hp < NH // 2:
                            stacked(b + 1, hp, "ks")
                        if hp in (3, 5):
                            denominators(b, (hp - 3) // 2)
                        if ahead and hp == 7:
                            turned_next(phase, b + 1)
                    if b + 2 < NB:
                        operands(b + 2, "values")
                    if ahead:
                        turned_max(phase, b + 1)
                    denominators(b, 2)
                    if b + 2 < NB:
                        operands(b + 2, "projected")
                    denominators(b, 3)
                    bank = begin(phase, "y", b)
                    for g in range(4):
                        pe.wait_ge(norm_ready, (b + (NB if causal else 0)) * 4 + g + 1)
                        for i in range(2):
                            last = mm(PS[:, bank, i * D:(i + 1) * D], OTN[:, g, i * P:(i + 1) * P], wo[:, g, :],
                                      start=g == 0 and i == 0, stop=g == 3, skip_group_check=True)
                    last.then_inc(filled[bank], 1)

            attention("grouped")

            def lora(b, p, nb):
                free("lora", 7, b, 0)
                free("lora", 0, b, 0)
                n = E2 + E2 * R2
                for i in range(2):
                    for c in range(2):
                        last = mm(PS[:, 0, i * n:(i + 1) * n], XT[p][:, c, i * P:(i + 1) * P], ra_2[:, c, :],
                                  start=c == 0, stop=c == 1)
                last.then_inc(filled[0], 1)
                free("lora", 6, b, 0)
                for i in range(2):
                    y = PS[:, 6, i * D:(i + 1) * D]
                    for c in range(2):
                        mm(y, XT[p][:, c, i * P:(i + 1) * P], wb_2[:, c, :], start=c == 0 and i == 0, stop=False,
                           skip_group_check=True)
                    mm(y, ones[0:1, :], biasb_2, start=False, stop=False, skip_group_check=True)
                pe.wait_ge(drained[0], fill("lora", 0, b, 0))
                free("lora", 1, b, 0)
                for i in range(2):
                    last = pe.transpose(PS[:, 1, i * P:(i + 1) * P], HW[:, i, :], ident[:, :])
                last.then_inc(filled[1], 1)
                prepare("lora", b)
                pe.wait_ge(drained[1], fill("lora", 1, b, 0))
                for i in range(2):
                    last = mm(PS[:, 6, i * D:(i + 1) * D], HWT[0:E2 * R2, i * P:(i + 1) * P], bt_2,
                              start=False, stop=True, skip_group_check=True)
                last.then_inc(filled[6], 1)
            pairs(pe, lora)
            attention("causal")

            for b in range(NB):
                p = b % 2
                free("adapter", 7, b, 0)
                free("adapter", 0, b, 0)
                n = E3 * R3 + E3
                for i in range(2):
                    for c in range(2):
                        mm(PS[:, 0, i * n:(i + 1) * n], XT[p][:, c, i * P:(i + 1) * P], dr_3[:, c, :],
                           start=c == 0, stop=False)
                    last = mm(PS[:, 0, i * n:(i + 1) * n], ones[0:1, :], bdr_3, start=False, stop=True)
                last.then_inc(filled[0], 1)
                pe.wait_ge(drained[0], fill("adapter", 0, b, 0))
                free("adapter", 1, b, 0)
                for i in range(2):
                    pe.transpose(PS[:, 1, i * P:(i + 1) * P], HW[:, i, :], ident[:, :])
                    last = pe.transpose(PS[0:E3, 1, S + i * P:S + (i + 1) * P], CM[:, i, 0:E3], ident[:, :])
                last.then_inc(filled[1], 1)
                if b < NB - 1:
                    prepare("adapter", b)
                pe.wait_ge(drained[1], fill("adapter", 1, b, 0))
                free("adapter", 6, b, 0)
                for i in range(2):
                    y = PS[:, 6, i * D:(i + 1) * D]
                    mm(y, HWT[:, i * P:(i + 1) * P], wu_3, start=True, stop=False)
                    last = mm(y, WT[:, i * P:(i + 1) * P], bu_3, start=False, stop=True)
                last.then_inc(filled[6], 1)


def kernel(**inputs):
    import ml_dtypes
    import numpy as np
    import concourse.bacc as bacc
    from concourse.bass_utils import run_bass_kernel_spmd

    f32 = np.float32
    g = {k: np.asarray(v) for k, v in inputs.items()}
    arrays = {}

    def chunked(w, c=P):
        return w.reshape(w.shape[0] // c, c, w.shape[1]).transpose(1, 0, 2)

    arrays["x"] = g["x"].reshape(NB * S, D)
    ctx = g["ctx_512"].reshape(NB * S, DC)
    swapped = np.concatenate([ctx[:, DC // 2:], ctx[:, :DC // 2]], axis=1)
    arrays["ctx"], arrays["ctxT"] = ctx, ctx.T
    arrays["ctx_swapped"], arrays["ctxT_swapped"] = swapped, swapped.T
    gates = np.concatenate([g["g_xattn"], g["g_ffn"], g["L0_xattn_gamma_raw"].reshape(1)])
    arrays["gates"] = np.broadcast_to(gates, (P, 9))
    arrays["ident"] = np.eye(P, dtype=f32)
    arrays["wqk0"] = np.stack([g["L0_xattn_Wq"].T, g["L0_xattn_Wk"].T], axis=1)

    w13, sw13 = g["L0_ffn_w13"], g["L0_ffn_sw13"]
    arrays["w_g0"] = chunked(np.concatenate([w13[:, :I0].reshape(-1, D), sw13[:2 * I0]]).T)
    arrays["w_u0"] = chunked(np.concatenate([w13[:, I0:].reshape(-1, D), sw13[2 * I0:]]).T)
    arrays["w_d0"] = np.concatenate([g["L0_ffn_w2"].transpose(0, 2, 1).reshape(-1, D), g["L0_ffn_sw2"].T])
    arrays["w_r0"] = chunked(g["L0_ffn_gate_w"].T)
    sel = np.zeros((3, PART, F0), f32)
    for f in range(F0):
        sel[:, min(f // I0, E0), f] = 1.0
    arrays["sel_e"] = sel.reshape(3 * PART, F0).astype(ml_dtypes.bfloat16)

    def groups(w):
        return w.reshape(4, 4, *w.shape[1:])

    arrays["wq1"] = groups(g["L1_xattn_Wq"].reshape(NH, P, D)).transpose(0, 2, 1, 3)
    arrays["wkq1T"] = groups(g["L1_xattn_w_kc_q"]).reshape(4, 4, P, 2, 96).transpose(0, 4, 3, 1, 2)
    arrays["wqr1T"] = groups(g["L1_xattn_W_qr"]).transpose(0, 3, 1, 2)
    arrays["wkr1T"] = groups(g["L1_xattn_W_kr"]).transpose(0, 3, 1, 2)
    arrays["wkv1"] = groups(g["L1_xattn_w_kc_kv"]).transpose(0, 2, 1, 3)
    arrays["wo1T"] = groups(g["L1_xattn_Wo"].T.reshape(NH, P, D)).transpose(0, 2, 1, 3)
    inv = (f32(1.0) / np.power(f32(10000.0), np.arange(0, DC, 2, dtype=f32) / f32(DC))).astype(f32)
    freq = np.arange(S, dtype=f32)[:, None] * inv[None, :]
    cos, sin = np.repeat(np.cos(freq), 2, axis=1), np.repeat(np.sin(freq), 2, axis=1)
    sin = np.concatenate([-sin[:, :DC // 2], sin[:, DC // 2:]], axis=1)
    rope = np.stack([cos, sin])
    arrays["ropeN"] = rope.reshape(2, 2, P, DC).transpose(2, 1, 0, 3)
    arrays["ropeT"] = rope.transpose(2, 0, 1)
    w12 = np.concatenate([chunked(g["L1_ffn_w1"].T), chunked(g["L1_ffn_w2"].T)], axis=1)
    arrays["w12"], arrays["w3T"] = w12, g["L1_ffn_w3"].T

    def slots(rows, cols=0):
        return np.zeros((rows, NH, 32), f32)

    v2 = slots(DC + 1)
    for h in range(NH):
        for d in range(16):
            v2[16 * (h // 4) + d, h, d] = 1.0
    v2[DC:, :, 16:] = 1.0
    arrays["sel_v2"] = v2.reshape(DC + 1, 512)
    wkv = g["L3_xattn_Wkv_expand"]
    v3 = slots(DC + 1)
    v3[:DC, :, :16] = wkv[D:].T.reshape(DC, NH, 16)
    v3[DC:, :, 16:] = 1.0
    arrays["wk_3"], arrays["wv_3"] = wkv[:D].T, v3.reshape(DC + 1, 512)
    arrays["wq_3"] = chunked(g["L3_xattn_Wq"].T)
    pairings = ((0, 1, 0, 1, 0, 2), (0, 0, 1, 1, 2, 0))
    stack = np.zeros((8, 16, 6, 8, 6, 16), f32)
    for keys in range(2):
        for block, part in enumerate(pairings[keys]):
            for h in range(8):
                stack[h, :, 3 * keys + part, h, block, :] = np.eye(16)
    arrays["key_ones"] = np.ones((3, NH, S), ml_dtypes.bfloat16)
    arrays["stack"] = stack.reshape(P, 6, 8, ROWS).astype(ml_dtypes.bfloat16)
    for name, w in (("wo_2", g["L2_xattn_Wc"]), ("wo_3", g["L3_xattn_Wout"])):
        o = np.zeros((NH, 32, D), f32)
        o[:, :16] = w.T.reshape(NH, 16, D)
        if name == "wo_2":
            o[0, 16] = g["L2_xattn_bc"]
        arrays[name] = chunked(o.reshape(512, D))
    arrays["wb_2"] = chunked(g["L2_ffn_W_base"].T)
    ra = np.concatenate([g["L2_ffn_W_router"], g["L2_ffn_A_w"].reshape(-1, D)]).T
    arrays["ra_2"] = chunked(ra)
    arrays["bt_2"] = g["L2_ffn_B_w"].transpose(0, 2, 1).reshape(E2 * R2, D)
    arrays["biasb_2"] = g["L2_ffn_b_base"].reshape(1, D)
    wd = g["L3_ffn_Wd"].transpose(1, 0, 2).reshape(D, E3 * R3)
    arrays["dr_3"] = chunked(np.concatenate([wd, g["L3_ffn_Wr"]], axis=1))
    arrays["bdr_3"] = np.concatenate([g["L3_ffn_bd"].reshape(-1), g["L3_ffn_br"]]).reshape(1, -1)
    arrays["wu_3"] = g["L3_ffn_Wu"].reshape(E3 * R3, D)
    arrays["bu_3"] = g["L3_ffn_bu"]
    den = np.zeros((P, P), f32)
    for j in range(4):
        den[32 * j + 16, 32 * j:32 * j + 32] = 1.0
    arrays["sel_den"] = den
    later = np.where(np.arange(P)[None, :] > np.arange(P)[:, None], f32(-1e38), f32(0.0))
    arrays["maskS"] = later.astype(ml_dtypes.bfloat16)
    arrays["maskT"] = later.T.astype(ml_dtypes.bfloat16)

    nc = bacc.Bacc("TRN2", target_bir_lowering=False, num_devices=1)
    arrays = {f"in_{k}": np.ascontiguousarray(v) for k, v in arrays.items()}
    aps = {k[3:]: nc.dram_tensor(k, v.shape, mybir.dt.from_np(v.dtype), kind="ExternalInput").ap()
           for k, v in arrays.items()}
    out = nc.dram_tensor("out", (NB * S, D), F32, kind="ExternalOutput").ap()
    build(nc, aps, out)
    got = run_bass_kernel_spmd(nc, [arrays], core_ids=[0]).results[0]["out"]
    return got.reshape(NB, S, D)
```

```python
from contextlib import ExitStack

import concourse.bass as bass
from concourse import mybir

F32 = mybir.dt.float32
BF16 = mybir.dt.bfloat16
ACT = mybir.ActivationFunctionType
ALU = mybir.AluOpType
AX = mybir.AxisListType.X

P = 128
NB = 4
S = 256
D = 256
TILES = NB * S // P
NH = 16
DC = 64
TOPK = int(S * 0.3)
E0, I0, K0 = 16, 176, 6
F0 = E0 * I0 + 2 * I0
CH0 = -(-F0 // P)
PAIRS0 = -(-CH0 // 2)
SLICE0 = 4 * 2 * P
PART = E0 + 1
H1 = 704
CH1 = -(-H1 // P)
E2, R2 = 8, 8
E3, R3 = 8, 16
LOW = -3.0e38
BONUS = 3.0 * (1.0 - 1.0 / 625.0)

KEY_HEADS = {"grouped": 4, "causal": NH}
ROWS = 6 * 16
ALL_ROWS = ROWS + 3

FOLD_AT = 3
ROUNDS_AT = {1: (0, 1), 2: (2, 3), 3: (4, 5), 4: (6,), 5: (7,), 6: (8,), 7: (9,)}
GRAPH_AT = 9
TURN_AT = 11

PHASES = ["moe", "latent", "ternary", "grouped", "causal"]
ATTENTIONS = ("latent", "grouped", "causal")
FILLS = {
    "moe": {0: 7, 1: 6, 2: 7, 3: 6, 4: 7, 5: 6, 6: 1},
    "ternary": {0: 2, 1: 2, 2: 2, 6: 1, 7: 1},
}


def job(phase, b):
    if phase == "grouped":
        return ("lora", b - 1, b - 1) if b else None
    return ("adapter", b - 1, NB + b - 1) if b else ("lora", NB - 1, NB - 1)


def normalised():
    order = []
    for b in range(NB):
        order += [("graph", b), ("moe", b)]
    order += [("latent", b) for b in range(NB)] + [("ternary", b) for b in range(NB)] + [("grouped", 0)]
    for phase in ("grouped", "causal"):
        order.append((phase, 1))
        for b in range(NB + (phase == "causal")):
            if job(phase, b):
                order.append(job(phase, b)[:2])
            if b + 2 < NB:
                order.append((phase, b + 2))
            elif b + 2 == NB and phase == "grouped":
                order.append(("causal", 0))
    return order


NORMALISED = normalised()


def after_moe(b):
    return NORMALISED.index(("moe", b + 1) if b + 1 < NB else ("latent", 0))


JOB_TURN, JOB_DOWN, JOB_CHOICE, JOB_WEIGHTS, JOB_MIXED = 1, 2, 4, 5, 7
NEXT_TURN = 8


def front(phase, b):
    if phase == "latent":
        return [(i % 2, "q", b, i) for i in range(NH // 2)]
    projected = [(0, "q", b, 0), (1, "k", b, 0)] if phase == "causal" else []
    return [(t, "v", b, t) for t in range(2)] + projected


def stacks(phase, b, n):
    shift = 2 if b == 0 and n % 2 else 0
    return [(5 - shift, "qs", b, n)] + ([(4 - shift, "ks", b, n)] if n < KEY_HEADS[phase] // 2 else [])


def turns_next(phase, b):
    return b + 1 < NB and not (phase == "causal" and b + 2 == NB)


def attention_fills(phase):
    stacked = phase != "latent"

    def scores(b, n):
        return [(h % 2, "s", b, h) for h in (2 * n, 2 * n + 1)] if b < NB and 0 <= n < NH // 2 else []

    order = front(phase, 0)
    for hp in range(NH // 2 + 1):
        if stacked:
            if hp < NH // 2:
                order += stacks(phase, 0, hp)
            order += scores(0, hp - 1)
        else:
            order += scores(0, hp)
    order += [(7, "turn", 0, 0), (7, "max", 0, 0)]
    order += front(phase, 1)
    for b in range(NB):
        ahead = b + 1 < NB
        for hp in range(NH // 2 + 1):
            if stacked and job(phase, b) and hp == JOB_TURN:
                order.append((7, "job_turn", b, 0))
            if stacked and job(phase, b) and hp == JOB_DOWN:
                order.append((7, "job_down", b, 0))
            if hp < NH // 2:
                order += [(2 + h % 2, "st", b, h) for h in (2 * hp, 2 * hp + 1)] if stacked \
                    else [(2 + 2 * (hp % 2), "st", b, hp)]
            if stacked:
                order += scores(b + 1, hp - 1)
            if hp and (phase == "latent" or hp % 2 == 0):
                order.append((6, "o", b, hp - 1 if phase == "latent" else hp // 2 - 1))
            if not stacked:
                order += scores(b + 1, hp)
            elif ahead and hp < NH // 2:
                order += stacks(phase, b + 1, hp)
            if stacked and hp in (3, 5):
                order.append((7, "den", b, (hp - 3) // 2))
            if stacked and job(phase, b) and hp == JOB_MIXED:
                order.append((7, "job_mixed", b, 0))
            if stacked and turns_next(phase, b) and hp == NEXT_TURN:
                order.append((7, "turn", b + 1, 0))
            if not stacked and ahead and hp == 7:
                order.append((7, "turn", b + 1, 0))
        if stacked and job(phase, b):
            order.append((2, "job_y", b, 0))
        if ahead:
            order.append((7, "max", b + 1, 0))
        if stacked:
            order += [(5, "den", b, 2), (4, "den", b, 3)]
        if b + 2 < NB:
            order += front(phase, b + 2)
        order.append((6 if stacked else 7, "y", b, 0))
    if phase == "causal":
        order += [(7, "job_" + step, NB, 0) for step in ("turn", "down", "mixed")] + [(2, "job_y", NB, 0)]
    return order


def moe_fills():
    order = [("fold", 0, k) for k in range(3)] + [("graph", 0, 0), ("fold", 0, 3), ("turn", -1, 0)]
    for b in range(NB):
        order += [("router", b, 0), ("combine", b, 0)]
        if b + 1 < NB:
            order += [("fold", b + 1, k) for k in range(4)] + [("graph", b + 1, 0)]
        else:
            order.append(("abs", 0, 0))
        order.append(("turn", b, 0))
    return [("moe",) + key for key in order]


def all_fills():
    banks = {k: ["start"] for k in range(8)}
    banks[7] += moe_fills()
    for phase in PHASES:
        if phase in ATTENTIONS:
            for bank, what, b, k in attention_fills(phase):
                banks[bank].append((phase, what, b, k))
        else:
            for bank, n in FILLS[phase].items():
                banks[bank] += [(phase, b, k) for b in range(NB) for k in range(n)]
    return banks


BANK_FILLS = all_fills()


def fills_before(phase, bank):
    for n, key in enumerate(BANK_FILLS[bank]):
        if key[0] in PHASES[PHASES.index(phase):]:
            return n
    return len(BANK_FILLS[bank])


def fill(phase, bank, b, k):
    return fills_before(phase, bank) + b * FILLS[phase][bank] + k + 1


def fill_at(phase, what, b, k=0):
    for bank, keys in BANK_FILLS.items():
        if (phase, what, b, k) in keys:
            return bank, keys.index((phase, what, b, k)) + 1
    raise KeyError((phase, what, b, k))


def build(nc, a, out):
    with ExitStack() as ctx:
        def sb(name, shape, dt=F32):
            return ctx.enter_context(nc.sbuf_tensor(name, shape, dt))

        def sem(name):
            return ctx.enter_context(nc.semaphore(name))

        PS = ctx.enter_context(nc.psum_tensor("PS", [P, 8, 512], F32))

        X = sb("X", [P, TILES, D])
        XN = sb("XN", [P, 2, D])
        XT = [sb(f"XT{p}", [P, 2, S]) for p in range(2)]
        BN = sb("BN", [P, 2, 6])
        MV = sb("MV", [P, 2, 2])
        RS = sb("RS", [P, 2])
        neg_half = sb("neg_half", [P, 2])
        eps = sb("eps", [P, 2])
        carrier = sb("carrier", [P, 4])
        ident = sb("ident", [P, P])
        identb = sb("identb", [P, P], BF16)
        ones = sb("ones", [P, P])
        gates = sb("gates", [P, 9])
        TG = sb("TG", [P, 9])
        CA = sb("CA", [P, 4])
        ctxT = sb("ctxT", [DC + 1, NB * S])
        W_g = sb("W_g", [P, 2, F0])
        W_u = sb("W_u", [P, 2, F0])
        W_d = sb("W_d", [P, CH0, D])
        W_r = sb("W_r", [P, 2, E0])
        sel_e = sb("sel_e", [3 * PART, F0], BF16)
        tanh_g = sb("tanh_g", [P, 2, 512])
        mlp_tmp = sb("mlp_tmp", [P, 4 * 512])
        gated, hidden = mlp_tmp[:, 0:512], mlp_tmp[:, 512:1024]
        H = mlp_tmp[:, 1024:2048].rearrange("p (a b s) -> p a b s", a=2, b=2)
        CT = [sb(f"CT{p}", [3 * PART, S], BF16) for p in range(2)]
        NMAX = sb("NMAX", [P, 2])
        EX = sb("EX", [P, 2, 16])
        Z = sb("Z", [P, 2])
        RZ = sb("RZ", [P, 2])
        SC = sb("SC", [P, 2, 18])
        T8 = sb("T8", [P, 2, 8])
        REP = sb("REP", [P, 2, 18])
        CM = sb("CM", [P, 2, PART])
        SU = sb("SU", [P, 2])
        C3 = sb("C3", [P, 2, P], BF16)
        NW = sb("NW", [P, 2, NH * DC])
        PM = sb("PM", [P, NH // 2, D])
        ropeN = sb("ropeN", [P, 2, 2, DC])
        ropeT = sb("ropeT", [DC, 2, S])
        KR = [sb(f"KR{p}", [DC + 1, S]) for p in range(2)]
        VV = [sb(f"VV{p}", [P, 2, 3 * DC]) for p in range(2)]
        def areas(flat, start):
            at = [start]

            def cut(parts, *shape):
                n = 1
                for x in shape:
                    n *= x
                v = flat[0:parts, at[0]:at[0] + n]
                at[0] += n
                assert at[0] <= flat.shape[1]
                if len(shape) == 2:
                    return v.rearrange("p (a b) -> p a b", a=shape[0])
                if len(shape) == 3:
                    return v.rearrange("p (a b c) -> p a b c", a=shape[0], b=shape[1])
                return v
            return cut

        arena = sb("arena", [P, 8992])
        FG = NH // 4
        fold_w = []
        for slot in range(2):
            cut = areas(arena, slot * 4352)
            fold_w.append([cut(P, 4, D), cut(96, 2, 4, P), cut(DC, 4, 192), cut(DC, 4, DC),
                           cut(P, 4, DC), cut(P, 4, D)])
        W_d_flat = W_d[:, :, :].rearrange("p a b -> p (a b)")
        cut = areas(arena, 0)
        qT1 = [cut(DC + 1, NH, S), areas(W_d_flat, 0)(DC + 1, NH, S)]
        probs = cut(P, 2, 2, 512)
        OT1 = cut(P, NH // 2, S)
        NM = cut(P, 2, NH)
        NMT = cut(NH, S)
        RD = cut(P, 2, S)
        cut = areas(arena, 0)
        VB = [cut(P, 2, 512) for _ in range(2)]
        XJ = cut(P, 2, S)
        cut = areas(arena, 4096 + 2048)
        OTN, OTR = cut(P, 4, S), cut(P, 4, S)
        fold_b = sb("fold_b", [96, 4, 2, DC])
        fold_c = sb("fold_c", [P, 4, DC])
        wqk0 = sb("wqk0", [DC, 2, DC])
        qk0 = areas(W_d_flat, 0)(DC, 2, NB * S)
        mlp_w = sb("mlp_w", [P, 4 * H1 + CH1 * D])
        cut = areas(mlp_w, 0)
        sim = [cut(P, 2, S) for _ in range(NB)]
        sg, work, AM, S2 = cut(P, 2, S), cut(P, 2, S), cut(P, 2, S), cut(P, 2, S)
        g8 = sb("g8", [P, 2, 8])
        def half(cut, parts, *shape):
            n = 1
            for x in shape:
                n *= x
            v = cut(parts, n // 2).bitcast(BF16)
            if len(shape) == 2:
                return v.rearrange("p (a b) -> p a b", a=shape[0])
            return v.rearrange("p (a b c) -> p a b c", a=shape[0], b=shape[1])

        cut = areas(W_d_flat, 0)
        QS = [half(cut, ALL_ROWS, NH, S) for _ in range(2)]
        QP, KP = half(cut, P, 3, 2, S), half(cut, P, 3, 2, S)
        rest = cut(P, 2, S)
        cut = areas(mlp_w, 0)
        KS = [half(cut, ALL_ROWS, NH, S) for _ in range(2)]
        NM3, RM = sb("NM3", [NH, 3, S], BF16), sb("RM", [NH, S])
        cut = areas(W_g[:, :, :].rearrange("p a b -> p (a b)"), 0)
        stack = half(cut, P, 6, 8, ROWS)
        wv_2 = cut(DC + 1, 512)
        wo_2 = cut(P, 4, D)
        wb_2 = cut(P, 2, D)
        ra_2 = cut(P, 2, E2 + E2 * R2)
        bt_2 = cut(E2 * R2, D)
        biasb_2 = cut(1, D)
        cut = areas(W_u[:, :, :].rearrange("p a b -> p (a b)"), 0)
        wq_3 = cut(P, 2, D)
        wk_3, wv_3 = cut(DC, D), cut(DC + 1, 512)
        wo_3 = cut(P, 4, D)
        dr_3 = cut(P, 2, E3 * R3 + E3)
        bdr_3 = cut(1, E3 * R3 + E3)
        wu_3 = cut(E3 * R3, D)
        bu_3 = cut(E3, D)
        ctxTs = cut(DC, NB * S)
        KG = cut(DC, 3 * NB * S // 2).bitcast(BF16).rearrange("p (k s) -> p k s", k=3)
        r3, r4 = cut(DC, S), cut(DC, S)
        sel_den = sb("sel_den", [P, P])
        maskS = sb("maskS", [P, P], BF16)
        maskT = sb("maskT", [P, P], BF16)
        cut = areas(mlp_w, 0)
        w12, w3 = cut(P, 4, H1), cut(P, CH1, D)
        absum, mean_w = sb("absum", [P, 4]), sb("mean_w", [P, 4])
        thr = sb("thr", [P, 2, 3])
        less = mlp_tmp[:, 0:2 * H1]
        HD = areas(arena, 0)(P, CH1, S)
        HW = sb("HW", [P, 2, P])
        HWT = sb("HWT", [P, S])
        WT = sb("WT", [E3, S])
        LG = sb("LG", [P, 2, 14])
        LR = sb("LR", [P, 2, E3 * R3 + E3])
        ctxN = sb("ctxN", [P, TILES, DC])
        ctxNs = sb("ctxNs", [P, TILES, DC])
        r1, r2 = sb("r1", [P, 2 * DC]), sb("r2", [P, 2 * DC])

        filled = [sem(f"bank_filled{k}") for k in range(8)]
        drained = [sem(f"bank_drained{k}") for k in range(8)]
        consts_set = sem("consts_set")
        ident_ready = sem("ident_ready")
        context_loaded = sem("context_loaded")
        first_loaded = sem("first_loaded")
        fold_loaded = [sem(f"fold_loaded{n}") for n in range(2)]
        down_loaded = sem("down_loaded")
        router_loaded = sem("router_loaded")
        expert_loaded = [sem(f"expert_loaded{k}") for k in range(3)]
        rope_loaded = sem("rope_loaded")
        mlp_loaded = sem("mlp_loaded")
        late_loaded = sem("late_loaded")
        stored = sem("stored")
        v_step = sem("v_step")
        g_step = sem("g_step")
        gates_ready = sem("gates_ready")
        qk_filled, qk_copied = sem("qk_filled"), sem("qk_copied")
        sim_filled, sim_scaled, sg_ready = sem("sim_filled"), sem("sim_scaled"), sem("sg_ready")
        masked = sem("masked")
        graph_added = sem("graph_added")
        mv_ready, rstd_ready, xn_ready = sem("mv_ready"), sem("rstd_ready"), sem("xn_ready")
        nmax_ready, comb_ready = sem("nmax_ready"), sem("comb_ready")
        tanh_ready, h_used = sem("tanh_ready"), sem("h_used")
        kv_ready = sem("kv_ready")
        max_placed, max_split = sem("max_placed"), sem("max_split")
        keys_ready = sem("keys_ready")
        parts_ready, ones_set = sem("parts_ready"), sem("ones_set")
        abs_ready, thr_ready, ternary_ready = sem("abs_ready"), sem("thr_ready"), sem("ternary_ready")
        tanh1_ready = sem("tanh1_ready")
        probs_used = sem("probs_used")
        norm_ready, divided = sem("norm_ready"), sem("divided")
        exp_ready, weighted = sem("exp_ready"), sem("weighted")
        block = ctx.enter_context(nc.Block())

        def pairs(eng, body):
            with eng.Fori(0, NB // 2) as j:
                for p in range(2):
                    body(j * 2 + p, p, (j * 2 + 1) if p == 0 else (j * -2 + 2))

        def next_no(phase, b):
            return NORMALISED.index((phase, 0)) + b + 1

        N_FIRST = 3

        @block.sync
        def _(sp):
            xv = a["x"].rearrange("(t p) d -> p t d", p=P)
            sp.dma_start(wqk0[:, :, :], a["wqk0"]).then_inc(context_loaded, 16)
            sp.dma_start(ctxT[0:DC, :], a["ctxT"]).then_inc(context_loaded, 16)
            sp.dma_start(ident[:, :], a["ident"]).then_inc(first_loaded, 16)
            sp.dma_start(gates[:, :], a["gates"]).then_inc(first_loaded, 16)
            sp.dma_start(X[:, :, :], xv).then_inc(first_loaded, 16)

            def fold_group(n):
                for dst, name in zip(fold_w[n % 2], ("wq1", "wkq1T", "wqr1T", "wkr1T", "wkv1", "wo1T")):
                    sp.dma_start(dst, a[name][n]).then_inc(fold_loaded[n % 2], 16)

            fold_group(0)
            sp.dma_start(W_r[:, :, :], a["w_r0"]).then_inc(router_loaded, 16)
            sp.dma_start(sel_e[:, :], a["sel_e"]).then_inc(router_loaded, 16)
            for k in range(3):
                cols = slice(k * SLICE0, (k + 1) * SLICE0 if k < 2 else F0)
                sp.dma_start(W_g[:, :, cols], a["w_g0"][:, :, cols]).then_inc(expert_loaded[k], 16)
                sp.dma_start(W_u[:, :, cols], a["w_u0"][:, :, cols]).then_inc(expert_loaded[k], 16)
                if k == 0:
                    sp.wait_ge(sim_filled, NB)
                    full = F0 // P
                    sp.dma_start(W_d[:, 0:full, :], a["w_d0"][0:full * P, :].rearrange("(c p) d -> p c d", p=P)) \
                        .then_inc(down_loaded, 16)
                    sp.dma_start(W_d[0:F0 - full * P, full, :], a["w_d0"][full * P:F0, :]) \
                        .then_inc(down_loaded, 16)
            fold_group(1)
            sp.dma_start(ctxN[:, :, :], a["ctx"].rearrange("(t p) d -> p t d", p=P)).then_inc(rope_loaded, 16)
            sp.dma_start(ctxNs[:, :, :], a["ctx_swapped"].rearrange("(t p) d -> p t d", p=P)) \
                .then_inc(rope_loaded, 16)
            sp.dma_start(ropeN[:, :, :, :], a["ropeN"]).then_inc(rope_loaded, 16)
            sp.dma_start(ropeT[:, :, :], a["ropeT"]).then_inc(rope_loaded, 16)
            for n in range(2, FG):
                sp.wait_ge(filled[7], fill_at("moe", "fold", n - 2, 3)[1])
                fold_group(n)
            sp.wait_ge(graph_added, NB)
            sp.dma_start(w12[:, :, :], a["w12"]).then_inc(mlp_loaded, 16)
            full = H1 // P
            sp.dma_start(w3[:, 0:full, :], a["w3T"][0:full * P, :].rearrange("(c p) d -> p c d", p=P)) \
                .then_inc(mlp_loaded, 16)
            sp.dma_start(w3[0:H1 - full * P, full, :], a["w3T"][full * P:H1, :]).then_inc(mlp_loaded, 16)
            sp.wait_ge(filled[6], fill("moe", 6, NB - 1, 0))
            sp.dma_start(ctxTs, a["ctxT_swapped"]).then_inc(rope_loaded, 16)
            for dst, name in ((stack, "stack"), (wv_2, "sel_v2"), (wo_2, "wo_2"),
                              (wb_2, "wb_2"), (ra_2, "ra_2"), (bt_2, "bt_2"),
                              (biasb_2, "biasb_2"), (wq_3, "wq_3"), (wk_3, "wk_3"), (wv_3, "wv_3"),
                              (wo_3, "wo_3"), (dr_3, "dr_3"), (bdr_3, "bdr_3"), (wu_3, "wu_3"),
                              (bu_3, "bu_3"), (sel_den[:, :], "sel_den"), (maskS[:, :], "maskS"),
                              (maskT[:, :], "maskT")):
                sp.dma_start(dst, a[name]).then_inc(late_loaded, 16)

            def place_max(phase):
                for b in range(NB):
                    if phase == "latent":
                        bank, value = fill_at(phase, "max", b)
                        sp.wait_ge(drained[bank], value)
                        sp.dma_start(qT1[b % 2][DC:DC + 1, :, :], NMT).then_inc(max_placed, 16)
                        continue
                    sp.wait_ge(max_split, b + 1 + (NB if phase == "causal" else 0))
                    for part in range(3):
                        row = ROWS + part
                        sp.dma_start(QS[b % 2][row:row + 1, :, :], NM3[:, part, :]).then_inc(max_placed, 16)

            place_max("latent")
            sp.wait_ge(filled[6], fill("ternary", 6, NB - 1, 0))
            for p in range(2):
                sp.dma_start(KS[p][ROWS:ALL_ROWS, :, :], a["key_ones"]).then_inc(ones_set, 16)
            place_max("grouped")
            place_max("causal")
            ov = out.rearrange("(t p) d -> p t d", p=P)
            for b in range(NB):
                bank, value = fill_at("causal", "job_y", b + 1)
                sp.wait_ge(drained[bank], value)
                sp.dma_start(ov[:, 2 * b:2 * b + 2, :], X[:, 2 * b:2 * b + 2, :]).then_inc(stored, 16)
            sp.wait_ge(stored, 16 * NB)

        LATE = 16 * 18

        @block.gpsimd
        def _(pool):
            def rstd(n, first=False):
                pool.wait_ge(mv_ready, n + 1)
                if not first:
                    pool.wait_ge(xn_ready, n)
                pool.tensor_tensor(RS[:, :], MV[:, :, 1], eps[:, :], ALU.add).then_inc(g_step, 1)
                pool.wait_ge(g_step, n + 1)
                pool.tensor_tensor(RS[:, :], RS[:, :], neg_half[:, :], ALU.pow).then_inc(rstd_ready, 1)

            pool.wait_ge(consts_set, 1)

            rstd(0, first=True)
            for n in range(1, 2 * NB + 1):
                rstd(n)

            def prepare(phase):
                def body(b, p, nb):
                    rstd(next_no(phase, b))
                return body

            pool.wait_ge(rope_loaded, 16 * 5)
            pool.wait_ge(context_loaded, 16 * 2)

            def rotate(b):
                p = b % 2
                if b >= 2:
                    bank, value = fill_at("latent", "o", b - 2, NH // 2 - 1)
                    pool.wait_ge(filled[bank], value)
                s = slice(b * S, (b + 1) * S)
                rn = [ropeN[:, :, k, :] for k in range(2)]
                v1 = r1[:, :].rearrange("p (a b) -> p a b", a=2)
                v2 = r2[:, :].rearrange("p (a b) -> p a b", a=2)
                n = b * 4
                pool.tensor_tensor(v1, ctxN[:, 2 * b:2 * b + 2, :], rn[0], ALU.mult)
                pool.tensor_tensor(v2, ctxNs[:, 2 * b:2 * b + 2, :], rn[1], ALU.mult).then_inc(kv_ready, 1)
                pool.wait_ge(kv_ready, n + 1)
                pool.tensor_tensor(r3[:, :], ctxT[0:DC, s], ropeT[:, 0, :], ALU.mult)
                pool.tensor_tensor(r4[:, :], ctxTs[:, s], ropeT[:, 1, :], ALU.mult).then_inc(kv_ready, 1)
                pool.wait_ge(kv_ready, n + 2)
                pool.tensor_tensor(VV[p][:, :, DC:2 * DC], v1, v2, ALU.add).then_inc(kv_ready, 1)
                pool.wait_ge(kv_ready, n + 3)
                pool.tensor_tensor(KR[p][0:DC, :], r3[:, :], r4[:, :], ALU.add).then_inc(kv_ready, 1)
                pool.wait_ge(kv_ready, n + 4)

            rotate(0)
            rstd(next_no("latent", 0))
            rotate(1)
            for b in range(NB):
                if b < NB - 1:
                    rstd(next_no("latent", b + 1))
                if b < NB - 2:
                    rotate(b + 2)

            left = areas(W_d_flat, NH * S)(DC, NB * S)
            steps = ((KG[:, 0, :], ctxT[0:DC, :], None), (left, ctxT[0:DC, :], KG[:, 0, :]),
                     (KG[:, 1, :], left, None), (KG[:, 2, :], left, KG[:, 1, :]))
            for k, (dst, src, less_) in enumerate(steps):
                if less_ is None:
                    pool.tensor_copy(dst, src).then_inc(keys_ready, 1)
                else:
                    pool.tensor_tensor(dst, src, less_, ALU.subtract).then_inc(keys_ready, 1)
                pool.wait_ge(keys_ready, k + 1)

            pool.wait_ge(thr_ready, 1)
            for k, (w, c) in enumerate(((w12[:, 0:2, :], 0), (w12[:, 2:4, :], 1), (w3[:, 0:5, :], 2),
                                        (w3[0:H1 - 5 * P, 5, :], 2))):
                parts = P if k < 3 else H1 - 5 * P
                wf = w.rearrange("p a b -> p (a b)") if k < 3 else w
                n = 2 * H1 if k < 2 else (5 * D if k == 2 else D)
                pool.tensor_scalar(less[0:parts, 0:n], wf, thr[0:parts, 1, c:c + 1], None, ALU.is_lt) \
                    .then_inc(ternary_ready, 1)
                pool.tensor_scalar(wf, wf, thr[0:parts, 0, c:c + 1], None, ALU.is_gt) \
                    .then_inc(ternary_ready, 1)
                pool.wait_ge(ternary_ready, 3 * k + 2)
                pool.tensor_tensor(wf, wf, less[0:parts, 0:n], ALU.subtract).then_inc(ternary_ready, 1)
                pool.wait_ge(ternary_ready, 3 * k + 3)
            pairs(pool, prepare("ternary"))

            for n in range(NORMALISED.index(("grouped", 1)), len(NORMALISED)):
                rstd(n)

        @block.scalar
        def _(act):
            for n in range(2):
                for k in range(2):
                    act.wait_ge(qk_filled, 2 * n + k + 1)
                    act.activation(qk0[:, k, n * 512:(n + 1) * 512], PS[0:DC, 4 + 2 * k + n, :], ACT.Copy) \
                        .then_inc(qk_copied, 1)
                for b in (2 * n, 2 * n + 1):
                    act.wait_ge(sim_filled, b + 1)
                    act.activation(sim[b], PS[:, b, :].rearrange("p (a b) -> p a b", a=2), ACT.Copy, scale=0.0625) \
                        .then_inc(sim_scaled, 1)

            act.wait_ge(first_loaded, 16 * N_FIRST)
            act.activation(TG[:, 0:8], gates[:, 0:8], ACT.Tanh)
            act.activation(TG[:, 8:9], gates[:, 8:9], ACT.Tanh, scale=0.5).then_inc(gates_ready, 1)
            act.activation(identb[:, :], ident[:, :], ACT.Copy).then_inc(ident_ready, 1)

            def edge_gates(b):
                act.wait_ge(sim_scaled, b + 1)
                if b:
                    act.wait_ge(masked, b)
                act.activation(sg, sim[b], ACT.Tanh, scale=0.5).then_inc(sg_ready, 1)

            def evacuate(phase, what, b, k, *copies):
                bank, value = fill_at(phase, what, b, k)
                act.wait_ge(filled[bank], value)
                for dst, src in copies:
                    last = act.activation(dst, src, ACT.Copy)
                last.then_inc(drained[bank], 1)

            def fold_out(n, k):
                dst, src = [(fold_b[:, :, :, :], PS[0:96, 7, :].rearrange("p (h c d) -> p h c d", h=4, c=2)),
                            (fold_c[:, :, :], PS[:, 7, 0:4 * DC].rearrange("p (h d) -> p h d", h=4)),
                            (NW[:, :, 4 * n * DC:(4 * n + 4) * DC], PS[:, 7, :].rearrange("p (c n) -> p c n", c=2)),
                            (PM[:, 2 * n:2 * n + 2, :], PS[:, 7, :].rearrange("p (h d) -> p h d", h=2))][k]
                evacuate("moe", "fold", n, k, (dst, src))

            edge_gates(0)
            for k in range(4):
                fold_out(0, k)

            def xt_out(value, p):
                act.wait_ge(filled[7], value)
                act.activation(XT[p][:, :, :], PS[:, 7, :].rearrange("p (c s) -> p c s", c=2), ACT.Copy) \
                    .then_inc(drained[7], 1)

            xt_out(fill_at("moe", "turn", -1)[1], 0)

            for b in range(NB):
                p = b % 2
                act.wait_ge(nmax_ready, b + 1)
                for i in range(2):
                    last = act.activation(EX[:, i, :], PS[:, 7, i * E0:(i + 1) * E0], ACT.Exp,
                                          bias=NMAX[:, i:i + 1], accum_out=Z[:, i:i + 1])
                last.then_inc(drained[7], 1)
                for c in range(PAIRS0):
                    g = c % 2
                    act.wait_ge(filled[g], fill("moe", g, b, c // 2))
                    if c >= 2:
                        act.wait_ge(drained[g], fill("moe", g, b, c // 2 - 1))
                    else:
                        act.wait_ge(drained[g], fill("moe", g, b, -1))
                    if c == PAIRS0 - 1:
                        act.activation(tanh_g[0:F0 % P, g, 0:S], PS[0:F0 % P, g, 0:S], ACT.Tanh, scale=0.5) \
                            .then_inc(tanh_ready, 1)
                    else:
                        act.activation(tanh_g[:, g, :], PS[:, g, :], ACT.Tanh, scale=0.5) \
                            .then_inc(tanh_ready, 1)
                    if c == 1:
                        evacuate("moe", "combine", b, 0, (CT[p][:, :], PS[0:3 * PART, 7, 0:P].bitcast(BF16)))
                    if b + 1 < NB:
                        if c == 2:
                            edge_gates(b + 1)
                        if FOLD_AT <= c < FOLD_AT + 4:
                            fold_out(b + 1, c - FOLD_AT)
                    if c == TURN_AT:
                        xt_out(fill_at("moe", "turn", b)[1], 1 - p)

            def latent_queries(b):
                for i in range(NH // 2):
                    evacuate("latent", "q", b, i, (qT1[b % 2][0:DC, 2 * i, :], PS[0:DC, i % 2, 0:S]),
                             (qT1[b % 2][0:DC, 2 * i + 1, :], PS[DC:P, i % 2, 0:S]))

            def max_out(b):
                evacuate("latent", "max", b, 0, (NMT, PS[0:NH, 7, 0:S]))

            def outputs_out(b, hp):
                if b and hp == 0:
                    bank, value = fill_at("latent", "y", b - 1)
                    act.wait_ge(filled[bank], value)
                if b * NH // 2 + hp >= 2:
                    act.wait_ge(divided, b * NH // 2 + hp - 1)
                evacuate("latent", "o", b, hp, (OT1[0:DC, hp, :], PS[0:DC, 6, 0:S]),
                         (OT1[DC:P, hp, :], PS[DC:P, 6, S:2 * S]),
                         (RD[0:DC, hp % 2, :], PS[DC:P, 6, 0:S]), (RD[DC:P, hp % 2, :], PS[0:DC, 6, S:2 * S]))

            latent_queries(0)
            xt_out(fill_at("latent", "turn", 0)[1], 1)
            max_out(0)
            latent_queries(1)
            for b in range(NB):
                for hp in range(NH // 2):
                    s = hp % 2
                    bank, value = fill_at("latent", "st", b, hp)
                    act.wait_ge(filled[bank], value)
                    if hp >= 2:
                        act.wait_ge(filled[6], fill_at("latent", "o", b, hp - 2)[1])
                    act.activation(probs[:, s, :, :], PS[:, bank:bank + 2, :], ACT.Exp).then_inc(drained[bank], 1)
                    if hp:
                        outputs_out(b, hp - 1)
                if b < NB - 1:
                    xt_out(fill_at("latent", "turn", b + 1)[1], b % 2)
                outputs_out(b, NH // 2 - 1)
                if b < NB - 1:
                    max_out(b + 1)
                if b + 2 < NB:
                    latent_queries(b + 2)

            def ternary(b, p, nb):
                for k in range(CH1):
                    m = min(P, H1 - k * P)
                    act.wait_ge(filled[k % 3], fill("ternary", k % 3, b, k // 3))
                    if k >= 2:
                        act.wait_ge(drained[(k - 2) % 3], fill("ternary", (k - 2) % 3, b, (k - 2) // 3))
                    else:
                        act.wait_ge(drained[(k + 1) % 3], fill("ternary", (k + 1) % 3, b, -1))
                    act.activation(tanh_g[0:m, k % 2, 0:S], PS[0:m, k % 3, 0:S], ACT.Tanh, scale=0.5) \
                        .then_inc(tanh1_ready, 1)
                xt_out(fill("ternary", 7, b, 0), 1 - p)
            pairs(act, ternary)

            def values_out(phase, b):
                for t in range(2):
                    evacuate(phase, "v", b, t, (VB[b % 2][:, t, :], PS[:, t, :]))

            def stacks_out(phase, b, n):
                for bank, what, _, _ in stacks(phase, b, n):
                    to = QS if what == "qs" else KS
                    evacuate(phase, what, b, n, (to[b % 2][0:ROWS, 2 * n:2 * n + 2, :], PS[0:ROWS, bank, :]
                                                 .rearrange("p (a s) -> p a s", a=2)))

            def job_turned(phase, b):
                evacuate(phase, "job_turn", b, 0, (XJ, PS[:, 7, :].rearrange("p (c s) -> p c s", c=2)))

            def job_exp(phase, b):
                act.wait_ge(nmax_ready, NB + job(phase, b)[2] + 1)
                for i in range(2):
                    last = act.activation(EX[:, i, 0:E3], LG[:, i, 0:E3], ACT.Exp, bias=NMAX[:, i:i + 1],
                                          accum_out=Z[:, i:i + 1])
                last.then_inc(exp_ready, 1)

            def job_mixed(phase, b):
                if job(phase, b)[0] == "lora":
                    evacuate(phase, "job_mixed", b, 0, (HWT[0:E2 * R2, :], PS[0:E2 * R2, 7, 0:S]))
                else:
                    evacuate(phase, "job_mixed", b, 0, (HWT[:, :], PS[:, 7, 0:S]), (WT[:, :], PS[0:E3, 7, S:2 * S]))

            def attention(phase):
                values_out(phase, 0)
                for n in range(NH // 2):
                    stacks_out(phase, 0, n)
                xt_out(fill_at(phase, "turn", 0)[1], 1)
                values_out(phase, 1)
                n = 512 if phase == "grouped" else 384
                for b in range(NB):
                    ahead = b < NB - 1
                    half = 4 * b if phase == "grouped" else 4 * b + 4 * NB
                    for hp in range(NH // 2):
                        s, g = hp % 2, hp // 2
                        if job(phase, b):
                            if hp == JOB_TURN:
                                job_turned(phase, b)
                            if hp == JOB_DOWN + 2:
                                job_exp(phase, b)
                        if g and s == 0:
                            act.wait_ge(probs_used, half + g)
                        elif g:
                            act.wait_ge(filled[6], fill_at(phase, "o", b, g - 1)[1])
                        for e in range(2):
                            bank, value = fill_at(phase, "st", b, 2 * hp + e)
                            act.wait_ge(filled[bank], value)
                            act.activation(probs[:, s, e, 0:n], PS[:, bank, 0:n], ACT.Exp, scale=0.25) \
                                .then_inc(drained[bank], 1)
                        if ahead:
                            stacks_out(phase, b + 1, hp)
                        if s == 0 and g:
                            evacuate(phase, "o", b, g - 1, (OTR[:, g - 1, :], PS[:, 6, 0:S]))
                        if job(phase, b) and hp == JOB_MIXED:
                            job_mixed(phase, b)
                    evacuate(phase, "o", b, 3, (OTR[:, 3, :], PS[:, 6, 0:S]))
                    if turns_next(phase, b):
                        xt_out(fill_at(phase, "turn", b + 1)[1], b % 2)
                    if b + 2 < NB:
                        values_out(phase, b + 2)

            attention("grouped")

            attention("causal")
            job_turned("causal", NB)
            job_exp("causal", NB)
            job_mixed("causal", NB)

        @block.vector
        def _(dve):
            done = [0, 0]

            parts = [0]

            def part():
                k = parts[0] % 4
                parts[0] += 1
                dve.memset(carrier[:, k:k + 1], 0.0)

            def start(at_):
                done[0], done[1] = at_, 0

            def link(ins):
                ins.then_inc(v_step, 1)
                done[1] += 1
                dve.wait_ge(v_step, done[0] + done[1])

            def loop(name, body, count):
                base = v_total[0]
                def one(b, p, nb):
                    start(base + b * count)
                    body(b, p, nb)
                    assert done[1] == count, (name, done[1])
                pairs(dve, one)
                v_total[0] = base + NB * count
                start(v_total[0])

            v_total = [0]

            def stats(b):
                link(dve.bn_stats(BN[:, 0, :], X[:, b * 2, :]))
                link(dve.bn_stats(BN[:, 1, :], X[:, b * 2 + 1, :]))
                part()
                dve.bn_aggr(MV[:, 0, :], BN[:, 0, :])
                dve.bn_aggr(MV[:, 1, :], BN[:, 1, :]).then_inc(mv_ready, 1)

            def normalise(n, b, used):
                dve.wait_ge(rstd_ready, n + 1)
                if used is not None:
                    dve.wait_ge(filled[7], used)
                for i in range(2):
                    last = dve.tensor_scalar(XN[:, i, :], X[:, b * 2 + i, :], MV[:, i, 0:1], RS[:, i:i + 1],
                                             ALU.subtract, ALU.mult)
                last.then_inc(xn_ready, 1)

            def add_residual(phase, b, gate):
                dve.wait_ge(filled[6], fill(phase, 6, b, 0))
                xb = X[:, bass.ds(b * 2, 2), :]
                dve.scalar_tensor_tensor(xb, PS[:, 6, :].rearrange("p (a d) -> p a d", a=2), gate, xb,
                                         ALU.mult, ALU.add).then_inc(drained[6], 1)
                dve.wait_ge(drained[6], fill(phase, 6, b, 0))

            for dst, value in ((neg_half[:, :], -0.5), (eps[:, :], 1e-5), (ones[:, :], 1.0),
                               (ctxT[DC:DC + 1, :], 1.0), (KR[0][DC:DC + 1, :], 1.0),
                               (KR[1][DC:DC + 1, :], 1.0), (VV[0][:, :, :], 1.0), (VV[1][:, :, :], 1.0),
                               (SC[:, :, :], LOW), (LG[:, :, :], LOW), (CM[:, :, :], 0.5),
                               (HW[:, :, :], 0.0), (C3[:, :, :], 0.0)):
                last = dve.memset(dst, value)
            last.then_inc(consts_set, 1)

            rounds = (TOPK - 1) // 8

            def graph_round(b, r):
                if r == 0:
                    dve.wait_ge(sim_scaled, b + 1)
                cur = sim[b] if r == 0 else work
                for i in range(2):
                    last = dve.max(g8[:, i, :], cur[:, i, :])
                link(last)
                if r < rounds:
                    for i in range(2):
                        last = dve.match_replace(work[:, i, :], g8[:, i, :], cur[:, i, :], LOW)
                    link(last)

            def graph_mask(b):
                dve.wait_ge(sg_ready, b + 1)
                link(dve.tensor_scalar(sg, sg, 1.0, None, ALU.add))
                kth = (TOPK - 1) % 8
                for i in range(2):
                    last = dve.scalar_tensor_tensor(AM[:, i, :], sim[b][:, i, :], g8[:, i, kth:kth + 1],
                                                    sg[:, i, :], ALU.is_ge, ALU.mult)
                last.then_inc(masked, 1)
                dve.wait_ge(masked, b + 1)

            def graph_norm(b):
                n = NORMALISED.index(("graph", b))
                normalise(n, b, fill_at("moe", "turn", b - 2)[1] if b else None)
                dve.wait_ge(xn_ready, n + 1)
                xb = X[:, 2 * b:2 * b + 2, :]
                link(dve.scalar_tensor_tensor(xb, XN[:, :, :], CA[:, 0:1], xb, ALU.mult, ALU.add))

            def graph_add(b):
                bank, value = fill_at("moe", "graph", b)
                dve.wait_ge(filled[bank], value)
                dve.tensor_tensor(S2, AM, PS[:, bank, :].rearrange("p (a s) -> p a s", a=2), ALU.add) \
                    .then_inc(drained[bank], 1)
                dve.wait_ge(drained[bank], value)
                xb = X[:, 2 * b:2 * b + 2, :]
                dve.scalar_tensor_tensor(xb, S2, CA[:, 1:2], xb, ALU.mult, ALU.add).then_inc(graph_added, 1)
                dve.wait_ge(graph_added, b + 1)

            start(0)
            for r in range(rounds):
                graph_round(0, r)
            dve.wait_ge(gates_ready, 1)
            link(dve.tensor_scalar(CA[:, 2:3], TG[:, 8:9], -0.5, 0.5, ALU.mult, ALU.add))
            link(dve.tensor_tensor(CA[:, 0:1], CA[:, 2:3], TG[:, 0:1], ALU.mult))
            link(dve.tensor_scalar(CA[:, 3:4], TG[:, 8:9], 0.125, 0.125, ALU.mult, ALU.add))
            link(dve.tensor_tensor(CA[:, 1:2], CA[:, 3:4], TG[:, 0:1], ALU.mult))
            link(dve.tensor_scalar(CA[:, 2:3], TG[:, 5:6], 0.5, None, ALU.mult))
            dve.wait_ge(first_loaded, 16 * N_FIRST)
            stats(0)
            graph_round(0, rounds)
            graph_mask(0)
            graph_norm(0)
            graph_add(0)
            stats(0)
            normalise(1, 0, None)
            dve.wait_ge(consts_set, 1)

            def weight_sums():
                dve.wait_ge(mlp_loaded, 16 * 3)
                link(dve.memset(absum[:, :], 0.0))
                for k, w in enumerate((w12[:, 0:2, :], w12[:, 2:4, :], w3[:, 0:5, :])):
                    dve.tensor_reduce(absum[:, k:k + 1], w.rearrange("p a b -> p (a b)"), AX, ALU.add,
                                      apply_absolute_value=True)
                dve.tensor_reduce(absum[0:H1 - 5 * P, 3:4], w3[0:H1 - 5 * P, 5, :], AX, ALU.add,
                                  apply_absolute_value=True).then_inc(abs_ready, 1)

            def thresholds():
                bank, value = fill_at("moe", "abs", 0)
                dve.wait_ge(filled[bank], value)
                dve.tensor_copy(mean_w[:, :], PS[:, bank, 0:4]).then_inc(drained[bank], 1)
                dve.wait_ge(drained[bank], value)
                link(dve.tensor_tensor(mean_w[:, 2:3], mean_w[:, 2:3], mean_w[:, 3:4], ALU.add))
                link(dve.tensor_scalar(mean_w[:, 0:3], mean_w[:, 0:3], 1.0 / (H1 * D), 1e-8, ALU.mult, ALU.add))
                dve.tensor_scalar(thr[:, 0, :], mean_w[:, 0:3], 0.5, None, ALU.mult)
                dve.tensor_scalar(thr[:, 1, :], mean_w[:, 0:3], -0.5, None, ALU.mult).then_inc(thr_ready, 1)

            for b in range(NB):
                bank, value = fill_at("moe", "router", b)
                dve.wait_ge(filled[bank], value)
                dve.tensor_reduce(NMAX[:, :], PS[:, 7, 0:2 * E0].rearrange("p (a e) -> p a e", a=2), AX, ALU.max,
                                  negate=True).then_inc(nmax_ready, 1)
                dve.wait_ge(drained[bank], value)
                link(dve.reciprocal(RZ[:, :], Z[:, :]))
                for i in range(2):
                    last = dve.tensor_scalar(SC[:, i, 0:E0], EX[:, i, :], RZ[:, i:i + 1], None, ALU.mult)
                link(last)
                for i in range(2):
                    last = dve.max(T8[:, i, :], SC[:, i, 0:E0])
                link(last)
                link(dve.memset(T8[:, :, K0:8], LOW))
                for i in range(2):
                    last = dve.match_replace(REP[:, i, :], T8[:, i, :], SC[:, i, :], 0.0)
                link(last)
                link(dve.tensor_tensor(CM[:, :, 0:E0], SC[:, :, 0:E0], REP[:, :, 0:E0], ALU.subtract))
                link(dve.tensor_reduce(SU[:, :], CM[:, :, 0:E0], AX, ALU.add))
                link(dve.tensor_scalar(SU[:, :], SU[:, :], 1e-20, None, ALU.add))
                link(dve.reciprocal(SU[:, :], SU[:, :]))
                for i in range(2):
                    last = dve.tensor_scalar(CM[:, i, 0:E0], CM[:, i, 0:E0], SU[:, i:i + 1], 0.5,
                                             ALU.mult, ALU.mult)
                link(last)
                link(dve.tensor_copy(C3[:, :, 0:PART], CM[:, :, :]))
                link(dve.tensor_tensor(REP[:, :, 0:PART], CM[:, :, :], C3[:, :, 0:PART], ALU.subtract))
                link(dve.tensor_copy(C3[:, :, PART:2 * PART], REP[:, :, 0:PART]))
                dve.tensor_tensor(C3[:, :, 2 * PART:3 * PART], REP[:, :, 0:PART], C3[:, :, PART:2 * PART],
                                  ALU.subtract).then_inc(comb_ready, 1)
                for c in range(PAIRS0):
                    g, m, n = c % 2, P, 512
                    if c == PAIRS0 - 1:
                        m, n = F0 % P, S
                    dve.wait_ge(tanh_ready, b * PAIRS0 + c + 1)
                    dve.scalar_tensor_tensor(gated[0:m, 0:n], tanh_g[0:m, g, 0:n], 1.0, PS[0:m, g, 0:n],
                                             ALU.add, ALU.mult).then_inc(drained[g], 1)
                    dve.wait_ge(drained[g], fill("moe", g, b, c // 2))
                    dve.wait_ge(filled[2 + g], fill("moe", 2 + g, b, c // 2))
                    dve.tensor_tensor(hidden[0:m, 0:n], gated[0:m, 0:n], PS[0:m, 2 + g, 0:n], ALU.mult) \
                        .then_inc(drained[2 + g], 1)
                    dve.wait_ge(drained[2 + g], fill("moe", 2 + g, b, c // 2))
                    dve.wait_ge(filled[4 + g], fill("moe", 4 + g, b, c // 2))
                    if c >= 2:
                        dve.wait_ge(h_used, b * (PAIRS0 - 1) + c - 1)
                    dve.tensor_tensor(H[0:m, g, :, :].rearrange("p a s -> p (a s)")[:, 0:n], hidden[0:m, 0:n],
                                      PS[0:m, 4 + g, 0:n], ALU.mult).then_inc(drained[4 + g], 1)
                    if b + 1 < NB:
                        if c == 0:
                            stats(b + 1)
                        for r in ROUNDS_AT.get(c, ()):
                            graph_round(b + 1, r)
                        if c == 4:
                            graph_norm(b + 1)
                        if c == 7:
                            graph_mask(b + 1)
                        if c == GRAPH_AT - 1:
                            graph_add(b + 1)
                    else:
                        if c == 2:
                            weight_sums()
                        if c == GRAPH_AT - 1:
                            thresholds()
                    if c == GRAPH_AT - 1:
                        stats((b + 1) % NB)
                    if c == GRAPH_AT:
                        normalise(after_moe(b), (b + 1) % NB,
                                  fill_at("moe", "turn", b - 1)[1])
                add_residual("moe", b, TG[:, 4:5])
            v_total[0] = done[0] + done[1]

            def sequence():
                start(v_total[0])

            def sequence_end():
                v_total[0] = done[0] + done[1]
                start(v_total[0])

            def prepare_next(phase, b, counted=False):
                nb = (b + 1) % NB
                if not counted:
                    stats(nb)
                at_ = [n + 1 for n, key in enumerate(BANK_FILLS[7])
                       if key == (phase, "turn", b - 1, 0)] or [fills_before(phase, 7)]
                if phase == "latent":
                    normalise(next_no(phase, b), nb, at_[0])
                    return
                if b and job(phase, b - 1):
                    at_ = [fill_at(phase, "job_turn", b - 1)[1]]
                n = NORMALISED.index((phase, b + 1) if b + 1 < NB else ("causal", 0))
                normalise(n, nb, at_[0])

            def output(phase, b, gate):
                bank, value = fill_at(phase, "y", b)
                dve.wait_ge(filled[bank], value)
                xb = X[:, 2 * b:2 * b + 2, :]
                dve.scalar_tensor_tensor(xb, PS[:, bank, :].rearrange("p (a d) -> p a d", a=2), gate, xb,
                                         ALU.mult, ALU.add).then_inc(drained[bank], 1)
                dve.wait_ge(drained[bank], value)

            def maximum(phase, b, h):
                bank, value = fill_at(phase, "s", b, h)
                if h == 0:
                    dve.wait_ge(filled[7], fill_at(phase, "max", b - 1)[1] if b else fills_before(phase, 7))
                dve.wait_ge(filled[bank], value)
                if phase == "causal":
                    dve.tensor_reduce(NM[:, 0, h:h + 1], PS[:, bank, 0:P], AX, ALU.max, negate=True)
                    dve.tensor_reduce(NM[:, 1, h:h + 1], PS[:, bank, S:2 * S], AX, ALU.max,
                                      negate=True).then_inc(drained[bank], 1)
                else:
                    dve.tensor_reduce(NM[:, :, h], PS[:, bank, :].rearrange("p (a s) -> p a s", a=2), AX,
                                      ALU.max, negate=True).then_inc(drained[bank], 1)

            def divide(b, hp):
                bank, value = fill_at("latent", "o", b, hp)
                dve.wait_ge(drained[bank], value)
                link(dve.reciprocal(RD[:, hp % 2, :], RD[:, hp % 2, :]))
                dve.tensor_tensor(OT1[:, hp, :], OT1[:, hp, :], RD[:, hp % 2, :], ALU.mult).then_inc(divided, 1)

            sequence()
            prepare_next("latent", 0)
            for h in range(NH):
                maximum("latent", 0, h)
            for b in range(NB):
                for hp in range(NH // 2):
                    if hp:
                        divide(b, hp - 1)
                    if b < NB - 1:
                        maximum("latent", b + 1, 2 * hp)
                        maximum("latent", b + 1, 2 * hp + 1)
                        if hp == 4:
                            prepare_next("latent", b + 1)
                divide(b, NH // 2 - 1)
                output("latent", b, TG[:, 1:2])
            sequence_end()

            def ternary(b, p, nb):
                dve.wait_ge(filled[6], fill("ternary", 6, b, -1))
                for k in range(CH1):
                    if k == 1:
                        stats(nb)
                    if k == 3:
                        normalise(next_no("ternary", b), nb, fill("ternary", 7, b, -1))
                    m = min(P, H1 - k * P)
                    dve.wait_ge(tanh1_ready, b * CH1 + k + 1)
                    dve.scalar_tensor_tensor(HD[0:m, k, :], tanh_g[0:m, k % 2, 0:S], 1.0,
                                             PS[0:m, k % 3, S:2 * S], ALU.add, ALU.mult) \
                        .then_inc(drained[k % 3], 1)
                add_residual("ternary", b, CA[:, 2:3])
            loop("ternary", ternary, 2)

            dve.wait_ge(late_loaded, LATE)

            def split(parts, source, rest_, ready, n, bank=None, value=None):
                link(dve.tensor_copy(parts[0], source))
                taken = dve.tensor_tensor(rest_, source, parts[0], ALU.subtract)
                if bank is None:
                    link(taken)
                else:
                    taken.then_inc(drained[bank], 1)
                    dve.wait_ge(drained[bank], value)
                link(dve.tensor_copy(parts[1], rest_))
                dve.tensor_tensor(parts[2], rest_, parts[1], ALU.subtract).then_inc(ready, 1)
                dve.wait_ge(ready, n)

            def split_operands(phase, b):
                n = 2 * b + NB if phase == "causal" else b
                if phase == "grouped":
                    bank, value = (7, fills_before(phase, 7)) if b == 0 else fill_at(phase, "turn", b - 1)
                    dve.wait_ge(drained[bank], value)
                    dve.wait_ge(keys_ready, 4)
                    split([QP[:, k, :, :] for k in range(3)], XT[b % 2][:, :, :], rest, parts_ready, n + 1)
                    return
                for k, (what, parts) in enumerate((("q", QP), ("k", KP))):
                    bank, value = fill_at(phase, what, b)
                    dve.wait_ge(filled[bank], value)
                    split([parts[:, i, :, :] for i in range(3)], PS[:, bank, :].rearrange("p (g s) -> p g s", g=2),
                          rest, parts_ready, n + k + 1, bank, value)

            def split_max(phase, b):
                bank, value = fill_at(phase, "max", b)
                dve.wait_ge(filled[bank], value)
                split([NM3[:, k, :] for k in range(3)], PS[0:NH, bank, 0:S], RM[:, :], max_split,
                      b + 1 + (NB if phase == "causal" else 0), bank, value)

            def over_denominator(phase, b, g):
                bank, value = fill_at(phase, "den", b, g)
                dve.wait_ge(filled[bank], value)
                dve.reciprocal(RD[:, g % 2, :], PS[:, bank, 0:S]).then_inc(drained[bank], 1)
                dve.wait_ge(drained[bank], value)
                dve.tensor_tensor(OTN[:, g, :], OTR[:, g, :], RD[:, g % 2, :], ALU.mult).then_inc(norm_ready, 1)

            def job_norm(phase, b):
                kind, of, _ = job(phase, b)
                before = [n + 1 for n, key in enumerate(BANK_FILLS[7])
                          if n < fill_at(phase, "job_turn", b)[1] and key[1] in ("turn", "job_turn")]
                normalise(NORMALISED.index((kind, of)), of, before[-1] - (before[-1] == fill_at(
                    phase, "job_turn", b)[1]))

            def job_down(phase, b):
                kind, _, number = job(phase, b)
                bank, value = fill_at(phase, "job_down", b)
                dve.wait_ge(filled[bank], value)
                n = E2 * R2 + E2 if kind == "lora" else E3 * R3 + E3
                dve.tensor_copy(LR[:, :, 0:n], PS[:, bank, 0:2 * n].rearrange("p (a n) -> p a n", a=2)) \
                    .then_inc(drained[bank], 1)
                dve.wait_ge(drained[bank], value)
                link(dve.tensor_scalar(LG[:, :, 0:8], LR[:, :, n - 8:n], 0.0 if kind == "lora" else BONUS, None,
                                       ALU.add))
                dve.tensor_reduce(NMAX[:, :], LG[:, :, 0:8], AX, ALU.max, negate=True).then_inc(nmax_ready, 1)
                dve.wait_ge(nmax_ready, NB + number + 1)

            def job_choice(phase, b):
                kind, _, number = job(phase, b)
                dve.wait_ge(exp_ready, number + 1)
                if kind == "adapter":
                    link(dve.reciprocal(RZ[:, :], Z[:, :]))
                    for i in range(2):
                        last = dve.tensor_scalar(LG[:, i, 0:E3], EX[:, i, 0:E3], RZ[:, i:i + 1], None, ALU.mult)
                    link(last)
                for i in range(2):
                    last = dve.max(T8[:, i, :], LG[:, i, 0:8])
                link(last)
                link(dve.memset(T8[:, :, 2:8], LOW))
                for i in range(2):
                    last = dve.match_replace(REP[:, i, 0:14], T8[:, i, :], LG[:, i, :],
                                             -3.3e38 if kind == "lora" else 0.0)
                link(last)
                if kind == "lora":
                    link(dve.tensor_tensor(SC[:, :, 0:8], LG[:, :, 0:8], REP[:, :, 0:8], ALU.not_equal))
                    link(dve.tensor_tensor(SC[:, :, 0:8], SC[:, :, 0:8], EX[:, :, 0:8], ALU.mult))
                else:
                    link(dve.tensor_tensor(SC[:, :, 0:8], LG[:, :, 0:8], REP[:, :, 0:8], ALU.subtract))

            def job_weights(phase, b):
                kind = job(phase, b)[0]
                link(dve.tensor_reduce(SU[:, :], SC[:, :, 0:8], AX, ALU.add))
                link(dve.reciprocal(SU[:, :], SU[:, :]))
                for i in range(2):
                    last = dve.tensor_scalar(CM[:, i, 0:8], SC[:, i, 0:8], SU[:, i:i + 1],
                                             2.0 if kind == "lora" else 1.0, ALU.mult, ALU.mult)
                link(last)
                for i in range(2):
                    if kind == "lora":
                        w = CM[:, i, 0:E2].unsqueeze(2).to_broadcast([P, E2, R2])
                        last = dve.tensor_tensor(HW[:, i, 0:E2 * R2].rearrange("p (e r) -> p e r", e=E2),
                                                 LR[:, i, 0:E2 * R2].rearrange("p (e r) -> p e r", e=E2), w,
                                                 ALU.mult)
                    else:
                        w = CM[:, i, 0:E3].unsqueeze(2).to_broadcast([P, E3, R3])
                        last = dve.scalar_tensor_tensor(HW[:, i, :].rearrange("p (e r) -> p e r", e=E3),
                                                        LR[:, i, 0:E3 * R3].rearrange("p (e r) -> p e r", e=E3),
                                                        0.0, w, ALU.max, ALU.mult)
                last.then_inc(weighted, 1)

            def job_output(phase, b):
                kind, of, _ = job(phase, b)
                bank, value = fill_at(phase, "job_y", b)
                dve.wait_ge(filled[bank], value)
                xb = X[:, 2 * of:2 * of + 2, :]
                dve.scalar_tensor_tensor(xb, PS[:, bank, :].rearrange("p (a d) -> p a d", a=2),
                                         TG[:, 6:7] if kind == "lora" else TG[:, 7:8], xb,
                                         ALU.mult, ALU.add).then_inc(drained[bank], 1)
                dve.wait_ge(drained[bank], value)

            JOB_STEPS = {0: job_norm, JOB_DOWN + 1: job_down, JOB_CHOICE: job_choice, JOB_WEIGHTS: job_weights}

            def attention(phase, gate):
                sequence()
                split_operands(phase, 0)
                prepare_next(phase, 0)
                for h in range(NH):
                    maximum(phase, 0, h)
                split_max(phase, 0)
                split_operands(phase, 1)
                for b in range(NB):
                    ahead = b < NB - 1
                    work_on = JOB_STEPS if job(phase, b) else {}
                    if work_on:
                        stats(job(phase, b)[1])
                    for hp in range(NH // 2 + 1):
                        if ahead and hp:
                            maximum(phase, b + 1, 2 * hp - 2)
                            maximum(phase, b + 1, 2 * hp - 1)
                        if hp in (4, 6):
                            over_denominator(phase, b, (hp - 4) // 2)
                        if hp in work_on:
                            work_on[hp](phase, b)
                        if turns_next(phase, b):
                            if hp == 4:
                                stats((b + 2) % NB)
                            if hp == 7:
                                prepare_next(phase, b + 1, True)
                    if work_on:
                        job_output(phase, b)
                    if ahead:
                        split_max(phase, b + 1)
                    over_denominator(phase, b, 2)
                    over_denominator(phase, b, 3)
                    if b + 2 < NB:
                        split_operands(phase, b + 2)
                    output(phase, b, gate)
                sequence_end()

            attention("grouped", TG[:, 2:3])
            attention("causal", TG[:, 3:4])
            sequence()
            stats(NB - 1)
            for step in sorted(JOB_STEPS):
                JOB_STEPS[step]("causal", NB)
            job_output("causal", NB)
            sequence_end()

        @block.tensor
        def _(pe):
            mm = pe.matmul
            pe.wait_ge(consts_set, 1)
            for k in range(8):
                pe.sem_inc(filled[k], 1)
                pe.sem_inc(drained[k], 1)
            pe.wait_ge(context_loaded, 16 * 2)
            for n in range(2):
                for k in range(2):
                    mm(PS[0:DC, 4 + 2 * k + n, :], wqk0[:, k, :], ctxT[0:DC, n * 512:(n + 1) * 512],
                       start=True, stop=True).then_inc(qk_filled, 1)
                pe.wait_ge(qk_copied, 2 * n + 2)
                for b in (2 * n, 2 * n + 1):
                    for i in range(2):
                        last = mm(PS[:, b, i * S:(i + 1) * S], qk0[:, 0, (2 * b + i) * P:(2 * b + i + 1) * P],
                                  qk0[:, 1, b * S:(b + 1) * S], start=True, stop=True)
                    last.then_inc(sim_filled, 1)
            pe.wait_ge(first_loaded, 16 * N_FIRST)

            def begin(phase, what, b, k=0):
                bank, value = fill_at(phase, what, b, k)
                pe.wait_ge(drained[bank], value - 1)
                return bank

            def fold(n, k):
                wq1, wkq1T, wqr1T, wkr1T, wkv1, wo1T = fold_w[n % 2]
                if k == 0:
                    pe.wait_ge(fold_loaded[n % 2], 16 * 6 * (n // 2 + 1))
                begin("moe", "fold", n, k)
                for h in range(4):
                    if k == 3:
                        q = DC * (h % 2)
                        last = mm(PS[q:q + DC, 7, (h // 2) * S:(h // 2 + 1) * S], wkv1[:, h, :],
                                  wo1T[:, h, :], start=True, stop=True)
                        continue
                    for c in range(2):
                        if k == 0:
                            last = mm(PS[0:96, 7, (h * 2 + c) * DC:(h * 2 + c + 1) * DC],
                                      wqr1T[:, h, c * 96:(c + 1) * 96], wkr1T[:, h, :], start=True, stop=True)
                        elif k == 1:
                            last = mm(PS[:, 7, h * DC:(h + 1) * DC], wkq1T[:, c, h, :], fold_b[:, h, c, :],
                                      start=c == 0, stop=c == 1)
                        else:
                            last = mm(PS[:, 7, c * S + h * DC:c * S + (h + 1) * DC],
                                      wq1[:, h, c * P:(c + 1) * P], fold_c[:, h, :], start=True, stop=True)
                last.then_inc(filled[7], 1)

            def graph_turn(b):
                pe.wait_ge(masked, b + 1)
                bank = begin("moe", "graph", b)
                for m in range(2):
                    for i in range(2):
                        last = pe.transpose(PS[:, bank, m * S + i * P:m * S + (i + 1) * P],
                                            AM[:, i, m * P:(m + 1) * P], ident[:, :])
                last.then_inc(filled[bank], 1)

            def turn(n, drain):
                pe.wait_ge(xn_ready, n + 1)
                pe.wait_ge(drained[7], drain)
                for c in range(2):
                    for i in range(2):
                        last = pe.transpose(PS[:, 7, c * S + i * P:c * S + (i + 1) * P],
                                            XN[:, i, c * P:(c + 1) * P], ident[:, :])
                last.then_inc(filled[7], 1)

            def free(phase, k, b, n):
                pe.wait_ge(drained[k], fill(phase, k, b, n - 1))

            for k in range(3):
                fold(0, k)
            graph_turn(0)
            fold(0, 3)
            turn(1, fill_at("moe", "turn", -1)[1] - 1)
            pe.wait_ge(sim_scaled, NB)
            pe.wait_ge(router_loaded, 16 * 2)
            pe.wait_ge(ident_ready, 1)

            for b in range(NB):
                p = b % 2
                begin("moe", "router", b)
                for i in range(2):
                    for c in range(2):
                        last = mm(PS[:, 7, i * E0:(i + 1) * E0], XT[p][:, c, i * P:(i + 1) * P], W_r[:, c, :],
                                  start=c == 0, stop=c == 1)
                last.then_inc(filled[7], 1)

                def chunks(c):
                    for f in range(2 * c, min(2 * c + 2, CH0)):
                        yield f, f % 2, f * P, min(P, F0 - f * P)

                def up(c):
                    for first, w in ((0, W_g), (2, W_u)):
                        k = first + c % 2
                        free("moe", k, b, c // 2)
                        for f, e, f0, m in chunks(c):
                            for d in range(2):
                                last = mm(PS[0:m, k, e * S:(e + 1) * S], w[:, d, f0:f0 + m], XT[p][:, d, :],
                                          start=d == 0, stop=d == 1)
                        last.then_inc(filled[k], 1)

                def weights(c):
                    k = 4 + c % 2
                    free("moe", k, b, c // 2)
                    for f, e, f0, m in chunks(c):
                        last = mm(PS[0:m, k, e * S:(e + 1) * S], sel_e[:, f0:f0 + m], CT[p][:, :],
                                  start=True, stop=True)
                    last.then_inc(filled[k], 1)

                def down(c):
                    k = 4 + c % 2
                    pe.wait_ge(drained[k], fill("moe", k, b, c // 2))
                    if c == 0:
                        pe.wait_ge(down_loaded, 16 * 2)
                        free("moe", 6, b, 0)
                    for f, e, f0, m in chunks(c):
                        for i in range(2):
                            last = mm(PS[:, 6, i * D:(i + 1) * D], H[0:m, c % 2, e, i * P:(i + 1) * P],
                                      W_d[0:m, f, :], start=f == 0 and i == 0, stop=f == CH0 - 1,
                                      skip_group_check=True)
                    last.then_inc(h_used if c < PAIRS0 - 1 else filled[6], 1)

                for c in range(PAIRS0):
                    if b == 0 and c % 4 == 0 and c < 12:
                        pe.wait_ge(expert_loaded[c // 4], 16 * 2)
                    up(c)
                    if c == 1:
                        pe.wait_ge(comb_ready, b + 1)
                        begin("moe", "combine", b)
                        turned_w = PS[:, 7, 0:P].bitcast(BF16)
                        for i in range(2):
                            last = pe.transpose(turned_w[:, i * P:(i + 1) * P], C3[:, i, :], identb[:, :])
                        last.then_inc(filled[7], 1)
                        bank, value = fill_at("moe", "combine", b)
                        pe.wait_ge(drained[bank], value)
                    if c >= 1:
                        weights(c - 1)
                    if c >= 2:
                        down(c - 2)
                    if b + 1 < NB and FOLD_AT <= c < FOLD_AT + 4:
                        fold(b + 1, c - FOLD_AT)
                    if c == GRAPH_AT and b + 1 < NB:
                        graph_turn(b + 1)
                    elif c == GRAPH_AT:
                        pe.wait_ge(abs_ready, 1)
                        bank = begin("moe", "abs", 0)
                        mm(PS[:, bank, 0:4], ones[:, :], absum[:, :], start=True, stop=True) \
                            .then_inc(filled[bank], 1)
                    if c == TURN_AT:
                        turn(after_moe(b), fill_at("moe", "turn", b)[1] - 1)
                weights(PAIRS0 - 1)
                down(PAIRS0 - 2)
                down(PAIRS0 - 1)

            def turned_max(phase, b):
                for h in (NH - 2, NH - 1):
                    bank, value = fill_at(phase, "s", b, h)
                    pe.wait_ge(drained[bank], value)
                bank = begin(phase, "max", b)
                for i in range(2):
                    last = pe.transpose(PS[0:NH, bank, i * P:(i + 1) * P], NM[:, i, :], ident[:, :])
                last.then_inc(filled[bank], 1)

            def turned_next(phase, b):
                bank, value = fill_at(phase, "turn", b)
                if phase == "latent":
                    n = next_no(phase, b)
                else:
                    n = NORMALISED.index((phase, b + 1) if b + 1 < NB else ("causal", 0))
                turn(n, value - 1)

            def xt_there(phase, b):
                if b == 0:
                    pe.wait_ge(drained[7], fills_before(phase, 7))
                else:
                    pe.wait_ge(drained[7], fill_at(phase, "turn", b - 1)[1])

            def latent_queries(b):
                xt_there("latent", b)
                for i in range(NH // 2):
                    bank = begin("latent", "q", b, i)
                    for c in range(2):
                        last = mm(PS[:, bank, 0:S], NW[:, c, i * P:(i + 1) * P], XT[b % 2][:, c, :],
                                  start=c == 0, stop=c == 1)
                    last.then_inc(filled[bank], 1)

            def latent_scores(b, h):
                if h == 0:
                    pe.wait_ge(kv_ready, b * 4 + 4)
                    for i in (NH // 2 - 2, NH // 2 - 1):
                        bank, value = fill_at("latent", "q", b, i)
                        pe.wait_ge(drained[bank], value)
                bank = begin("latent", "s", b, h)
                for i in range(2):
                    last = mm(PS[:, bank, i * S:(i + 1) * S], qT1[b % 2][0:DC, h, i * P:(i + 1) * P],
                              KR[b % 2][0:DC, :], start=True, stop=True)
                last.then_inc(filled[bank], 1)

            def latent_exponents(b, hp):
                bank = begin("latent", "st", b, hp)
                for e in range(2):
                    for t in range(2):
                        last = mm(PS[:, bank + e, t * S:(t + 1) * S], KR[b % 2][:, t * P:(t + 1) * P],
                                  qT1[b % 2][:, 2 * hp + e, :], start=True, stop=True)
                last.then_inc(filled[bank], 1)

            def latent_values(b, hp):
                s = hp % 2
                bank, value = fill_at("latent", "st", b, hp)
                pe.wait_ge(drained[bank], value)
                bank = begin("latent", "o", b, hp)
                for e in range(2):
                    v0 = DC * (1 - e)
                    for t in range(2):
                        last = mm(PS[:, bank, e * S:(e + 1) * S], VV[b % 2][:, t, v0:v0 + P],
                                  probs[:, s, e, t * S:(t + 1) * S], start=t == 0, stop=t == 1)
                last.then_inc(filled[bank], 1)

            latent_queries(0)
            for h in range(NH):
                latent_scores(0, h)
            turned_next("latent", 0)
            turned_max("latent", 0)
            latent_queries(1)
            for b in range(NB):
                ahead = b < NB - 1
                pe.wait_ge(max_placed, (b + 1) * 16)
                for hp in range(NH // 2 + 1):
                    if hp < NH // 2:
                        latent_exponents(b, hp)
                    if hp:
                        latent_values(b, hp - 1)
                    if ahead and hp < NH // 2:
                        latent_scores(b + 1, 2 * hp)
                        latent_scores(b + 1, 2 * hp + 1)
                    if ahead and hp == 7:
                        turned_next("latent", b + 1)
                if ahead:
                    turned_max("latent", b + 1)
                if b + 2 < NB:
                    latent_queries(b + 2)
                bank = begin("latent", "y", b)
                for hp in range(NH // 2):
                    pe.wait_ge(divided, b * NH // 2 + hp + 1)
                    for i in range(2):
                        last = mm(PS[:, bank, i * D:(i + 1) * D], OT1[:, hp, i * P:(i + 1) * P], PM[:, hp, :],
                                  start=hp == 0 and i == 0, stop=hp == NH // 2 - 1, skip_group_check=True)
                last.then_inc(filled[bank], 1)

            pe.wait_ge(ternary_ready, 12)

            def ternary(b, p, nb):
                free("ternary", 7, b, 0)

                def down(k):
                    m = min(P, H1 - k * P)
                    pe.wait_ge(drained[k % 3], fill("ternary", k % 3, b, k // 3))
                    if k == 0:
                        free("ternary", 6, b, 0)
                    for i in range(2):
                        last = mm(PS[:, 6, i * D:(i + 1) * D], HD[0:m, k, i * P:(i + 1) * P], w3[0:m, k, :],
                                  start=k == 0 and i == 0, stop=k == CH1 - 1, skip_group_check=True)
                    if k == CH1 - 1:
                        last.then_inc(filled[6], 1)

                for k in range(CH1):
                    m = min(P, H1 - k * P)
                    free("ternary", k % 3, b, k // 3)
                    for w in range(2):
                        for c in range(2):
                            last = mm(PS[0:m, k % 3, w * S:(w + 1) * S], w12[:, 2 * w + c, k * P:k * P + m],
                                      XT[p][:, c, :], start=c == 0, stop=c == 1)
                    last.then_inc(filled[k % 3], 1)
                    if k >= 1:
                        down(k - 1)
                turn(next_no("ternary", b), fill("ternary", 7, b, -1))
                down(CH1 - 1)
            pairs(pe, ternary)
            pe.wait_ge(late_loaded, LATE)

            def attention(phase):
                wv, wo = (wv_2, wo_2) if phase == "grouped" else (wv_3, wo_3)
                causal = phase == "causal"
                key_heads = KEY_HEADS[phase]

                def operands(b):
                    context = ctxT[:, b * S:(b + 1) * S]
                    for t in range(2):
                        bank = begin(phase, "v", b, t)
                        mm(PS[:, bank, :], context[:, t * P:(t + 1) * P], wv, start=True, stop=True) \
                            .then_inc(filled[bank], 1)
                    if causal:
                        xt_there(phase, b)
                        bank = begin(phase, "q", b)
                        for g in range(2):
                            for c in range(2):
                                last = mm(PS[:, bank, g * S:(g + 1) * S], wq_3[:, c, g * P:(g + 1) * P],
                                          XT[b % 2][:, c, :], start=c == 0, stop=c == 1)
                        last.then_inc(filled[bank], 1)
                        bank = begin(phase, "k", b)
                        for g in range(2):
                            last = mm(PS[:, bank, g * S:(g + 1) * S], wk_3[:, g * P:(g + 1) * P],
                                      context[0:DC, :], start=True, stop=True)
                        last.then_inc(filled[bank], 1)

                def stacked(b, n, kind):
                    done = 2 * b + NB if causal else b
                    for bank, what, _, _ in stacks(phase, b, n):
                        if what != kind:
                            continue
                        keys = what == "ks"
                        if keys and not causal:
                            pe.wait_ge(keys_ready, 4)
                        else:
                            pe.wait_ge(parts_ready, done + keys + 1)
                        begin(phase, what, b, n)
                        parts, rows = (KP, P if causal else DC) if keys else (QP, P)
                        for e in range(2):
                            h = 2 * n + e
                            for k in range(3):
                                part = parts[0:rows, k, h // 8, :] if causal or not keys else \
                                    KG[:, k, b * S:(b + 1) * S]
                                last = mm(PS[0:ROWS, bank, e * S:(e + 1) * S], stack[0:rows, 3 * keys + k, h % 8, :],
                                          part, start=k == 0, stop=k == 2)
                        last.then_inc(filled[bank], 1)

                def key_head(h):
                    return h * key_heads // NH

                def there(b, n):
                    for what, m in (("qs", n), ("ks", key_head(2 * n) // 2)):
                        bank, value = fill_at(phase, what, b, m)
                        pe.wait_ge(drained[bank], value)

                def scores(b, h):
                    if h % 2 == 0:
                        there(b, h // 2)
                    bank = begin(phase, "s", b, h)
                    for i in range(2):
                        n = P if causal and i == 0 else S
                        last = mm(PS[:, bank, i * S:i * S + n], QS[b % 2][0:ROWS, h, i * P:(i + 1) * P],
                                  KS[b % 2][0:ROWS, key_head(h), 0:n], start=True, stop=not causal)
                        if causal:
                            last = mm(PS[:, bank, i * S + i * P:i * S + (i + 1) * P], identb[:, :], maskS[:, :],
                                      start=False, stop=True)
                    last.then_inc(filled[bank], 1)

                def exponents(b, hp):
                    for h in (2 * hp, 2 * hp + 1):
                        bank = begin(phase, "st", b, h)
                        for t in range(2):
                            q0 = P if causal and t == 1 else 0
                            last = mm(PS[:, bank, t * S:t * S + S - q0],
                                      KS[b % 2][:, key_head(h), t * P:(t + 1) * P],
                                      QS[b % 2][:, h, q0:S], start=True, stop=not causal)
                            if causal:
                                last = mm(PS[:, bank, t * S:t * S + P], identb[:, :], maskT[:, :],
                                          start=False, stop=True)
                        last.then_inc(filled[bank], 1)

                def values(b, hp):
                    s, g = hp % 2, hp // 2
                    if s == 0:
                        begin(phase, "o", b, g)
                    for e in range(2):
                        h = 2 * hp + e
                        bank, value = fill_at(phase, "st", b, h)
                        pe.wait_ge(drained[bank], value)
                        j = h % 4
                        for t in range(2):
                            q0 = P if causal and t == 1 else 0
                            last = mm(PS[32 * j:32 * j + 32, 6, q0:S], VB[b % 2][:, t, h * 32:(h + 1) * 32],
                                      probs[:, s, e, t * S:t * S + S - q0], start=t == 0, stop=t == 1,
                                      skip_group_check=True)
                    last.then_inc(probs_used if s == 0 else filled[6], 1)

                def denominators(b, g):
                    bank, value = fill_at(phase, "o", b, g)
                    pe.wait_ge(drained[bank], value)
                    bank = begin(phase, "den", b, g)
                    mm(PS[:, bank, 0:S], sel_den[:, :], OTR[:, g, :], start=True, stop=True) \
                        .then_inc(filled[bank], 1)

                def max_loads(b):
                    return (NB + (3 * NB if causal else 0) + 3 * b + 3) * 16

                def job_turn(b):
                    turn(NORMALISED.index(job(phase, b)[:2]), fill_at(phase, "job_turn", b)[1] - 1)

                def job_down(b):
                    lora = job(phase, b)[0] == "lora"
                    bank = begin(phase, "job_down", b)
                    n = E2 * R2 + E2 if lora else E3 * R3 + E3
                    for i in range(2):
                        y = PS[:, bank, i * n:(i + 1) * n]
                        for c in range(2):
                            last = mm(y, XJ[:, c, i * P:(i + 1) * P], (ra_2 if lora else dr_3)[:, c, :],
                                      start=c == 0, stop=lora and c == 1)
                        if not lora:
                            last = mm(y, ones[0:1, :], bdr_3, start=False, stop=True)
                    last.then_inc(filled[bank], 1)

                def job_mixed(b):
                    kind, _, number = job(phase, b)
                    pe.wait_ge(weighted, number + 1)
                    bank = begin(phase, "job_mixed", b)
                    for i in range(2):
                        last = pe.transpose(PS[:, bank, i * P:(i + 1) * P], HW[:, i, :], ident[:, :])
                        if kind == "adapter":
                            last = pe.transpose(PS[0:E3, bank, S + i * P:S + (i + 1) * P], CM[:, i, 0:E3],
                                                ident[:, :])
                    last.then_inc(filled[bank], 1)

                def job_y(b):
                    lora = job(phase, b)[0] == "lora"
                    bank = begin(phase, "job_y", b)
                    mixed, value = fill_at(phase, "job_mixed", b)
                    pe.wait_ge(drained[mixed], value)
                    for i in range(2):
                        y = PS[:, bank, i * D:(i + 1) * D]
                        tokens = slice(i * P, (i + 1) * P)
                        if lora:
                            mm(y, HWT[0:E2 * R2, tokens], bt_2, start=True, stop=False)
                            for c in range(2):
                                mm(y, XJ[:, c, tokens], wb_2[:, c, :], start=False, stop=False)
                            last = mm(y, ones[0:1, :], biasb_2, start=False, stop=True)
                        else:
                            mm(y, HWT[:, tokens], wu_3, start=True, stop=False)
                            last = mm(y, WT[:, tokens], bu_3, start=False, stop=True)
                    last.then_inc(filled[bank], 1)

                job_steps = {JOB_TURN: job_turn, JOB_DOWN: job_down, JOB_MIXED: job_mixed}

                operands(0)
                for hp in range(NH // 2 + 1):
                    if hp < NH // 2:
                        stacked(0, hp, "qs")
                        stacked(0, hp, "ks")
                    if hp:
                        scores(0, 2 * hp - 2)
                        scores(0, 2 * hp - 1)
                turned_next(phase, 0)
                turned_max(phase, 0)
                operands(1)
                for b in range(NB):
                    ahead = b < NB - 1
                    work_on = job_steps if job(phase, b) else {}
                    if b in (0, NB - 1):
                        pe.wait_ge(ones_set, 32)
                        pe.wait_ge(max_placed, max_loads(b))
                    for hp in range(NH // 2 + 1):
                        if hp < NH // 2 and (hp or b in (0, NB - 1)):
                            exponents(b, hp)
                        if ahead and hp:
                            scores(b + 1, 2 * hp - 2)
                            scores(b + 1, 2 * hp - 1)
                        if ahead and hp < NH // 2:
                            stacked(b + 1, hp, "qs")
                        if hp:
                            values(b, hp - 1)
                        if ahead and hp < NH // 2:
                            stacked(b + 1, hp, "ks")
                        if hp in (3, 5):
                            denominators(b, (hp - 3) // 2)
                        if hp in work_on:
                            work_on[hp](b)
                        if turns_next(phase, b) and hp == NEXT_TURN:
                            turned_next(phase, b + 1)
                    if work_on:
                        job_y(b)
                    if ahead:
                        turned_max(phase, b + 1)
                    denominators(b, 2)
                    denominators(b, 3)
                    if b + 2 < NB:
                        operands(b + 2)
                    bank = begin(phase, "y", b)
                    for g in range(4):
                        pe.wait_ge(norm_ready, (b + (NB if causal else 0)) * 4 + g + 1)
                        if g == 2 and b + 2 < NB:
                            pe.wait_ge(max_placed, max_loads(b + 1))
                            exponents(b + 1, 0)
                        for i in range(2):
                            last = mm(PS[:, bank, i * D:(i + 1) * D], OTN[:, g, i * P:(i + 1) * P], wo[:, g, :],
                                      start=g == 0 and i == 0, stop=g == 3, skip_group_check=True)
                    last.then_inc(filled[bank], 1)
                if causal:
                    for step in sorted(job_steps):
                        job_steps[step](NB)
                    job_y(NB)

            attention("grouped")
            attention("causal")


def kernel(**inputs):
    import ml_dtypes
    import numpy as np
    import concourse.bacc as bacc
    from concourse.bass_utils import run_bass_kernel_spmd

    f32 = np.float32
    g = {k: np.asarray(v) for k, v in inputs.items()}
    arrays = {}

    def chunked(w, c=P):
        return w.reshape(w.shape[0] // c, c, w.shape[1]).transpose(1, 0, 2)

    arrays["x"] = g["x"].reshape(NB * S, D)
    ctx = g["ctx_512"].reshape(NB * S, DC)
    swapped = np.concatenate([ctx[:, DC // 2:], ctx[:, :DC // 2]], axis=1)
    arrays["ctx"], arrays["ctxT"] = ctx, ctx.T
    arrays["ctx_swapped"], arrays["ctxT_swapped"] = swapped, swapped.T
    gates = np.concatenate([g["g_xattn"], g["g_ffn"], g["L0_xattn_gamma_raw"].reshape(1)])
    arrays["gates"] = np.broadcast_to(gates, (P, 9))
    arrays["ident"] = np.eye(P, dtype=f32)
    arrays["wqk0"] = np.stack([g["L0_xattn_Wq"].T, g["L0_xattn_Wk"].T], axis=1)

    w13, sw13 = g["L0_ffn_w13"], g["L0_ffn_sw13"]
    arrays["w_g0"] = chunked(np.concatenate([w13[:, :I0].reshape(-1, D), sw13[:2 * I0]]).T)
    arrays["w_u0"] = chunked(np.concatenate([w13[:, I0:].reshape(-1, D), sw13[2 * I0:]]).T)
    arrays["w_d0"] = np.concatenate([g["L0_ffn_w2"].transpose(0, 2, 1).reshape(-1, D), g["L0_ffn_sw2"].T])
    arrays["w_r0"] = chunked(g["L0_ffn_gate_w"].T)
    sel = np.zeros((3, PART, F0), f32)
    for f in range(F0):
        sel[:, min(f // I0, E0), f] = 1.0
    arrays["sel_e"] = sel.reshape(3 * PART, F0).astype(ml_dtypes.bfloat16)

    def groups(w):
        return w.reshape(4, 4, *w.shape[1:])

    arrays["wq1"] = groups(g["L1_xattn_Wq"].reshape(NH, P, D)).transpose(0, 2, 1, 3)
    arrays["wkq1T"] = groups(g["L1_xattn_w_kc_q"]).reshape(4, 4, P, 2, 96).transpose(0, 4, 3, 1, 2)
    arrays["wqr1T"] = groups(g["L1_xattn_W_qr"]).transpose(0, 3, 1, 2)
    arrays["wkr1T"] = groups(g["L1_xattn_W_kr"]).transpose(0, 3, 1, 2)
    arrays["wkv1"] = groups(g["L1_xattn_w_kc_kv"]).transpose(0, 2, 1, 3)
    arrays["wo1T"] = groups(g["L1_xattn_Wo"].T.reshape(NH, P, D)).transpose(0, 2, 1, 3)
    inv = (f32(1.0) / np.power(f32(10000.0), np.arange(0, DC, 2, dtype=f32) / f32(DC))).astype(f32)
    freq = np.arange(S, dtype=f32)[:, None] * inv[None, :]
    cos, sin = np.repeat(np.cos(freq), 2, axis=1), np.repeat(np.sin(freq), 2, axis=1)
    sin = np.concatenate([-sin[:, :DC // 2], sin[:, DC // 2:]], axis=1)
    rope = np.stack([cos, sin])
    arrays["ropeN"] = rope.reshape(2, 2, P, DC).transpose(2, 1, 0, 3)
    arrays["ropeT"] = rope.transpose(2, 0, 1)
    w12 = np.concatenate([chunked(g["L1_ffn_w1"].T), chunked(g["L1_ffn_w2"].T)], axis=1)
    arrays["w12"], arrays["w3T"] = w12, g["L1_ffn_w3"].T

    def slots(rows, cols=0):
        return np.zeros((rows, NH, 32), f32)

    v2 = slots(DC + 1)
    for h in range(NH):
        for d in range(16):
            v2[16 * (h // 4) + d, h, d] = 1.0
    v2[DC:, :, 16:] = 1.0
    arrays["sel_v2"] = v2.reshape(DC + 1, 512)
    wkv = g["L3_xattn_Wkv_expand"]
    v3 = slots(DC + 1)
    v3[:DC, :, :16] = wkv[D:].T.reshape(DC, NH, 16)
    v3[DC:, :, 16:] = 1.0
    arrays["wk_3"], arrays["wv_3"] = wkv[:D].T, v3.reshape(DC + 1, 512)
    arrays["wq_3"] = chunked(g["L3_xattn_Wq"].T)
    pairings = ((0, 1, 0, 1, 0, 2), (0, 0, 1, 1, 2, 0))
    stack = np.zeros((8, 16, 6, 8, 6, 16), f32)
    for keys in range(2):
        for block, part in enumerate(pairings[keys]):
            for h in range(8):
                stack[h, :, 3 * keys + part, h, block, :] = np.eye(16)
    arrays["key_ones"] = np.ones((3, NH, S), ml_dtypes.bfloat16)
    arrays["stack"] = stack.reshape(P, 6, 8, ROWS).astype(ml_dtypes.bfloat16)
    for name, w in (("wo_2", g["L2_xattn_Wc"]), ("wo_3", g["L3_xattn_Wout"])):
        o = np.zeros((NH, 32, D), f32)
        o[:, :16] = w.T.reshape(NH, 16, D)
        if name == "wo_2":
            o[0, 16] = g["L2_xattn_bc"]
        arrays[name] = chunked(o.reshape(512, D))
    arrays["wb_2"] = chunked(g["L2_ffn_W_base"].T)
    ra = np.concatenate([g["L2_ffn_A_w"].reshape(-1, D), g["L2_ffn_W_router"]]).T
    arrays["ra_2"] = chunked(ra)
    arrays["bt_2"] = g["L2_ffn_B_w"].transpose(0, 2, 1).reshape(E2 * R2, D)
    arrays["biasb_2"] = g["L2_ffn_b_base"].reshape(1, D)
    wd = g["L3_ffn_Wd"].transpose(1, 0, 2).reshape(D, E3 * R3)
    arrays["dr_3"] = chunked(np.concatenate([wd, g["L3_ffn_Wr"]], axis=1))
    arrays["bdr_3"] = np.concatenate([g["L3_ffn_bd"].reshape(-1), g["L3_ffn_br"]]).reshape(1, -1)
    arrays["wu_3"] = g["L3_ffn_Wu"].reshape(E3 * R3, D)
    arrays["bu_3"] = g["L3_ffn_bu"]
    den = np.zeros((P, P), f32)
    for j in range(4):
        den[32 * j + 16, 32 * j:32 * j + 32] = 1.0
    arrays["sel_den"] = den
    later = np.where(np.arange(P)[None, :] > np.arange(P)[:, None], f32(-1e38), f32(0.0))
    arrays["maskS"] = later.astype(ml_dtypes.bfloat16)
    arrays["maskT"] = later.T.astype(ml_dtypes.bfloat16)

    nc = bacc.Bacc("TRN2", target_bir_lowering=False, num_devices=1)
    arrays = {f"in_{k}": np.ascontiguousarray(v) for k, v in arrays.items()}
    aps = {k[3:]: nc.dram_tensor(k, v.shape, mybir.dt.from_np(v.dtype), kind="ExternalInput").ap()
           for k, v in arrays.items()}
    out = nc.dram_tensor("out", (NB * S, D), F32, kind="ExternalOutput").ap()
    build(nc, aps, out)
    got = run_bass_kernel_spmd(nc, [arrays], core_ids=[0]).results[0]["out"]
    return got.reshape(NB, S, D)
```
